# Optimizing a Trainium2 kernel written in Bass

```python
import numpy as np
import jax
import jax.numpy as jnp

def _softmax(x, axis=-1):
    return jax.nn.softmax(x, axis=axis)

def _gelu(x):
    return jax.nn.gelu(x, approximate=True)

def _silu(x):
    return jax.nn.silu(x)

def _sigmoid(x):
    return jax.nn.sigmoid(x)

def _layernorm(x, axis=-1, eps=1e-05):
    m = jnp.mean(x, axis=axis, keepdims=True)
    v = jnp.var(x, axis=axis, keepdims=True)
    return (x - m) / jnp.sqrt(v + eps)

def _scatter_add(tgt, idx, src, axis=0):
    return tgt.at[idx].add(src)

def _segment_sum(src, seg, n):
    return jax.ops.segment_sum(src, seg, n)
kernel_name = 'mk_cond_resid_d4_seqx_r2_fac945'

def setup_inputs(seed: int=0):
    np.random.seed(seed)
    _w = jnp.asarray

    def _rec_inputs():
        import jax
        import jax.numpy as jnp
        _rk = jax.random.key(seed)
        x = -0.0003929 + 0.9999 * jax.random.normal(jax.random.fold_in(_rk, 1), (32, 128, 512), jnp.float32)
        _lenS = 128 - jax.random.randint(jax.random.fold_in(_rk, 7), (32,), 0, max(1, 128 // 4) + 1, jnp.int32)
        _lenS2 = 128 - jax.random.randint(jax.random.fold_in(_rk, 8), (32,), 0, max(1, 128 // 4) + 1, jnp.int32)
        itok_B_0_7 = jax.random.randint(jax.random.fold_in(_rk, 11), (32,), 0, 8, jnp.int32)
        itok_B_0_8 = jax.random.randint(jax.random.fold_in(_rk, 12), (32,), 0, 9, jnp.int32)
        condB_tauraws = -5.74692 + 0.777674 * jax.random.normal(jax.random.fold_in(_rk, 13), (32,), jnp.float32)
        cond_256 = -0.000235209 + 0.019331 * jax.random.normal(jax.random.fold_in(_rk, 14), (32, 128), jnp.float32)
        condB_bn2 = jnp.zeros((32,), jnp.float32)
        cond_1024 = -4.10585e-05 + 0.0199478 * jax.random.normal(jax.random.fold_in(_rk, 16), (32, 512), jnp.float32)
        condB_zX = jax.random.uniform(jax.random.fold_in(_rk, 17), (32,), jnp.float32, 0.0, 0.983423)
        condB_zY = jax.random.uniform(jax.random.fold_in(_rk, 18), (32,), jnp.float32, 0.0, 0.979075)
        condB_zR = jax.random.uniform(jax.random.fold_in(_rk, 19), (32,), jnp.float32, 0.0, 0.9968)
        return (x, itok_B_0_7, itok_B_0_8, condB_tauraws, cond_256, condB_bn2, cond_1024, condB_zX, condB_zY, condB_zR)
    x, itok_B_0_7, itok_B_0_8, condB_tauraws, cond_256, condB_bn2, cond_1024, condB_zX, condB_zY, condB_zR = _rec_inputs()

    def _L0_cond_setup():
        import jax, jax.numpy as jnp
        import numpy as np
        S, O, H = (8, 512, 512)
        B, N = (32, 256)
        key = jax.random.key(seed)
        k1, k2, k3, k4 = jax.random.split(key, 4)
        x = jax.random.normal(k1, (B, N, H), dtype=jnp.float32)
        subject_id = jax.random.randint(k2, (B,), 0, S)
        wbound = jnp.sqrt(2.0 / 6.0) * jnp.sqrt(3.0 / H)
        weight = jax.random.uniform(k3, (S, O, H), minval=-wbound, maxval=wbound, dtype=jnp.float32)
        bbound = 1.0 / jnp.sqrt(H)
        bias = jax.random.uniform(k4, (S, O), minval=-bbound, maxval=bbound, dtype=jnp.float32)
        return {'x': x, 'subject_id': subject_id, 'weight': weight, 'bias': bias}
    _L0_cond_all = _L0_cond_setup()
    _L0_cond_in = {k: v for k, v in _L0_cond_all.items() if k in ('weight', 'bias')}
    del _L0_cond_all

    def _L1_cond_setup():
        import jax, jax.numpy as jnp
        import numpy as np
        LN_EPS = 1e-05
        key = jax.random.key(seed)
        ks = jax.random.split(key, 8)
        B, S, H, A, L = (32, 1024, 512, 128, 10)
        return {'hidden_states': jax.random.normal(ks[0], (B, S, H), dtype=jnp.float32), 'language_ids': jax.random.randint(ks[1], (B,), 0, L, dtype=jnp.int64), 'W1': jax.random.normal(ks[2], (L, H, A), dtype=jnp.float32) * (1.0 / np.sqrt(H)), 'b1': jnp.zeros((L, A), dtype=jnp.float32), 'W2': jax.random.normal(ks[3], (L, A, H), dtype=jnp.float32) * (1.0 / np.sqrt(A)), 'b2': jnp.zeros((L, H), dtype=jnp.float32), 'gamma': jnp.ones((L, H), dtype=jnp.float32), 'beta': jnp.zeros((L, H), dtype=jnp.float32)}
    _L1_cond_all = _L1_cond_setup()
    _L1_cond_in = {k: v for k, v in _L1_cond_all.items() if k in ('W1', 'b1', 'W2', 'b2', 'gamma', 'beta')}
    del _L1_cond_all

    def _L2_cond_setup():
        import jax, jax.numpy as jnp
        import numpy as np
        import math
        B, T, E, D = (4, 1024, 512, 4)

        def _tau_init(t):
            a = 0.1 ** (1.0 / max(t - 1, 1))
            tt = -math.log(max(a, 1e-10))
            return math.log(math.exp(tt) - 1 + 1e-10)

        def causal_ema(b, tau_raw):
            alpha = jnp.exp(-jax.nn.softplus(tau_raw)).astype(b.dtype)

            def step(h, bt):
                h = alpha * h + bt
                return (h, h)
            h0 = jnp.zeros((b.shape[0], b.shape[2]), b.dtype)
            _, hs = jax.lax.scan(step, h0, jnp.swapaxes(b, 0, 1))
            return jnp.swapaxes(hs, 0, 1)
        key = jax.random.key(seed)
        ks = jax.random.split(key, 10)
        s = 0.02
        return {'x': jax.random.normal(ks[0], (B, T, E), jnp.float32), 'tau_ctx': jnp.float32(_tau_init(max(T // 2, 4))), 'tau_raws': jnp.array([_tau_init(max(T // 2 ** i, 2)) for i in range(D)], jnp.float32), 'Wg': jax.random.normal(ks[1], (E, 2 * E), jnp.float32) * s, 'bg': jnp.full((E,), -0.5, jnp.float32), 'Wn1': jax.random.normal(ks[2], (E // 4, E), jnp.float32) * s, 'bn1': jnp.zeros((E // 4,), jnp.float32), 'Wn2': jax.random.normal(ks[3], (D, E // 4), jnp.float32) * s, 'bn2': jnp.zeros((D,), jnp.float32), 'blend': jax.random.normal(ks[4], (D, E), jnp.float32) * s, 'Wsoma': jax.random.normal(ks[5], (E, E), jnp.float32) * s, 'bsoma': jnp.zeros((E,), jnp.float32), 'Wtemp': jax.random.normal(ks[6], (E, E), jnp.float32) * s, 'btemp': jnp.zeros((E,), jnp.float32), 'Wout': jax.random.normal(ks[7], (E, E), jnp.float32) * s, 'gamma': jnp.ones((E,), jnp.float32), 'beta': jnp.zeros((E,), jnp.float32)}
    _L2_cond_all = _L2_cond_setup()
    _L2_cond_in = {k: v for k, v in _L2_cond_all.items() if k in ('tau_ctx', 'Wg', 'bg', 'Wn1', 'bn1', 'Wsoma', 'bsoma', 'Wtemp', 'btemp', 'Wout', 'gamma', 'beta')}
    del _L2_cond_all

    def _L3_cond_setup():
        import jax, jax.numpy as jnp
        import numpy as np
        key = jax.random.key(seed)
        k1, k2, k3, k4 = jax.random.split(key, 4)
        B, H, W = (64, 512, 512)
        return {'y': jax.random.uniform(k1, (B, H, W), dtype=jnp.float32), 'zX': jax.random.uniform(k2, (B, 1), dtype=jnp.float32), 'zY': jax.random.uniform(k3, (B, 1), dtype=jnp.float32), 'zR': jax.random.uniform(k4, (B, 1), dtype=jnp.float32), 'dx': 1, 'dy': 1}
    _L3_cond_all = _L3_cond_setup()
    _L3_cond_in = {k: v for k, v in _L3_cond_all.items() if k in ()}
    del _L3_cond_all
    return {'x': x, 'itok_B_0_7': itok_B_0_7, 'itok_B_0_8': itok_B_0_8, 'condB_tauraws': condB_tauraws, 'cond_256': cond_256, 'condB_bn2': condB_bn2, 'cond_1024': cond_1024, 'condB_zX': condB_zX, 'condB_zY': condB_zY, 'condB_zR': condB_zR, 'L0_cond_weight': _L0_cond_in['weight'], 'L0_cond_bias': _L0_cond_in['bias'], 'L1_cond_W1': _L1_cond_in['W1'], 'L1_cond_b1': _L1_cond_in['b1'], 'L1_cond_W2': _L1_cond_in['W2'], 'L1_cond_b2': _L1_cond_in['b2'], 'L1_cond_gamma': _L1_cond_in['gamma'], 'L1_cond_beta': _L1_cond_in['beta'], 'L2_cond_tau_ctx': _L2_cond_in['tau_ctx'], 'L2_cond_Wg': _L2_cond_in['Wg'], 'L2_cond_bg': _L2_cond_in['bg'], 'L2_cond_Wn1': _L2_cond_in['Wn1'], 'L2_cond_bn1': _L2_cond_in['bn1'], 'L2_cond_Wsoma': _L2_cond_in['Wsoma'], 'L2_cond_bsoma': _L2_cond_in['bsoma'], 'L2_cond_Wtemp': _L2_cond_in['Wtemp'], 'L2_cond_btemp': _L2_cond_in['btemp'], 'L2_cond_Wout': _L2_cond_in['Wout'], 'L2_cond_gamma': _L2_cond_in['gamma'], 'L2_cond_beta': _L2_cond_in['beta']}

def reference(x, itok_B_0_7, itok_B_0_8, condB_tauraws, cond_256, condB_bn2, cond_1024, condB_zX, condB_zY, condB_zR, L0_cond_weight, L0_cond_bias, L1_cond_W1, L1_cond_b1, L1_cond_W2, L1_cond_b2, L1_cond_gamma, L1_cond_beta, L2_cond_tau_ctx, L2_cond_Wg, L2_cond_bg, L2_cond_Wn1, L2_cond_bn1, L2_cond_Wsoma, L2_cond_bsoma, L2_cond_Wtemp, L2_cond_btemp, L2_cond_Wout, L2_cond_gamma, L2_cond_beta):
    import jax
    import jax.numpy as jnp

    def _L0_cond_ref(x, subject_id, weight, bias):
        import jax, jax.numpy as jnp
        import numpy as np
        S, O, H = (8, 512, 512)
        B, N = (32, 256)
        W = weight[subject_id]
        b = bias[subject_id]
        y = jnp.einsum('bnh,boh->bno', x, W) + b[:, None, :]
        return y

    def _L1_cond_ref(hidden_states, language_ids, W1, b1, W2, b2, gamma, beta):
        import jax, jax.numpy as jnp
        import numpy as np
        LN_EPS = 1e-05
        w1 = W1[language_ids]
        w2 = W2[language_ids]
        h = jnp.einsum('bsh,bha->bsa', hidden_states, w1) + b1[language_ids][:, None, :]
        h = jax.nn.relu(h)
        adapted = jnp.einsum('bsa,bah->bsh', h, w2) + b2[language_ids][:, None, :]
        x = hidden_states + adapted
        mean = jnp.mean(x, axis=-1, keepdims=True)
        var = jnp.mean(jnp.square(x - mean), axis=-1, keepdims=True)
        normed = (x - mean) * jax.lax.rsqrt(var + LN_EPS)
        return normed * gamma[language_ids][:, None, :] + beta[language_ids][:, None, :]

    def _L2_cond_ref(x, tau_ctx, tau_raws, Wg, bg, Wn1, bn1, Wn2, bn2, blend, Wsoma, bsoma, Wtemp, btemp, Wout, gamma, beta):
        import jax, jax.numpy as jnp
        import numpy as np
        import math
        B, T, E, D = (4, 1024, 512, 4)

        def _tau_init(t):
            a = 0.1 ** (1.0 / max(t - 1, 1))
            tt = -math.log(max(a, 1e-10))
            return math.log(math.exp(tt) - 1 + 1e-10)

        def causal_ema(b, tau_raw):
            alpha = jnp.exp(-jax.nn.softplus(tau_raw)).astype(b.dtype)

            def step(h, bt):
                h = alpha * h + bt
                return (h, h)
            h0 = jnp.zeros((b.shape[0], b.shape[2]), b.dtype)
            _, hs = jax.lax.scan(step, h0, jnp.swapaxes(b, 0, 1))
            return jnp.swapaxes(hs, 0, 1)
        ctx = causal_ema(x, tau_ctx)
        gate_in = jnp.concatenate([x, ctx], axis=-1)
        wg = jax.nn.sigmoid(jnp.einsum('btc,ec->bte', gate_in, Wg) + bg)
        gated = x * wg
        h1 = jax.nn.gelu(jnp.einsum('btc,hc->bth', x, Wn1) + bn1, approximate=False)
        mod = 0.5 + jax.nn.sigmoid(jnp.einsum('bth,dh->btd', h1, Wn2) + bn2)
        traces = jax.vmap(lambda tau, m: causal_ema(gated * m[..., None], tau))(tau_raws, jnp.moveaxis(mod, -1, 0))
        blend_w = jax.nn.softmax(blend, axis=0)
        temporal = jnp.einsum('dbtc,dc->btc', traces, blend_w)
        gate = jax.nn.sigmoid(jnp.einsum('btc,ec->bte', temporal, Wtemp) + btemp)
        soma = jax.nn.gelu(jnp.einsum('btc,ec->bte', x, Wsoma) + bsoma, approximate=False)
        out = jnp.einsum('btc,ec->bte', soma * gate, Wout)
        mu = out.mean(-1, keepdims=True)
        var = out.var(-1, keepdims=True)
        return (out - mu) / jnp.sqrt(var + 1e-05) * gamma + beta

    def _L3_cond_ref(y, zX, zY, zR, dx, dy):
        import jax, jax.numpy as jnp
        import numpy as np
        yp_x = jnp.pad(y, ((0, 0), (0, 0), (1, 1)), mode='reflect')
        lap_x = (yp_x[:, :, :-2] - 2.0 * y + yp_x[:, :, 2:]) / (dx * dx)
        yp_y = jnp.pad(y, ((0, 0), (1, 1), (0, 0)), mode='reflect')
        lap_y = (yp_y[:, :-2, :] - 2.0 * y + yp_y[:, 2:, :]) / (dy * dy)
        du_dt = zX[:, :, None] * lap_x + zY[:, :, None] * lap_y + zR[:, :, None] * y * (1.0 - y)
        return du_dt
    x = x + _L0_cond_ref(x, itok_B_0_7, L0_cond_weight, L0_cond_bias)
    x = x + _L1_cond_ref(x, itok_B_0_8, L1_cond_W1, L1_cond_b1, L1_cond_W2, L1_cond_b2, L1_cond_gamma, L1_cond_beta)
    x = x + _L2_cond_ref(x, L2_cond_tau_ctx, condB_tauraws, L2_cond_Wg, L2_cond_bg, L2_cond_Wn1, L2_cond_bn1, cond_256, condB_bn2, cond_1024, L2_cond_Wsoma, L2_cond_bsoma, L2_cond_Wtemp, L2_cond_btemp, L2_cond_Wout, L2_cond_gamma, L2_cond_beta)
    x = x + _L3_cond_ref(x, condB_zX[:, None], condB_zY[:, None], condB_zR[:, None], 1, 1)
    return x

_drawn_inputs = setup_inputs


def setup_inputs(seed=0):
    import zlib

    import numpy as np

    out = dict(_drawn_inputs(seed))
    spreads = {'condB_bn2': (0.0, 2.0),
     'L1_cond_b1': (0.0, 0.1),
     'L1_cond_b2': (0.0, 0.1),
     'L1_cond_gamma': (1.0, 0.2),
     'L1_cond_beta': (0.0, 0.1),
     'L2_cond_bg': (-0.5, 0.6),
     'L2_cond_bn1': (0.0, 2.0),
     'L2_cond_bsoma': (0.0, 0.1),
     'L2_cond_btemp': (0.0, 0.8),
     'L2_cond_gamma': (1.0, 0.2),
     'L2_cond_beta': (0.0, 0.1)}
    factors = {'condB_tauraws': 8.0, 'cond_256': 8.0, 'cond_1024': 64.0, 'L2_cond_Wn1': 8.0}
    for name, (base, spread) in spreads.items():
        noise = np.random.default_rng([zlib.crc32(name.encode()), seed]).standard_normal(out[name].shape)
        drawn = base * np.exp(spread * noise) if base else spread * noise
        out[name] = jnp.asarray(drawn.astype(out[name].dtype))
    for name, factor in factors.items():
        out[name] = (out[name] * factor).astype(out[name].dtype)
    return out
```

```python
import concourse.bass as bass
from concourse import mybir
from contextlib import ExitStack


def cond_resid_kernel(nc, x, subject, language, tau, wn2, bn2, blend, zx, zy, zr, l0_w, l0_b,
                      l1_w1, l1_b1, l1_w2, l1_b2, l1_gamma, l1_beta, tau_ctx, wg, bg, wn1, bn1,
                      wsoma, bsoma, wtemp, btemp, wout, l2_gamma, l2_beta, out):
    f32, f32r, bf16, i32 = mybir.dt.float32, mybir.dt.float32r, mybir.dt.bfloat16, mybir.dt.int32
    ALU, ACT, AX = mybir.AluOpType, mybir.ActivationFunctionType, mybir.AxisListType

    P = 128
    NB, T, C = x.shape
    NS = l0_w.shape[0]
    NL, _, H1 = l1_w1.shape
    D = tau.shape[0]
    HN = wn1.shape[0]
    CC = C // P
    Q = 8
    NK = T // Q
    KG = P // D
    NG = NK // KG
    QUAD = 32
    EPS = 1e-5
    W_TILES = [(0,), (1, 7), (2, 6), (3, 5), (4,)]
    NW = len(W_TILES)
    assert T == P and D == QUAD and C == 512 and H1 == P and HN == P and NL <= QUAD and NS <= QUAD

    with ExitStack() as ctx:
        def sb(name, shape, dt=f32):
            return ctx.enter_context(nc.sbuf_tensor(name, shape, dt))

        def sem(name):
            return ctx.enter_context(nc.semaphore(name))

        wg_r = sb("wg_r", [P, 2, 2 * CC, C], f32r)
        wsoma_r = sb("wsoma_r", [P, 2, CC, C], f32r)
        wn1_r = sb("wn1_r", [P, 2, CC, HN], f32r)
        wtemp_t = sb("wtemp_t", [P, CC, C])
        wout_t = sb("wout_t", [P, CC, C])
        wn2_t = sb("wn2_t", [P, P])
        w0_t = sb("w0_t", [P, 2, CC, C])
        w1_t = sb("w1_t", [P, 2, CC, H1])
        w2_t = sb("w2_t", [P, 2, C])
        l0_wt_dram = nc.dram_tensor("l0_wt_dram", (NS, P, CC * C), f32, kind="Internal").ap()
        TB = {}
        at = 0
        for name, width in (("b0", C), ("b2", C), ("gamma", C), ("beta", C), ("bg", C), ("bsoma", C),
                            ("btemp", C), ("b1", H1), ("bn1", HN)):
            TB[name] = (at, width)
            at += width
        tables = sb("tables", [P, at], bf16)
        n_table = at

        def table(name):
            o, w = TB[name]
            return tables[:, o:o + w]

        ones = sb("ones", [P, P], bf16)
        subj_hot = sb("subj_hot", [P, NB], bf16)
        lang_hot = sb("lang_hot", [P, NB], bf16)
        subj_rows = sb("subj_rows", [P, T], bf16)
        lang_rows = sb("lang_rows", [P, T], bf16)
        ident = sb("ident", [P, P])
        neigh = sb("neigh", [P, P])
        decay = sb("decay", [P, NK, D])
        spread = sb("spread", [P, Q, KG])
        blend_n = sb("blend_n", [P, C])
        vj = sb("vj", [P, Q, C], f32r)
        ctx_decay = sb("ctx_decay", [P, CC, T])
        gamma2 = sb("gamma2", [P, C])
        beta2 = sb("beta2", [P, C])
        zt = sb("zt", [P, NB, 4])
        zb = sb("zb", [P, 2, 4])
        bn2_c = sb("bn2_c", [P, 1])
        lo_rows = sb("lo_rows", [P, 1])
        scal = sb("scal", [P, 3])
        ids_sb = sb("ids_sb", [1, 2, NB], i32)
        n_work = 0
        plan = {}
        for name, width in (("actT", C), ("x1", C), ("h", H1), ("hT", H1), ("y", C),
                            ("n1", C), ("xb", C), ("x2", C), ("ctxT", C), ("g", C), ("gT", C), ("h1", HN),
                            ("h1T", HN), ("mt", T), ("m", T), ("amat", C), ("pj", NW * C),
                            ("u", 2 * C), ("tempT", C), ("soma", C), ("sg", C), ("sgT", C),
                            ("x3", C), ("x2b", 2 * C), ("sq", C), ("nb", C), ("fin", 2 * C),
                            ("mix", P), ("mixt", P), ("mixi", P), ("small", 64), ("x", 2 * C)):
            plan[name] = (n_work, width)
            n_work += width
        work = sb("work", [P, n_work])

        def buf(name):
            o, w = plan[name]
            return work[:, o:o + w]

        x_sb = buf("x").rearrange("p (a c) -> p a c", a=2)
        actT, x1, h, hT, y, n1, xb, x2 = (buf(n) for n in ("actT", "x1", "h", "hT", "y", "n1", "xb", "x2"))
        ctxT, g, gT, h1, h1T, mt, m = (buf(n) for n in ("ctxT", "g", "gT", "h1", "h1T", "mt", "m"))
        amat = buf("amat").rearrange("p (k d) -> p k d", d=D)
        pj = buf("pj").rearrange("p (w c) -> p w c", w=NW)
        u = buf("u").rearrange("p (a c) -> p a c", a=2)
        tempT, soma, sg, sgT, x3 = (buf(n) for n in ("tempT", "soma", "sg", "sgT", "x3"))
        x2b = buf("x2b").rearrange("p (a c) -> p a c", a=2)
        sq, nb = buf("sq"), buf("nb")
        fin = buf("fin").rearrange("p (a c) -> p a c", a=2)
        mix, mixt, mixi = buf("mix"), buf("mixt"), buf("mixi")
        sm = buf("small")
        st_a, mv_a, rs_a = sm[:, 0:6], sm[:, 8:10], sm[:, 12:15]
        st_c, mv_c, rs_c = sm[:, 16:22], sm[:, 24:26], sm[:, 28:31]
        prep = [n_table]

        def scratch(width, dt=f32):
            v = work[:, prep[0]:prep[0] + width]
            prep[0] += width
            assert prep[0] <= plan["x"][0]
            return v.bitcast(dt) if dt is not f32 else v

        wt_buf = scratch(CC * C).rearrange("p (a c) -> p a c", a=CC)
        lnat, lnat2 = scratch(D + 2), scratch(D + 2)
        zraw = scratch(3 * NB).rearrange("p (z b) -> p z b", z=3)
        idr = scratch(2 * NB, i32).rearrange("p (z b) -> p z b", z=2)
        idf = scratch(2 * NB).rearrange("p (z b) -> p z b", z=2)
        wn1_raw, wn2_raw, bl_raw = scratch(C), scratch(P), scratch(C)
        e_decay = scratch(NK * D, i32).rearrange("p (k d) -> p k d", k=NK)
        e_spread = scratch(Q * KG, i32).rearrange("p (q k) -> p q k", q=Q)
        e_spread_f = scratch(Q * KG).rearrange("p (q k) -> p q k", q=Q)
        e_j, e_p = scratch(Q, i32), scratch(1, i32)
        e_j_f, p_f, alpha_j, alpha_ctx = scratch(Q), scratch(1), scratch(Q), scratch(1)
        bl_m = scratch(CC)
        bl_t = scratch(CC * D).rearrange("p (a d) -> p a d", a=CC)
        bl_rep = scratch(CC * KG * D).rearrange("p (a r d) -> p a r d", a=CC, r=KG)
        vtmp = scratch(C)
        x2h = sb("x2h", [P, 2, C], f32r)
        ctxh = sb("ctxh", [P, 2, C], f32r)
        ms = sb("ms", [P, T], f32r)
        msh = sb("msh", [P, T], f32r)

        bank = [ctx.enter_context(nc.psum_tensor(f"bank{i}", [P, C], f32)) for i in range(8)]
        B_XG, B_C, B_A1, B_MOD, B_WG, B_R0, B_A2, B_R1 = bank
        h1_ps, h1T_ps, mt_ps, mn_ps = (B_MOD[:, 0:HN], B_MOD[:, P:2 * P], B_MOD[:, 2 * P:3 * P],
                                       B_MOD[:, 3 * P:4 * P])
        ring = [B_R0, B_R1]

        ident_ready = sem("ident_ready")
        raw_loaded = [sem("raw_loaded_even"), sem("raw_loaded_odd")]
        slab_turned = sem("slab_turned")
        act_evac = sem("act_evac")
        dve_evac = sem("dve_evac")
        wt_stored = sem("wt_stored")
        const_loaded = sem("const_loaded")
        ids_loaded = sem("ids_loaded")
        rows_zeroed = sem("rows_zeroed")
        rows_loaded = sem("rows_loaded")
        iota_ready = sem("iota_ready")
        iota2_ready = sem("iota2_ready")
        pool_done = sem("pool_done")
        dchain = sem("dve_step_done")
        achain = sem("act_step_done")
        lna_ready = sem("lna_ready")
        expo_ready = sem("expo_ready")
        raw_decay = sem("raw_decay")
        blend_turned = sem("blend_turned")
        blend_soft = sem("blend_soft")
        blend_back = sem("blend_back")
        blend_shift = sem("blend_shift")
        blend_exp = sem("blend_exp")
        wn_turned = sem("wn_turned")
        wn_hi = sem("wn_hi")
        consts_dve = sem("consts_dve")
        hot_ready = sem("hot_ready")
        zt_ready = sem("zt_ready")
        S = {n: [sem(n + "_even"), sem(n + "_odd")] for n in ("x_loaded", "w0_loaded", "w1_loaded", "w2_loaded",
                                                              "out_stored")}
        names = """subj_set lang_set zb_set mix_set
            xT_turned xT_ready l0_done x1_ready x1T_turned x1T_ready h_done h_ready hT_turned hT_ready
            l1_done y_ready st1_ready mv1_ready ve1_ready rs1_ready nm1_ready n1_ready gamma_done beta_done
            ng1_ready xb_ready x2_ready x2T_turned ctx_ready x2hi_ready x2lo_ready ctxhi_ready ctxlo_ready
            h1_done h1_ready h1T_turned h1T_ready mod_done mt_ready m_ready msh_ready ms_ready mn_turned
            amat_ready wg_done tg_ready g_ready gT_turned gT_ready w_done p_ready acc_ready soma_done
            soma_ready state_done u_ready spread_done temp_ready x2b_ready gate_done gate_ready sg_ready
            sgT_turned sgT_ready out_done st2_ready mv2_ready ve2_ready rs2_ready nm2_ready n2_ready
            ng2_ready x3_ready sq_ready nb_ready nbe_ready lap_done lap_ready fin_ready""".split()
        S.update({n: sem(n) for n in names})

        def transfers(b, par):
            return 8 * b + 16 - 8 * par

        def live(b):
            return not isinstance(b, int) or 0 <= b < NB

        def past(b, n):
            return not isinstance(b, int) or b >= n

        def steps(engine, step):
            for i in (-2, -1, 0, 1):
                step(i, i % 2)
            with engine.Fori(2, NB - 3, 2) as i:
                step(i, 0)
                step(i + 1, 1)
            for i in (NB - 2, NB - 1):
                step(i, i % 2)

        def slab_sources():
            return [wg[:, 0:C], wg[:, C:2 * C], wsoma, wtemp, wout]

        NSLAB = NS + 5
        N_CONST = 11 + 3 * KG
        N_POOL = 6 + 4 + 3
        ACC_AT = {j: n for n, j in enumerate(j for js in W_TILES for j in js if j)}

        def slab_bank(par, a):
            return bank[4 * par + a][:, :]

        def evacuated(k):
            half = CC // 2
            if not isinstance(k, int) or k < NS:
                return half * (k + 1)
            m_ = k - NS + 1
            return half * NS + CC * min(m_, 3) + half * max(m_ - 3, 0)

        def slabs(engine, slab):
            slab(0, 0)
            slab(1, 1)
            with engine.Fori(2, NS - 1, 2) as k:
                slab(k, 0)
                slab(k + 1, 1)
        block = ctx.enter_context(nc.Block())

        @block.sync
        def _(sp):
            with nc.allow_non_contiguous_dma(reason="small constant rows and columns"):
                def load_slab(k, par, src):
                    if not isinstance(k, int) or k >= 2:
                        sp.wait_ge(slab_turned, (k - 1) * CC)
                    sp.dma_start(w0_t[:, par], src.rearrange("(a p) c -> p a c", p=P)).then_inc(raw_loaded[par], 16)

                sp.dma_start(ids_sb[0:1, 0, :], subject.rearrange("(a b) -> a b", a=1)).then_inc(ids_loaded, 16)
                sp.dma_start(ids_sb[0:1, 1, :], language.rearrange("(a b) -> a b", a=1)).then_inc(ids_loaded, 16)
                load_slab(0, 0, l0_w[0])
                load_slab(1, 1, l0_w[1])
                sp.wait_ge(rows_zeroed, 1)
                stage = work[:, 0:n_table]
                for part in range(3):
                    r = QUAD * part
                    for name, src, n in (("b0", l0_b, NS), ("b1", l1_b1, NL), ("b2", l1_b2, NL),
                                         ("gamma", l1_gamma, NL), ("beta", l1_beta, NL)):
                        o, w = TB[name]
                        sp.dma_start(stage[r:r + n, o:o + w], src).then_inc(rows_loaded, 16)
                    for name, src in (("bg", bg), ("bsoma", bsoma), ("btemp", btemp), ("bn1", bn1)):
                        o, w = TB[name]
                        sp.dma_start(stage[r:r + 1, o:o + w], src.rearrange("(a c) -> a c", a=1)).then_inc(rows_loaded, 16)
                def store_slab(k):
                    sp.wait_ge(act_evac, evacuated(k))
                    sp.wait_ge(dve_evac, evacuated(k))
                    sp.dma_start(l0_wt_dram[bass.ds(k, 1)].rearrange("a p c -> (a p) c"),
                                 wt_buf.rearrange("p a c -> p (a c)")).then_inc(wt_stored, 16)

                with sp.Fori(2, NS - 1, 2) as k:
                    for par in range(2):
                        load_slab(k + par, par, l0_w[bass.ds(k + par, 1)].rearrange("a o c -> (a o) c"))
                        store_slab(k - 2 + par)
                for m_, src in enumerate(slab_sources()):
                    load_slab(NS + m_, (NS + m_) % 2, src)
                    if m_ < 2:
                        store_slab(NS - 2 + m_)
                sp.wait_ge(ids_loaded, 2 * 16)
                sp.wait_ge(wt_stored, 16 * NS)
                sp.wait_ge(slab_turned, NSLAB * CC)

                def load_row(b, par):
                    if past(b, 2):
                        sp.wait_ge(S["l0_done"], b - 1)
                        sp.wait_ge(S["h_done"], b - 1)
                        sp.wait_ge(S["l1_done"], b - 1)
                        sp.wait_ge(S["x1_ready"], b - 1)
                    sp.dma_start(x_sb[:, par], x[bass.ds(b, 1)].rearrange("a t c -> (a t) c")).then_inc(S["x_loaded"][par], 16)
                    s_id = sp.value_load(ids_sb[0:1, 0, bass.ds(b, 1)], min_val=0, max_val=NS - 1)
                    l_id = sp.value_load(ids_sb[0:1, 1, bass.ds(b, 1)], min_val=0, max_val=NL - 1)
                    sp.dma_start(w0_t[:, par].rearrange("p a c -> p (a c)"),
                                 l0_wt_dram[bass.ds(s_id, 1)].rearrange("a p c -> (a p) c")).then_inc(S["w0_loaded"][par], 16)
                    sp.dma_start(w1_t[:, par], l1_w1[bass.ds(l_id, 1)].rearrange("l (a p) h -> p (l a) h", p=P)).then_inc(S["w1_loaded"][par], 16)
                    sp.dma_start(w2_t[:, par], l1_w2[bass.ds(l_id, 1)].rearrange("l h c -> (l h) c")).then_inc(S["w2_loaded"][par], 16)

                def store_row(b, par):
                    sp.wait_ge(S["fin_ready"], b + 1)
                    sp.dma_start(out[bass.ds(b, 1)].rearrange("a t c -> (a t) c"), fin[:, par]).then_inc(S["out_stored"][par], 16)

                def step(i, par):
                    if live(i + 2):
                        load_row(i + 2, par)
                    if live(i - 1):
                        store_row(i - 1, 1 - par)

                steps(sp, step)
                store_row(NB - 1, 1)
                for par in range(2):
                    sp.wait_ge(S["out_stored"][par], transfers(NB - 2 + par, par))

        @block.gpsimd
        def _(pool):
            g_ = nc.gpsimd
            g_.memset(ident[:, :], 0.0).then_inc(pool_done, 1)
            g_.memset(work[:, 0:n_table], 0.0).then_inc(rows_zeroed, 1)
            pool.wait_ge(pool_done, 1)
            g_.affine_select(out=ident[:, :], in_=ident[:, :], compare_op=ALU.not_equal, fill=1.0, base=0,
                             pattern=[[-1, P]], channel_multiplier=1).then_inc(ident_ready, 1)
            with nc.allow_non_contiguous_dma(reason="small constant rows and columns"):
                def one(dst, src):
                    pool.dma_start(dst, src).then_inc(const_loaded, 16)
                taus = lnat[:, 0:D]
                one(taus, tau.partition_broadcast(P))
                one(lnat[:, D + 1:D + 2], tau_ctx.partition_broadcast(P))
                one(gamma2[:, :], l2_gamma.partition_broadcast(P))
                one(beta2[:, :], l2_beta.partition_broadcast(P))
                one(zraw[:, 0], zx.partition_broadcast(P))
                one(zraw[:, 1], zy.partition_broadcast(P))
                one(zraw[:, 2], zr.partition_broadcast(P))
                one(idr[:, 0], subject.partition_broadcast(P))
                one(idr[:, 1], language.partition_broadcast(P))
                one(wn1_raw, wn1)
                one(bl_raw[0:D, :], blend)
                for r in range(KG):
                    rows = slice(r * D, (r + 1) * D)
                    one(lnat[rows, D:D + 1], tau.rearrange("(d a) -> d a", a=1))
                    one(bn2_c[rows, :], bn2.rearrange("(d a) -> d a", a=1))
                    one(wn2_raw[rows, :], wn2)
            g_.iota(e_decay, pattern=[[Q, NK], [0, D]], base=-1, channel_multiplier=-1).then_inc(iota_ready, 1)
            g_.iota(e_spread, pattern=[[1, Q], [0, KG]], base=1, channel_multiplier=0).then_inc(iota_ready, 1)
            g_.iota(e_j, pattern=[[1, Q]], base=0, channel_multiplier=0).then_inc(iota_ready, 1)
            g_.iota(e_p, pattern=[[0, 1]], base=0, channel_multiplier=1).then_inc(iota_ready, 1)
            g_.memset(ones[:, :], 1.0).then_inc(pool_done, 1)
            for n, value in enumerate((-0.5, EPS, -1.0)):
                g_.memset(scal[:, n:n + 1], value).then_inc(pool_done, 1)
            g_.memset(neigh[:, :], 0.0).then_inc(pool_done, 1)
            n_done = 6
            for cols, base, fill in ((slice(0, P), 1, 1.0), (slice(0, P), -1, 1.0), (slice(0, 1), -1, 2.0),
                                     (slice(P - 1, P), 2 - P, 2.0)):
                width = cols.stop - cols.start
                pool.wait_ge(pool_done, n_done)
                g_.affine_select(out=neigh[:, cols], in_=neigh[:, cols], compare_op=ALU.not_equal, fill=fill,
                                 base=base, pattern=[[-1, width]], channel_multiplier=1).then_inc(pool_done, 1)
                n_done += 1
            pool.wait_ge(raw_decay, 2)
            g_.affine_select(out=decay[:, :, :], in_=decay[:, :, :], compare_op=ALU.is_ge, fill=0.0, base=-1,
                             pattern=[[Q, NK], [0, D]], channel_multiplier=-1).then_inc(pool_done, 1)
            g_.affine_select(out=spread[:, :, :], in_=spread[:, :, :], compare_op=ALU.is_ge, fill=0.0, base=0,
                             pattern=[[0, Q], [-D, KG]], channel_multiplier=1).then_inc(pool_done, 1)
            n_done += 2
            pool.wait_ge(pool_done, n_done)
            g_.affine_select(out=spread[:, :, :], in_=spread[:, :, :], compare_op=ALU.is_ge, fill=0.0, base=D - 1,
                             pattern=[[0, Q], [D, KG]], channel_multiplier=-1).then_inc(pool_done, 1)
            n_done += 1
            assert n_done == N_POOL
            pool.wait_ge(hot_ready, 2)
            pool.wait_ge(zt_ready, 1)
            pool.wait_ge(pool_done, n_done)
            pool.wait_ge(consts_dve, 1)

            def rstd(par_mv, par_rs, n, b):
                pool.wait_ge(S[f"mv{n}_ready"], b + 1)
                if past(b, 1):
                    pool.wait_ge(S[f"n{n}_ready"], b)
                g_.tensor_tensor(par_rs[:, 0:1], par_mv[:, 1:2], scal[:, 1:2], ALU.add)
                g_.tensor_tensor(par_rs[:, 2:3], par_mv[:, 0:1], scal[:, 2:3], ALU.mult).then_inc(S[f"ve{n}_ready"], 1)
                pool.wait_ge(S[f"ve{n}_ready"], b + 1)
                g_.tensor_tensor(par_rs[:, 1:2], par_rs[:, 0:1], scal[:, 0:1], ALU.pow).then_inc(S[f"rs{n}_ready"], 1)
                pool.wait_ge(S[f"rs{n}_ready"], b + 1)
                g_.tensor_tensor(par_rs[:, 2:3], par_rs[:, 2:3], par_rs[:, 1:2], ALU.mult).then_inc(S[f"nm{n}_ready"], 1)

            def step(i, par):
                A, B, Cr = i + 2, i + 1, i
                if live(A):
                    if past(A, 1):
                        pool.wait_ge(S["l0_done"], A)
                    g_.tensor_copy(subj_rows[:, :], subj_hot[:, bass.ds(A, 1)].to_broadcast([P, T])).then_inc(S["subj_set"], 1)
                    if past(A, 1):
                        pool.wait_ge(S["beta_done"], A)
                    g_.tensor_copy(lang_rows[:, :], lang_hot[:, bass.ds(A, 1)].to_broadcast([P, T])).then_inc(S["lang_set"], 1)
                if live(B):
                    pool.wait_ge(S["x2_ready"], B + 1)
                    if past(B, 2):
                        pool.wait_ge(S["x3_ready"], B - 1)
                    g_.tensor_tensor(x2b[:, 1 - par], x2, beta2[:, :], ALU.add).then_inc(S["x2b_ready"], 1)
                    pool.wait_ge(S["ctxhi_ready"], B + 1)
                    g_.tensor_tensor(ctxh[:, 1], ctxT, ctxh[:, 0].bitcast(f32), ALU.subtract).then_inc(S["ctxlo_ready"], 1)
                if live(Cr):
                    if past(Cr, 2):
                        pool.wait_ge(S["fin_ready"], Cr - 1)
                    g_.tensor_copy(zb[:, par], zt[:, bass.ds(Cr, 1), :].rearrange("p a z -> p (a z)")).then_inc(S["zb_set"], 1)
                    pool.wait_ge(S["zb_set"], Cr + 1)
                    if past(Cr, 1):
                        pool.wait_ge(S["lap_done"], Cr)
                    g_.tensor_tensor(mixt, neigh[:, :], zb[:, par, 1:2].to_broadcast([P, P]), ALU.mult).then_inc(S["mix_set"], 1)
                    g_.tensor_tensor(mixi, ident[:, :], zb[:, par, 0:1].to_broadcast([P, P]), ALU.mult).then_inc(S["mix_set"], 1)
                    pool.wait_ge(S["mix_set"], 3 * Cr + 2)
                    g_.tensor_tensor(mix, mixt, mixi, ALU.add).then_inc(S["mix_set"], 1)
                if live(Cr):
                    rstd(mv_c, rs_c, 2, Cr)
                if live(A):
                    rstd(mv_a, rs_a, 1, A)
                if live(Cr):
                    pool.wait_ge(S["n2_ready"], Cr + 1)
                    g_.tensor_tensor(x3, x3, gamma2[:, :], ALU.mult).then_inc(S["ng2_ready"], 1)
                    pool.wait_ge(S["x3_ready"], Cr + 1)
                    if past(Cr, 1):
                        pool.wait_ge(S["lap_ready"], Cr)
                    g_.tensor_tensor(nb[:, 1:C - 1], x3[:, 0:C - 2], x3[:, 2:C], ALU.add).then_inc(S["nb_ready"], 1)
                    g_.tensor_tensor(nb[:, 0:C:C - 1], x3[:, 1:C - 1:C - 3], x3[:, 1:C - 1:C - 3], ALU.add).then_inc(S["nbe_ready"], 1)

            steps(pool, step)

        @block.scalar
        def _(act):
            a_ = nc.scalar
            def slab(k, par):
                if past(k, 1):
                    act.wait_ge(wt_stored, 16 * k)
                for a in range(2):
                    act.wait_ge(slab_turned, k * CC + a + 1)
                    a_.activation(wt_buf[:, a], slab_bank(par, a), ACT.Copy).then_inc(act_evac, 1)

            slabs(act, slab)
            for s_ in range(5):
                k = NS + s_
                for a in range(CC):
                    act.wait_ge(slab_turned, k * CC + a + 1)
                    src = slab_bank(k % 2, a)
                    if s_ < 2:
                        a_.activation(wg_r[:, 0, s_ * CC + a], src, ACT.Copy).then_inc(act_evac, 1)
                    elif s_ == 2:
                        a_.activation(wsoma_r[:, 0, a], src, ACT.Copy).then_inc(act_evac, 1)
                    elif a < 2:
                        dst, f = ((wtemp_t, 1.0), (wout_t, 0.5))[s_ - 3]
                        a_.activation(dst[:, a], src, ACT.Copy, scale=f).then_inc(act_evac, 1)
            act.wait_ge(wn_turned, 1)
            a_.activation(wn1_r[:, 0].rearrange("p a h -> p (a h)"), bank[0][:, :], ACT.Copy).then_inc(wn_hi, 1)
            a_.activation(wn2_t[:, :], bank[1][:, 0:P], ACT.Copy).then_inc(wn_hi, 1)
            act.wait_ge(const_loaded, N_CONST * 16)
            a_.activation(lnat2, lnat, ACT.Abs).then_inc(achain, 1)
            act.wait_ge(achain, 1)
            a_.activation(lnat2, lnat2, ACT.Exp, scale=-1.0).then_inc(achain, 1)
            act.wait_ge(achain, 2)
            a_.activation(lnat2, lnat2, ACT.Ln, bias=1.0).then_inc(achain, 1)
            act.wait_ge(expo_ready, 1)
            a_.activation(decay[:, :, :], decay[:, :, :], ACT.Exp).then_inc(raw_decay, 1)
            a_.activation(spread[:, :, :], e_spread_f, ACT.Exp, scale=lnat[:, D:D + 1]).then_inc(raw_decay, 1)
            a_.activation(alpha_j, e_j_f, ACT.Exp, scale=lnat[:, D:D + 1]).then_inc(achain, 1)
            a_.activation(alpha_ctx, lnat[:, D + 1:D + 2], ACT.Exp).then_inc(achain, 1)
            act.wait_ge(blend_shift, 1)
            a_.activation(bl_t, bl_t, ACT.Exp).then_inc(blend_exp, 1)
            act.wait_ge(consts_dve, 1)

            def step(i, par):
                A, B, Cr = i + 2, i + 1, i
                if live(B):
                    act.wait_ge(S["x2T_turned"], B + 1)
                    if past(B, 1):
                        act.wait_ge(S["soma_done"], B)
                    a_.activation(x2h[:, 0], B_XG[:, :], ACT.Copy).then_inc(S["x2hi_ready"], 1)
                    act.wait_ge(S["ctx_ready"], B + 1)
                    if past(B, 1):
                        act.wait_ge(S["wg_done"], B)
                    a_.activation(ctxh[:, 0], ctxT, ACT.Copy).then_inc(S["ctxhi_ready"], 1)
                if live(Cr):
                    act.wait_ge(S["gate_done"], Cr + 1)
                    if past(Cr, 1):
                        act.wait_ge(S["sgT_turned"], Cr)
                    a_.activation(sg, B_C[:, :], ACT.Tanh, scale=0.5).then_inc(S["gate_ready"], 1)
                if live(B):
                    act.wait_ge(S["h1_done"], B + 1)
                    if past(B, 1):
                        act.wait_ge(S["h1T_turned"], B)
                    a_.activation(h1, h1_ps, ACT.Gelu).then_inc(S["h1_ready"], 1)
                    act.wait_ge(S["h1T_turned"], B + 1)
                    if past(B, 1):
                        act.wait_ge(S["mod_done"], B)
                    a_.activation(h1T, h1T_ps, ACT.Copy).then_inc(S["h1T_ready"], 1)
                    act.wait_ge(S["mod_done"], B + 1)
                    if past(B, 1):
                        act.wait_ge(S["m_ready"], B)
                    a_.activation(mt, mt_ps, ACT.Tanh, bias=bn2_c[:, :], scale=0.5).then_inc(S["mt_ready"], 1)
                    act.wait_ge(S["wg_done"], B + 1)
                    if past(B, 1):
                        act.wait_ge(S["state_done"], NG * B)
                        act.wait_ge(S["gT_turned"], B)
                    a_.activation(g, B_WG[:, :], ACT.Tanh, scale=0.5).then_inc(S["tg_ready"], 1)
                if live(Cr):
                    act.wait_ge(S["sgT_turned"], Cr + 1)
                    if past(Cr, 1):
                        act.wait_ge(S["out_done"], Cr)
                    a_.activation(sgT, B_C[:, :], ACT.Copy).then_inc(S["sgT_ready"], 1)
                if live(A):
                    act.wait_ge(S["xT_turned"], A + 1)
                    if past(A, 1):
                        act.wait_ge(S["h_done"], A)
                    a_.activation(actT, B_A1[:, :], ACT.Copy).then_inc(S["xT_ready"], 1)
                if live(B):
                    act.wait_ge(S["soma_done"], B + 1)
                    if past(B, 1):
                        act.wait_ge(S["sg_ready"], B)
                    a_.activation(soma, B_R0[:, :], ACT.Gelu).then_inc(S["soma_ready"], 1)
                    act.wait_ge(S["gT_turned"], B + 1)
                    if past(B, 1):
                        act.wait_ge(S["p_ready"], NW * B)
                    a_.activation(gT.rearrange("p (a q k) -> p a q k", a=CC, q=Q),
                                  B_XG[:, :].rearrange("p (a k q) -> p a q k", a=CC, q=Q), ACT.Copy).then_inc(S["gT_ready"], 1)
                if live(A):
                    act.wait_ge(S["x1T_turned"], A + 1)
                    act.wait_ge(S["l0_done"], A + 1)
                    a_.activation(actT, B_A1[:, :], ACT.Copy).then_inc(S["x1T_ready"], 1)
                    act.wait_ge(S["h_done"], A + 1)
                    if past(A, 1):
                        act.wait_ge(S["hT_turned"], A)
                    a_.activation(h, B_A1[:, 0:H1], ACT.Relu).then_inc(S["h_ready"], 1)
                if live(A):
                    act.wait_ge(S["hT_turned"], A + 1)
                    if past(A, 1):
                        act.wait_ge(S["l1_done"], A)
                    a_.activation(hT, B_A1[:, H1:2 * H1], ACT.Copy).then_inc(S["hT_ready"], 1)
                if live(Cr):
                    act.wait_ge(S["nm2_ready"], Cr + 1)
                    act.wait_ge(S["out_done"], Cr + 1)
                    if past(Cr, 1):
                        act.wait_ge(S["sq_ready"], Cr)
                        act.wait_ge(S["nbe_ready"], Cr)
                        act.wait_ge(S["nb_ready"], Cr)
                        act.wait_ge(S["lap_done"], Cr)
                    a_.activation(x3, B_C[:, :], ACT.Identity, scale=rs_c[:, 1:2], bias=rs_c[:, 2:3]).then_inc(S["n2_ready"], 1)
                if live(A):
                    act.wait_ge(S["nm1_ready"], A + 1)
                    if past(A, 1):
                        act.wait_ge(S["x2_ready"], A)
                    a_.activation(n1, y, ACT.Identity, scale=rs_a[:, 1:2], bias=rs_a[:, 2:3]).then_inc(S["n1_ready"], 1)
                if live(Cr):
                    act.wait_ge(S["x3_ready"], Cr + 1)
                    if past(Cr, 1):
                        act.wait_ge(S["fin_ready"], Cr)
                    a_.activation(sq, x3, ACT.Square).then_inc(S["sq_ready"], 1)

            steps(act, step)

        @block.vector
        def _(dve):
            v_ = nc.vector
            def slab(k, par):
                if past(k, 1):
                    dve.wait_ge(wt_stored, 16 * k)
                for a in (2, 3):
                    dve.wait_ge(slab_turned, k * CC + a + 1)
                    v_.tensor_copy(wt_buf[:, a], slab_bank(par, a)).then_inc(dve_evac, 1)

            slabs(dve, slab)
            for s_ in range(5):
                k = NS + s_
                for a in range(CC):
                    src = slab_bank(k % 2, a)
                    if s_ < 3:
                        hi, lo = ((wg_r[:, 0, s_ * CC + a], wg_r[:, 1, s_ * CC + a]) if s_ < 2 else
                                  (wsoma_r[:, 0, a], wsoma_r[:, 1, a]))
                        dve.wait_ge(act_evac, 2 * NS + CC * s_ + a + 1)
                        v_.tensor_tensor(lo, src, hi.bitcast(f32), ALU.subtract).then_inc(dve_evac, 1)
                    elif a >= 2:
                        dve.wait_ge(slab_turned, k * CC + a + 1)
                        dst, f = ((wtemp_t, 1.0), (wout_t, 0.5))[s_ - 3]
                        v_.tensor_scalar(dst[:, a], src, f, None, ALU.mult).then_inc(dve_evac, 1)
            dve.wait_ge(wn_hi, 1)
            v_.tensor_tensor(wn1_r[:, 1].rearrange("p a h -> p (a h)"), bank[0][:, :],
                             wn1_r[:, 0].rearrange("p a h -> p (a h)").bitcast(f32), ALU.subtract).then_inc(dchain, 1)
            done = [1]

            def link(ins):
                ins.then_inc(dchain, 1)
                done[0] += 1
                dve.wait_ge(dchain, done[0])

            for r in range(KG):
                link(v_.memset(lo_rows[r * D:(r + 1) * D, :], float(r % 2)))
            dve.wait_ge(rows_loaded, 27 * 16)
            stage = work[:, 0:n_table]
            link(v_.tensor_copy(tables[:, :], stage))
            for part in (1, 2):
                rows = slice(QUAD * part, QUAD * (part + 1))
                for _ in range(part):
                    link(v_.tensor_tensor(stage[rows], stage[rows], tables[rows, :], ALU.subtract))
                    link(v_.tensor_copy(tables[rows, :], stage[rows]))
            dve.wait_ge(const_loaded, N_CONST * 16)
            dve.wait_ge(achain, 3)
            dve.wait_ge(iota_ready, 4)
            link(v_.tensor_scalar(lnat, lnat, 0.0, None, ALU.max))
            link(v_.tensor_tensor(lnat, lnat, lnat2, ALU.add))
            link(v_.tensor_scalar(lnat, lnat, -1.0, None, ALU.mult))
            link(v_.tensor_scalar(decay[:, :, :], e_decay, 0.0, None, ALU.max))
            link(v_.tensor_tensor(decay[:, :, :], decay[:, :, :],
                                  lnat[:, 0:D].unsqueeze(1).to_broadcast([P, NK, D]), ALU.mult))
            link(v_.tensor_copy(e_spread_f, e_spread))
            v_.tensor_copy(e_j_f, e_j).then_inc(expo_ready, 1)
            link(v_.tensor_copy(idf, idr))
            link(v_.tensor_scalar(e_p, e_p, QUAD - 1, None, ALU.bitwise_and))
            link(v_.tensor_copy(p_f, e_p))
            v_.tensor_scalar(subj_hot[:, :], idf[:, 0], p_f, None, ALU.is_equal).then_inc(hot_ready, 1)
            v_.tensor_scalar(lang_hot[:, :], idf[:, 1], p_f, None, ALU.is_equal).then_inc(hot_ready, 1)
            link(v_.tensor_scalar(zt[:, :, 0], zraw[:, 2], 1.0, None, ALU.add))
            link(v_.scalar_tensor_tensor(zt[:, :, 0], zraw[:, 0], -2.0, zt[:, :, 0], ALU.mult, ALU.add))
            link(v_.scalar_tensor_tensor(zt[:, :, 0], zraw[:, 1], -2.0, zt[:, :, 0], ALU.mult, ALU.add))
            link(v_.tensor_copy(zt[:, :, 1], zraw[:, 1]))
            link(v_.tensor_copy(zt[:, :, 2], zraw[:, 0]))
            v_.tensor_scalar(zt[:, :, 3], zraw[:, 2], -1.0, None, ALU.mult).then_inc(zt_ready, 1)
            link(v_.tensor_scalar(bn2_c[:, :], bn2_c[:, :], 0.5, None, ALU.mult))
            dve.wait_ge(blend_turned, 1)
            bl_ps = bank[2][:, 0:CC * D].rearrange("p (a d) -> p a d", a=CC)
            link(v_.tensor_reduce(out=bl_m, in_=bl_ps, op=ALU.max, axis=AX.X))
            v_.tensor_tensor(bl_t, bl_ps, bl_m.unsqueeze(2).to_broadcast([P, CC, D]), ALU.subtract).then_inc(blend_shift, 1)
            dve.wait_ge(blend_exp, 1)
            link(v_.tensor_reduce(out=bl_m, in_=bl_t, op=ALU.add, axis=AX.X))
            link(v_.reciprocal(bl_m, bl_m))
            for r in range(KG):
                v_.tensor_tensor(bl_rep[:, :, r], bl_t, bl_m.unsqueeze(2).to_broadcast([P, CC, D]), ALU.mult).then_inc(blend_soft, 1)
            dve.wait_ge(blend_back, 1)
            link(v_.tensor_copy(blend_n[:, :], bank[3][:, :]))
            dve.wait_ge(achain, 5)
            for j in range(Q):
                link(v_.tensor_scalar(vtmp, blend_n[:, :], alpha_j[:, j:j + 1], None, ALU.mult))
                link(v_.tensor_copy(vj[:, j], vtmp))
                link(v_.tensor_tensor(vj[P // 2:P, j], vtmp[P // 2:P], vj[P // 2:P, j].bitcast(f32), ALU.subtract))
            link(v_.memset(ctx_decay[:, :, :], 1.0))
            link(v_.tensor_scalar(ctx_decay[:, :, :], ctx_decay[:, :, :], alpha_ctx, None, ALU.mult))
            dve.wait_ge(pool_done, N_POOL)
            v_.memset(ctx_decay[:, :, 0:1], 0.0).then_inc(consts_dve, 1)
            dve.wait_ge(consts_dve, 1)

            def stats(src, st, n, b):
                v_.bn_stats(st, src).then_inc(S[f"st{n}_ready"], 1)
                dve.wait_ge(S[f"st{n}_ready"], b + 1)
                if past(b, 1):
                    dve.wait_ge(S[f"nm{n}_ready"], b)

            def aggregate(st, mv, n):
                v_.bn_aggr(mv, st).then_inc(S[f"mv{n}_ready"], 1)

            def states_blend(B, s_):
                dve.wait_ge(S["state_done"], NG * B + s_ + 1)
                if s_ >= 2:
                    dve.wait_ge(S["spread_done"], NG * B + s_ - 1)
                v_.tensor_tensor(u[:, s_ % 2], ring[s_ % 2][:, :], blend_n[:, :], ALU.mult).then_inc(S["u_ready"], 1)

            def chunk_terms(B, w):
                dve.wait_ge(S["w_done"], NW * B + w + 1)
                at_ = 0
                for j in W_TILES[w]:
                    n = NK * (Q - j)
                    cols = slice(at_, at_ + CC * n)
                    ins = v_.tensor_tensor(pj[:, w, cols].rearrange("p (a t) -> p a t", a=CC),
                                           ring[(w + 1) % 2][:, cols].rearrange("p (a t) -> p a t", a=CC),
                                           gT.rearrange("p (a t) -> p a t", a=CC)[:, :, 0:n], ALU.mult)
                    at_ += CC * n
                ins.then_inc(S["p_ready"], 1)
                at_ = 0
                for j in W_TILES[w]:
                    n = NK * (Q - j)
                    if j:
                        dst = pj[:, 0].rearrange("p (a t) -> p a t", a=CC)[:, :, NK * j:T]
                        src = pj[:, w, at_:at_ + CC * n].rearrange("p (a t) -> p a t", a=CC)
                        dve.wait_ge(S["p_ready"], NW * B + w + 1)
                        if ACC_AT[j] or past(B, 1):
                            dve.wait_ge(S["acc_ready"], (Q - 1) * B + ACC_AT[j])
                        v_.tensor_tensor(dst, dst, src, ALU.add).then_inc(S["acc_ready"], 1)
                    at_ += CC * n

            def step(i, par):
                A, B, Cr = i + 2, i + 1, i
                if live(B):
                    dve.wait_ge(S["x2hi_ready"], B + 1)
                    if past(B, 1):
                        dve.wait_ge(S["ctxlo_ready"], B)
                        dve.wait_ge(S["ctxhi_ready"], B)
                    v_.tensor_tensor_scan(ctxT, ctx_decay[:, :, :].rearrange("p a t -> p (a t)"), B_XG[:, :], 0.0,
                                          ALU.mult, ALU.add).then_inc(S["ctx_ready"], 1)
                    v_.tensor_tensor(x2h[:, 1], B_XG[:, :], x2h[:, 0].bitcast(f32), ALU.subtract).then_inc(S["x2lo_ready"], 1)
                if live(Cr):
                    dve.wait_ge(S["gate_ready"], Cr + 1)
                    dve.wait_ge(S["soma_ready"], Cr + 1)
                    v_.scalar_tensor_tensor(sg, sg, 1.0, soma, ALU.add, ALU.mult).then_inc(S["sg_ready"], 1)
                if live(B):
                    dve.wait_ge(S["mt_ready"], B + 1)
                    v_.tensor_scalar(m, mt, 0.25, 0.5, ALU.mult, ALU.add).then_inc(S["m_ready"], 1)
                    dve.wait_ge(S["m_ready"], B + 1)
                    v_.tensor_scalar(msh[:, :], m, lo_rows[:, :], None, ALU.mult).then_inc(S["msh_ready"], 1)
                    dve.wait_ge(S["msh_ready"], B + 1)
                    v_.tensor_tensor(ms[:, :].rearrange("p (q k) -> p q k", q=Q), m.rearrange("p (k q) -> p q k", q=Q),
                                     msh[:, :].bitcast(f32).rearrange("p (k q) -> p q k", q=Q), ALU.subtract).then_inc(S["ms_ready"], 1)
                    dve.wait_ge(S["tg_ready"], B + 1)
                    v_.scalar_tensor_tensor(g, g, 1.0, x2, ALU.add, ALU.mult).then_inc(S["g_ready"], 1)
                    dve.wait_ge(S["mn_turned"], B + 1)
                    v_.tensor_tensor(amat, decay[:, :, :], mn_ps[:, 0:D].unsqueeze(1).to_broadcast([P, NK, D]), ALU.mult).then_inc(S["amat_ready"], 1)
                if live(B):
                    dve.wait_ge(S["gT_ready"], B + 1)
                    for w in range(3):
                        chunk_terms(B, w)
                if live(A):
                    dve.wait_ge(S["l0_done"], A + 1)
                    dve.wait_ge(S["x_loaded"][par], transfers(A, par))
                    if past(A, 1):
                        dve.wait_ge(S["xb_ready"], A)
                    v_.tensor_tensor(x1, B_A2[:, :], x_sb[:, par], ALU.add).then_inc(S["x1_ready"], 1)
                if live(B):
                    for w in range(3, NW):
                        chunk_terms(B, w)
                if live(Cr):
                    dve.wait_ge(S["out_done"], Cr + 1)
                    stats(B_C[:, :], st_c, 2, Cr)
                if live(A):
                    dve.wait_ge(S["l1_done"], A + 1)
                    if past(A, 1):
                        dve.wait_ge(S["n1_ready"], A)
                    v_.tensor_tensor(y, B_A2[:, :], x1, ALU.add).then_inc(S["y_ready"], 1)
                if live(Cr):
                    aggregate(st_c, mv_c, 2)
                if live(A):
                    dve.wait_ge(S["y_ready"], A + 1)
                    stats(y, st_a, 1, A)
                if live(B):
                    states_blend(B, 0)
                if live(A):
                    aggregate(st_a, mv_a, 1)
                if live(B):
                    for s_ in range(1, NG):
                        states_blend(B, s_)
                if live(A):
                    dve.wait_ge(S["beta_done"], A + 1)
                    if past(A, 1):
                        dve.wait_ge(S["x2_ready"], A)
                    v_.tensor_tensor(xb, B_A2[:, :], x1, ALU.add).then_inc(S["xb_ready"], 1)
                if live(Cr):
                    dve.wait_ge(S["ng2_ready"], Cr + 1)
                    dve.wait_ge(S["x2b_ready"], Cr + 1)
                    v_.tensor_tensor(x3, x3, x2b[:, par], ALU.add).then_inc(S["x3_ready"], 1)
                if live(A):
                    dve.wait_ge(S["n1_ready"], A + 1)
                    dve.wait_ge(S["gamma_done"], A + 1)
                    v_.tensor_tensor(n1, n1, B_A1[:, :], ALU.mult).then_inc(S["ng1_ready"], 1)
                    dve.wait_ge(S["ng1_ready"], A + 1)
                    if past(A, 1):
                        dve.wait_ge(S["x2b_ready"], A)
                        dve.wait_ge(S["x2T_turned"], A)
                    v_.tensor_tensor(x2, n1, xb, ALU.add).then_inc(S["x2_ready"], 1)
                if live(B):
                    dve.wait_ge(S["spread_done"], NG * (B + 1))
                    dve.wait_ge(S["acc_ready"], (Q - 1) * (B + 1))
                    if past(B, 1):
                        dve.wait_ge(S["gate_done"], B)
                    v_.tensor_tensor(tempT.rearrange("p (a k q) -> p a q k", a=CC, q=Q),
                                     B_WG[:, :].rearrange("p (a q k) -> p a q k", a=CC, q=Q),
                                     pj[:, 0].rearrange("p (a q k) -> p a q k", a=CC, q=Q), ALU.add).then_inc(S["temp_ready"], 1)
                if live(Cr):
                    dve.wait_ge(S["lap_done"], Cr + 1)
                    dve.wait_ge(S["nb_ready"], Cr + 1)
                    dve.wait_ge(S["nbe_ready"], Cr + 1)
                    v_.scalar_tensor_tensor(nb, nb, zb[:, par, 2:3], B_C[:, :], ALU.mult, ALU.add).then_inc(S["lap_ready"], 1)
                    dve.wait_ge(S["lap_ready"], Cr + 1)
                    dve.wait_ge(S["sq_ready"], Cr + 1)
                    if past(Cr, 2):
                        dve.wait_ge(S["out_stored"][par], transfers(Cr - 2, par))
                    v_.scalar_tensor_tensor(fin[:, par], sq, zb[:, par, 3:4], nb, ALU.mult, ALU.add).then_inc(S["fin_ready"], 1)

            steps(dve, step)

        @block.tensor
        def _(pe):
            mm = nc.tensor.matmul

            def turn(dst, src, n=CC):
                for a in range(n):
                    ins = nc.tensor.transpose(dst[:, a * P:(a + 1) * P], src[:, a * P:(a + 1) * P], ident[:, :])
                return ins

            def whole(dst, lhs, rhs, blocks=range(CC), start=False):
                for a in blocks:
                    ins = mm(dst, lhs[:, a * P:(a + 1) * P], rhs[:, a], start=(start and a == 0), stop=(a == CC - 1))
                return ins

            def split(dst, lhs, rhs, first=0, blocks=range(CC), stop=False):
                for a in blocks:
                    cols = slice(a * P, (a + 1) * P)
                    mm(dst, lhs[:, 0, cols], rhs[:, 0, first + a], start=False, stop=False)
                    mm(dst, lhs[:, 0, cols], rhs[:, 1, first + a], start=False, stop=False)
                    ins = mm(dst, lhs[:, 1, cols], rhs[:, 0, first + a], start=False, stop=(stop and a == CC - 1))
                return ins

            pe.wait_ge(ident_ready, 1)

            def slab(k, par):
                pe.wait_ge(raw_loaded[par], transfers(k, par))
                if past(k, 2):
                    pe.wait_ge(act_evac, evacuated(k - 2))
                    pe.wait_ge(dve_evac, evacuated(k - 2))
                raw = w0_t[:, par]
                for a in range(CC):
                    for o in range(CC):
                        ins = nc.tensor.transpose(slab_bank(par, a)[:, o * P:(o + 1) * P], raw[:, o, a * P:(a + 1) * P], ident[:, :])
                    ins.then_inc(slab_turned, 1)

            slabs(pe, slab)
            for k in range(NS, NSLAB):
                slab(k, k % 2)
            pe.wait_ge(const_loaded, N_CONST * 16)
            pe.wait_ge(act_evac, evacuated(NSLAB - 1))
            pe.wait_ge(dve_evac, evacuated(NSLAB - 1))
            turn(bank[0], wn1_raw)
            nc.tensor.transpose(bank[1][:, 0:P], wn2_raw, ident[:, :]).then_inc(wn_turned, 1)
            for a in range(CC):
                ins = nc.tensor.transpose(bank[2][:, a * D:(a + 1) * D], bl_raw[0:D, a * P:(a + 1) * P], ident[0:D, 0:D])
            ins.then_inc(blend_turned, 1)
            pe.wait_ge(blend_soft, KG)
            for a in range(CC):
                ins = nc.tensor.transpose(bank[3][:, a * P:(a + 1) * P], bl_rep[:, a].rearrange("p r d -> p (r d)"), ident[:, :])
            ins.then_inc(blend_back, 1)
            pe.wait_ge(consts_dve, 1)
            pe.wait_ge(wn_hi, 2)

            def ring_free(B, n):
                if n in (0, 1):
                    if past(B, 1):
                        pe.wait_ge(S["u_ready"], NG * B - 1 + n)
                elif n == 2:
                    pe.wait_ge(S["soma_ready"], B + 1)
                elif n < NW + 3:
                    pe.wait_ge(S["p_ready"], NW * B + n - 2)
                else:
                    pe.wait_ge(S["u_ready"], NG * B + n - NW - 2)

            def chunk_weights(B, w):
                ring_free(B, 1 + w)
                if w == 0:
                    pe.wait_ge(S["ms_ready"], B + 1)
                at_ = 0
                for j in W_TILES[w]:
                    n = NK * (Q - j)
                    for a in range(CC):
                        ins = mm(ring[(1 + w) % 2][:, at_ + a * n:at_ + (a + 1) * n], vj[:, j, a * P:(a + 1) * P],
                                 ms[:, 0:n], start=True, stop=True)
                    at_ += CC * n
                ins.then_inc(S["w_done"], 1)

            def state(B, s_):
                ring_free(B, NW + 1 + s_)
                mm(ring[s_ % 2][:, :], amat[:, s_ * KG:(s_ + 1) * KG, :].rearrange("p k d -> p (k d)"), g,
                   start=True, stop=True).then_inc(S["state_done"], 1)

            def spread_state(B, s_):
                pe.wait_ge(S["u_ready"], NG * B + s_ + 1)
                for a in range(CC):
                    dst = B_WG[:, a * T:(a + 1) * T].rearrange("p (q k) -> p q k", q=Q)[:, :, s_ * KG:(s_ + 1) * KG]
                    ins = mm(dst, u[:, s_ % 2, a * P:(a + 1) * P], spread[:, :, :], start=True, stop=True)
                ins.then_inc(S["spread_done"], 1)

            def step(i, par):
                A, B, Cr = i + 2, i + 1, i
                if live(B):
                    pe.wait_ge(S["x2_ready"], B + 1)
                    if past(B, 1):
                        pe.wait_ge(S["gT_ready"], B)
                    turn(B_XG, x2).then_inc(S["x2T_turned"], 1)
                if live(Cr):
                    pe.wait_ge(S["temp_ready"], Cr + 1)
                    if past(Cr, 1):
                        pe.wait_ge(S["lap_ready"], Cr)
                    mm(B_C[:, :], ones[:, :], table("btemp"), start=True, stop=False)
                    whole(B_C[:, :], tempT, wtemp_t).then_inc(S["gate_done"], 1)
                if live(B):
                    pe.wait_ge(S["x2hi_ready"], B + 1)
                    pe.wait_ge(S["x2lo_ready"], B + 1)
                    if past(B, 1):
                        pe.wait_ge(S["amat_ready"], B)
                    mm(h1_ps, ones[:, :], table("bn1"), start=True, stop=False)
                    split(h1_ps, x2h, wn1_r, stop=True).then_inc(S["h1_done"], 1)
                    if past(B, 1):
                        pe.wait_ge(S["temp_ready"], B)
                    mm(B_WG[:, :], ones[:, :], table("bg"), start=True, stop=False)
                    split(B_WG[:, :], x2h, wg_r)
                    pe.wait_ge(S["h1_ready"], B + 1)
                    nc.tensor.transpose(h1T_ps, h1, ident[:, :]).then_inc(S["h1T_turned"], 1)
                    pe.wait_ge(S["ctxhi_ready"], B + 1)
                    pe.wait_ge(S["ctxlo_ready"], B + 1)
                    split(B_WG[:, :], ctxh, wg_r, CC, range(2))
                    pe.wait_ge(S["h1T_ready"], B + 1)
                    mm(mt_ps, wn2_t[:, :], h1T, start=True, stop=True).then_inc(S["mod_done"], 1)
                    split(B_WG[:, :], ctxh, wg_r, CC, range(2, CC), stop=True).then_inc(S["wg_done"], 1)
                if live(Cr):
                    pe.wait_ge(S["sg_ready"], Cr + 1)
                    turn(B_C, sg).then_inc(S["sgT_turned"], 1)
                if live(A):
                    pe.wait_ge(S["x_loaded"][par], transfers(A, par))
                    if past(A, 1):
                        pe.wait_ge(S["ng1_ready"], A)
                    turn(B_A1, x_sb[:, par]).then_inc(S["xT_turned"], 1)
                if live(B):
                    ring_free(B, 0)
                    mm(B_R0[:, :], ones[:, :], table("bsoma"), start=True, stop=False)
                    split(B_R0[:, :], x2h, wsoma_r, blocks=range(2))
                    pe.wait_ge(S["m_ready"], B + 1)
                    nc.tensor.transpose(mn_ps, m, ident[:, :]).then_inc(S["mn_turned"], 1)
                    split(B_R0[:, :], x2h, wsoma_r, blocks=range(2, CC), stop=True).then_inc(S["soma_done"], 1)
                    pe.wait_ge(S["g_ready"], B + 1)
                    turn(B_XG, g).then_inc(S["gT_turned"], 1)
                if live(A):
                    pe.wait_ge(S["xT_ready"], A + 1)
                    pe.wait_ge(S["w0_loaded"][par], transfers(A, par))
                    pe.wait_ge(S["subj_set"], A + 1)
                    if past(A, 1):
                        pe.wait_ge(S["xb_ready"], A)
                    mm(B_A2[:, :], subj_rows[:, :], table("b0"), start=True, stop=False)
                for a in range(CC):
                    if live(A):
                        ins = whole(B_A2[:, :], actT, w0_t[:, par], (a,))
                        if a == CC - 1:
                            ins.then_inc(S["l0_done"], 1)
                    if live(B):
                        chunk_weights(B, a)
                if live(Cr):
                    pe.wait_ge(S["sgT_ready"], Cr + 1)
                    whole(B_C[:, :], sgT, wout_t, (0,), start=True)
                if live(B):
                    chunk_weights(B, NW - 1)
                if live(A):
                    pe.wait_ge(S["x1_ready"], A + 1)
                    turn(B_A1, x1).then_inc(S["x1T_turned"], 1)
                if live(Cr):
                    whole(B_C[:, :], sgT, wout_t, (1,))
                if live(A):
                    pe.wait_ge(S["x1T_ready"], A + 1)
                    pe.wait_ge(S["w1_loaded"][par], transfers(A, par))
                    pe.wait_ge(S["lang_set"], A + 1)
                    mm(B_A1[:, 0:H1], lang_rows[:, :], table("b1"), start=True, stop=False)
                    whole(B_A1[:, 0:H1], actT, w1_t[:, par]).then_inc(S["h_done"], 1)
                if live(Cr):
                    whole(B_C[:, :], sgT, wout_t, (2,))
                if live(A):
                    pe.wait_ge(S["h_ready"], A + 1)
                    nc.tensor.transpose(B_A1[:, H1:2 * H1], h, ident[:, :]).then_inc(S["hT_turned"], 1)
                if live(Cr):
                    whole(B_C[:, :], sgT, wout_t, (3,)).then_inc(S["out_done"], 1)
                if live(A):
                    pe.wait_ge(S["hT_ready"], A + 1)
                    pe.wait_ge(S["w2_loaded"][par], transfers(A, par))
                    mm(B_A2[:, :], lang_rows[:, :], table("b2"), start=True, stop=False)
                    mm(B_A2[:, :], hT, w2_t[:, par], start=False, stop=True).then_inc(S["l1_done"], 1)
                    mm(B_A1[:, :], lang_rows[:, :], table("gamma"), start=True, stop=True).then_inc(S["gamma_done"], 1)
                if live(B):
                    pe.wait_ge(S["amat_ready"], B + 1)
                    state(B, 0)
                    state(B, 1)
                if live(A):
                    pe.wait_ge(S["y_ready"], A + 1)
                    mm(B_A2[:, :], lang_rows[:, :], table("beta"), start=True, stop=True).then_inc(S["beta_done"], 1)
                if live(B):
                    state(B, 2)
                    spread_state(B, 0)
                    state(B, 3)
                    for s_ in range(1, NG):
                        spread_state(B, s_)
                if live(Cr):
                    pe.wait_ge(S["x3_ready"], Cr + 1)
                    pe.wait_ge(S["mix_set"], 3 * (Cr + 1))
                    mm(B_C[:, :], mix, x3, start=True, stop=True).then_inc(S["lap_done"], 1)

            steps(pe, step)


_INS = ["x", "itok_B_0_7", "itok_B_0_8", "condB_tauraws", "cond_256", "condB_bn2", "cond_1024", "condB_zX",
        "condB_zY", "condB_zR", "L0_cond_weight", "L0_cond_bias", "L1_cond_W1", "L1_cond_b1", "L1_cond_W2",
        "L1_cond_b2", "L1_cond_gamma", "L1_cond_beta", "L2_cond_tau_ctx", "L2_cond_Wg", "L2_cond_bg",
        "L2_cond_Wn1", "L2_cond_bn1", "L2_cond_Wsoma", "L2_cond_bsoma", "L2_cond_Wtemp", "L2_cond_btemp",
        "L2_cond_Wout", "L2_cond_gamma", "L2_cond_beta"]


def kernel(**inputs):
    import numpy as np
    import concourse.bacc as bacc
    from concourse.bass_utils import run_bass_kernel_spmd

    nc = bacc.Bacc("TRN2", target_bir_lowering=False, num_devices=1)
    arrays, args = {}, []
    for name in _INS:
        a = np.ascontiguousarray(inputs[name])
        a = a.reshape(a.shape or (1,))
        arrays[f"in_{name}"] = a
        args.append(nc.dram_tensor(f"in_{name}", a.shape, mybir.dt.from_np(a.dtype), kind="ExternalInput").ap())
    shape = arrays["in_x"].shape
    args.append(nc.dram_tensor("out_0", shape, mybir.dt.float32, kind="ExternalOutput").ap())
    cond_resid_kernel(nc, *args)
    r = run_bass_kernel_spmd(nc, [arrays], core_ids=[0])
    return r.results[0]["out_0"]
```

```python
import concourse.bass as bass
from concourse import mybir
from contextlib import ExitStack


def cond_resid_kernel(nc, x, subject, language, tau, wn2, bn2, blend, zx, zy, zr, l0_w, l0_b,
                      l1_w1, l1_b1, l1_w2, l1_b2, l1_gamma, l1_beta, tau_ctx, wg, bg, wn1, bn1,
                      wsoma, bsoma, wtemp, btemp, wout, l2_gamma, l2_beta, out):
    f32, f32r, bf16, i32 = mybir.dt.float32, mybir.dt.float32r, mybir.dt.bfloat16, mybir.dt.int32
    ALU, ACT, AX = mybir.AluOpType, mybir.ActivationFunctionType, mybir.AxisListType

    P = 128
    NB, T, C = x.shape
    NS = l0_w.shape[0]
    NL, _, H1 = l1_w1.shape
    D = tau.shape[0]
    HN = wn1.shape[0]
    CC = C // P
    Q = 8
    NK = T // Q
    KG = P // D
    NG = NK // KG
    QUAD = 32
    EPS = 1e-5
    W_TILES = [(0,), (1, 7), (2, 6), (3, 5), (4,)]
    NW = len(W_TILES)
    assert T == P and D == QUAD and C == 512 and H1 == P and HN == P and NL <= QUAD and NS <= QUAD

    with ExitStack() as ctx:
        def sb(name, shape, dt=f32):
            return ctx.enter_context(nc.sbuf_tensor(name, shape, dt))

        def sem(name):
            return ctx.enter_context(nc.semaphore(name))

        wg_r = sb("wg_r", [P, 2, 2 * CC, C], f32r)
        wsoma_r = sb("wsoma_r", [P, 2, CC, C], f32r)
        wn1_r = sb("wn1_r", [P, 2, CC, HN], f32r)
        wtemp_r = sb("wtemp_r", [P, 2, CC, C], f32r)
        wout_r = sb("wout_r", [P, 2, CC, C], f32r)
        wn2_t = sb("wn2_t", [P, P])
        w0_t = sb("w0_t", [P, CC, C])
        w1_t = sb("w1_t", [P, CC, H1])
        w2_t = sb("w2_t", [P, C])
        gamma_t = sb("gamma_t", [P, C])
        l0_wt_dram = nc.dram_tensor("l0_wt_dram", (NS, P, CC * C), f32, kind="Internal").ap()
        PART_ROW = (0, 2 * QUAD, 3 * QUAD)
        TB = {}
        at = 0
        for name, width in (("b0", C), ("b2", C), ("bg", C), ("bsoma", C),
                            ("btemp", C), ("b1", H1), ("bn1", HN)):
            TB[name] = (at, width)
            at += width
        tables = sb("tables", [P, at], bf16)
        n_table = at

        def table(name):
            o, w = TB[name]
            return tables[:, o:o + w]

        ones = sb("ones", [P, P], bf16)
        subj_hot = sb("subj_hot", [P, NB], bf16)
        lang_hot = sb("lang_hot", [P, NB], bf16)
        subj_rows = sb("subj_rows", [P, T], bf16)
        lang_rows = sb("lang_rows", [P, T], bf16)
        ident = sb("ident", [P, P])
        neigh = sb("neigh", [P, P])
        decay = sb("decay", [P, NK, D])
        spread = sb("spread", [P, KG, Q])
        blend_n = sb("blend_n", [P, C])
        vj = sb("vj", [P, Q, C], f32r)
        ctx_decay = sb("ctx_decay", [P, CC, T])
        gamma2 = sb("gamma2", [P, C])
        beta2 = sb("beta2", [P, C])
        zt = sb("zt", [P, NB, 4])
        zb = sb("zb", [P, 2, 4])
        bn2_c = sb("bn2_c", [P, 1])
        lo_rows = sb("lo_rows", [P, 1])
        scal = sb("scal", [P, 3])
        ids_sb = sb("ids_sb", [1, 2, NB], i32)
        n_work = 0
        plan = {}
        for name, width in (("actT", C), ("x1", C), ("h", H1), ("hT", H1), ("y", C),
                            ("n1", C), ("xb", C), ("x2", C), ("ctxT", C), ("g", C), ("gT", C), ("h1", HN),
                            ("h1T", HN), ("mt", T), ("m", T), ("pj", 3 * C),
                            ("u", NG * C), ("tempT", C), ("soma", C),
                            ("x3", C), ("x2b", 2 * C), ("sq", C), ("nb", C), ("fin", C),
                            ("mix", P), ("mixt", P), ("mixi", P), ("small", 64), ("x", C)):
            plan[name] = (n_work, width)
            n_work += width
        work = sb("work", [P, n_work])

        def buf(name):
            o, w = plan[name]
            return work[:, o:o + w]

        x_sb, fin = buf("x"), buf("fin")
        actT, x1, h, hT, y, n1, xb, x2 = (buf(n) for n in ("actT", "x1", "h", "hT", "y", "n1", "xb", "x2"))
        ctxT, g, gT, h1, h1T, mt, m = (buf(n) for n in ("ctxT", "g", "gT", "h1", "h1T", "mt", "m"))
        pj = buf("pj").rearrange("p (w c) -> p w c", w=3)
        u = buf("u").rearrange("p (a c) -> p a c", a=NG)
        tempT, soma, x3 = (buf(n) for n in ("tempT", "soma", "x3"))
        amat = u[:, NG - 1]
        tn = actT
        sg = tempT
        x2b = buf("x2b").rearrange("p (a c) -> p a c", a=2)
        sq, nb = buf("sq"), buf("nb")
        mix, mixt, mixi = buf("mix"), buf("mixt"), buf("mixi")
        sm = buf("small")
        st_a, mv_a, rs_a = sm[:, 0:6], sm[:, 8:10], sm[:, 12:15]
        st_c, mv_c, rs_c = sm[:, 16:22], sm[:, 24:26], sm[:, 28:31]
        prep = [n_table]

        def scratch(width, dt=f32):
            v = work[:, prep[0]:prep[0] + width]
            prep[0] += width
            assert prep[0] <= plan["x"][0]
            return v.bitcast(dt) if dt is not f32 else v

        wt_buf = scratch(2 * CC * C).rearrange("p (b a c) -> p b a c", b=2, a=CC)
        vtmp = wt_buf.rearrange("p b a c -> p (b a) c")
        raw_slab = [scratch(CC * C).rearrange("p (a c) -> p a c", a=CC), w0_t[:, :, :]]
        lnat, lnat2 = scratch(D + 2), scratch(D + 2)
        zraw = scratch(3 * NB).rearrange("p (z b) -> p z b", z=3)
        idr = scratch(2 * NB, i32).rearrange("p (z b) -> p z b", z=2)
        idf = scratch(2 * NB).rearrange("p (z b) -> p z b", z=2)
        wn1_raw, wn2_raw, bl_raw = scratch(C), scratch(P), scratch(C)
        e_decay = scratch(NK * D, i32).rearrange("p (k d) -> p k d", k=NK)
        e_spread = scratch(Q * KG, i32).rearrange("p (k q) -> p k q", q=Q)
        e_spread_f = scratch(Q * KG).rearrange("p (k q) -> p k q", q=Q)
        e_j, e_p = scratch(Q, i32), scratch(1, i32)
        e_j_f, p_f, alpha_j, alpha_ctx = scratch(Q), scratch(1), scratch(Q), scratch(1)
        bl_m = scratch(CC)
        bl_t = scratch(CC * D).rearrange("p (a d) -> p a d", a=CC)
        bl_rep = scratch(CC * KG * D).rearrange("p (a r d) -> p a r d", a=CC, r=KG)
        x2h = sb("x2h", [P, 2, C], f32r)
        ctxh = sb("ctxh", [P, 2, C], f32r)
        temph = sb("temph", [P, 2, C], f32r)
        sgh = ctxh
        gh = temph
        amath = sb("amath", [P, 2, C], f32r)
        ms = sb("ms", [P, T], f32r)
        msh = sb("msh", [P, T], f32r)

        bank = [ctx.enter_context(nc.psum_tensor(f"bank{i}", [P, C], f32)) for i in range(8)]
        B_XG, B_C, B_A1, B_MOD, B_WG, B_R0, B_A2, B_R1 = bank
        h1_ps, h1T_ps, mt_ps, mn_ps = (B_MOD[:, 0:HN], B_MOD[:, P:2 * P], B_MOD[:, 2 * P:3 * P],
                                       B_MOD[:, 3 * P:4 * P])
        ring = [B_R0, B_R1]
        state_bank = [B_R0, B_R1, B_WG, B_R0]

        ident_ready = sem("ident_ready")
        raw_loaded = [sem("raw_loaded_even"), sem("raw_loaded_odd")]
        slab_turned = sem("slab_turned")
        act_evac = sem("act_evac")
        dve_evac = sem("dve_evac")
        wt_stored = [sem("wt_stored_even"), sem("wt_stored_odd")]
        const_loaded = sem("const_loaded")
        ids_loaded = sem("ids_loaded")
        rows_zeroed = sem("rows_zeroed")
        rows_loaded = sem("rows_loaded")
        iota_ready = sem("iota_ready")
        pool_done = sem("pool_done")
        dchain = sem("dve_step_done")
        achain = sem("act_step_done")
        lna_ready = sem("lna_ready")
        expo_ready = sem("expo_ready")
        raw_decay = sem("raw_decay")
        blend_turned = sem("blend_turned")
        blend_soft = sem("blend_soft")
        blend_back = sem("blend_back")
        blend_shift = sem("blend_shift")
        blend_exp = sem("blend_exp")
        wn_turned = sem("wn_turned")
        blend_copied = sem("blend_copied")
        vj_full = sem("vj_full")
        vj_hi = sem("vj_hi")
        vj_lo = sem("vj_lo")
        consts_dve = sem("consts_dve")
        hot_ready = sem("hot_ready")
        zt_ready = sem("zt_ready")
        S = {n: sem(n) for n in ("x_loaded", "w0_loaded", "w1_loaded", "w2_loaded", "gamma_loaded", "beta_loaded",
                                 "out_stored")}
        names = """subj_set lang_set zb_set mix_set
            xT_turned xT_ready l0_done x1_ready x1T_turned x1T_ready h_done h_ready hT_turned hT_ready
            l1_done y_ready st1_ready mv1_ready ve1_ready rs1_ready nm1_ready n1_ready 
            ng1_ready xb_ready x2_ready x2T_turned ctx_ready x2hi_ready x2lo_ready ctxhi_ready ctxlo_ready
            h1_done h1_ready h1T_turned h1T_ready mod_done mt_ready m_ready msh_ready ms_ready mn_turned
            amat_ready wg_done tg_ready g_ready gT_turned gT_ready w_done p_ready acc_ready soma_done
            soma_ready state_done u_ready spread_done tn_ready tn_turned temp_ready x2b_ready gate_done gate_ready sg_ready
            temphi_ready templo_ready sgTlo_ready ghi_ready glo_ready amathi_ready amatlo_ready
            sgT_turned sgT_ready out_done st2_ready mv2_ready ve2_ready rs2_ready nm2_ready n2_ready
            ng2_ready x3_ready sq_ready nb_ready nbe_ready lap_done lap_ready fin_ready""".split()
        S.update({n: sem(n) for n in names})

        def transfers(b, par):
            return 8 * b + 16 - 8 * par

        def live(b):
            return not isinstance(b, int) or 0 <= b < NB

        def past(b, n):
            return not isinstance(b, int) or b >= n

        def steps(engine, step):
            for i in (-2, -1, 0, 1):
                step(i, i % 2)
            with engine.Fori(2, NB - 3, 2) as i:
                step(i, 0)
                step(i + 1, 1)
            for i in (NB - 2, NB - 1):
                step(i, i % 2)

        def slab_sources():
            return [wg[:, 0:C], wg[:, C:2 * C], wsoma, wtemp, wout]

        NSLAB = NS + 5
        N_CONST = 11 + 3 * KG
        N_POOL = 6 + 4 + 3
        ACC_AT = {j: n for n, j in enumerate(j for js in W_TILES for j in js if j)}

        def slab_bank(par, a):
            return bank[4 * par + a][:, :]

        def act_copies(k):
            return CC * (k + 1) + (0 if not isinstance(k, int) or k < NS - 2 else 2)

        def dve_copies(k):
            return CC * (k + 1 - NS) + 1

        def slabs(engine, slab, small):
            slab(0, 0)
            slab(1, 1)
            with engine.Fori(2, NS - 3, 2) as k:
                slab(k, 0)
                slab(k + 1, 1)
            small()
            slab(NS - 2, 0)
            slab(NS - 1, 1)
        block = ctx.enter_context(nc.Block())

        @block.sync
        def _(sp):
            with nc.allow_non_contiguous_dma(reason="small constant rows and columns"):
                def load_slab(k, par, src):
                    if past(k, 2):
                        sp.wait_ge(slab_turned, (k - 1) * CC)
                    sp.dma_start(raw_slab[par], src.rearrange("(a p) c -> p a c", p=P)).then_inc(raw_loaded[par], 16)

                def store_slab(k, par):
                    sp.wait_ge(act_evac, act_copies(k))
                    sp.dma_start(l0_wt_dram[bass.ds(k, 1)].rearrange("a p c -> (a p) c"),
                                 wt_buf[:, par].rearrange("p a c -> p (a c)")).then_inc(wt_stored[par], 16)

                load_slab(0, 0, l0_w[0])
                load_slab(1, 1, l0_w[1])
                sp.dma_start(ids_sb[0:1, 0, :], subject.rearrange("(a b) -> a b", a=1)).then_inc(ids_loaded, 16)
                sp.dma_start(ids_sb[0:1, 1, :], language.rearrange("(a b) -> a b", a=1)).then_inc(ids_loaded, 16)
                with sp.Fori(2, NS - 1, 2) as k:
                    for par in range(2):
                        load_slab(k + par, par, l0_w[bass.ds(k + par, 1)].rearrange("a o c -> (a o) c"))
                        store_slab(k - 2 + par, par)
                for m_, src in enumerate(slab_sources()):
                    load_slab(NS + m_, (NS + m_) % 2, src)
                    if m_ < 2:
                        store_slab(NS - 2 + m_, m_)
                sp.wait_ge(ids_loaded, 2 * 16)
                for par in range(2):
                    sp.wait_ge(wt_stored[par], 8 * NS)
                sp.wait_ge(slab_turned, (NSLAB - 1) * CC)

                def load_row(b):
                    s_id = sp.value_load(ids_sb[0:1, 0, bass.ds(b, 1)], min_val=0, max_val=NS - 1)
                    l_id = sp.value_load(ids_sb[0:1, 1, bass.ds(b, 1)], min_val=0, max_val=NL - 1)
                    if past(b, 1):
                        sp.wait_ge(S["l0_done"], b)
                    sp.dma_start(w0_t[:, :, :].rearrange("p a c -> p (a c)"),
                                 l0_wt_dram[bass.ds(s_id, 1)].rearrange("a p c -> (a p) c")).then_inc(S["w0_loaded"], 16)
                    if past(b, 1):
                        sp.wait_ge(S["x1_ready"], b)
                    sp.dma_start(x_sb, x[bass.ds(b, 1)].rearrange("a t c -> (a t) c")).then_inc(S["x_loaded"], 16)
                    if past(b, 1):
                        sp.wait_ge(S["h_done"], b)
                    sp.dma_start(w1_t[:, :, :], l1_w1[bass.ds(l_id, 1)].rearrange("l (a p) h -> p (l a) h", p=P)).then_inc(S["w1_loaded"], 16)
                    if past(b, 1):
                        sp.wait_ge(S["l1_done"], b)
                    sp.dma_start(w2_t[:, :], l1_w2[bass.ds(l_id, 1)].rearrange("l h c -> (l h) c")).then_inc(S["w2_loaded"], 16)
                    if past(b, 1):
                        sp.wait_ge(S["ng1_ready"], b)
                    sp.dma_start(gamma_t[:, :], l1_gamma[bass.ds(l_id, 1)].rearrange("l c -> (l c)").partition_broadcast(P)).then_inc(S["gamma_loaded"], 16)
                    if past(b, 1):
                        sp.wait_ge(S["x2_ready"], b)
                    sp.dma_start(xb, l1_beta[bass.ds(l_id, 1)].rearrange("l c -> (l c)").partition_broadcast(P)).then_inc(S["beta_loaded"], 16)

                def store_row(b):
                    sp.wait_ge(S["fin_ready"], b + 1)
                    sp.dma_start(out[bass.ds(b, 1)].rearrange("a t c -> (a t) c"), fin).then_inc(S["out_stored"], 16)

                def step(i, par):
                    if live(i + 2):
                        load_row(i + 2)
                    if live(i - 1):
                        store_row(i - 1)

                steps(sp, step)
                store_row(NB - 1)
                sp.wait_ge(S["out_stored"], 16 * NB)

        @block.gpsimd
        def _(pool):
            g_ = nc.gpsimd
            g_.memset(ident[:, :], 0.0).then_inc(pool_done, 1)
            pool.wait_ge(pool_done, 1)
            g_.affine_select(out=ident[:, :], in_=ident[:, :], compare_op=ALU.not_equal, fill=1.0, base=0,
                             pattern=[[-1, P]], channel_multiplier=1).then_inc(ident_ready, 1)
            with nc.allow_non_contiguous_dma(reason="small constant rows and columns"):
                def one(dst, src):
                    pool.dma_start(dst, src).then_inc(const_loaded, 16)
                taus = lnat[:, 0:D]
                one(taus, tau.partition_broadcast(P))
                one(lnat[:, D + 1:D + 2], tau_ctx.partition_broadcast(P))
                one(gamma2[:, :], l2_gamma.partition_broadcast(P))
                one(beta2[:, :], l2_beta.partition_broadcast(P))
                one(zraw[:, 0], zx.partition_broadcast(P))
                one(zraw[:, 1], zy.partition_broadcast(P))
                one(zraw[:, 2], zr.partition_broadcast(P))
                one(idr[:, 0], subject.partition_broadcast(P))
                one(idr[:, 1], language.partition_broadcast(P))
                one(wn1_raw, wn1)
                one(bl_raw[0:D, :], blend)
                for r in range(KG):
                    rows = slice(r * D, (r + 1) * D)
                    one(lnat[rows, D:D + 1], tau.rearrange("(d a) -> d a", a=1))
                    one(bn2_c[rows, :], bn2.rearrange("(d a) -> d a", a=1))
                    one(wn2_raw[rows, :], wn2)
            g_.iota(e_decay, pattern=[[Q, NK], [0, D]], base=-1, channel_multiplier=-1).then_inc(iota_ready, 1)
            g_.iota(e_spread, pattern=[[0, KG], [1, Q]], base=1, channel_multiplier=0).then_inc(iota_ready, 1)
            g_.iota(e_j, pattern=[[1, Q]], base=0, channel_multiplier=0).then_inc(iota_ready, 1)
            g_.iota(e_p, pattern=[[0, 1]], base=0, channel_multiplier=1).then_inc(iota_ready, 1)
            g_.memset(ones[:, :], 1.0).then_inc(pool_done, 1)
            for n, value in enumerate((-0.5, EPS, -1.0)):
                g_.memset(scal[:, n:n + 1], value).then_inc(pool_done, 1)
            g_.memset(neigh[:, :], 0.0).then_inc(pool_done, 1)
            n_done = 6
            for cols, base, fill in ((slice(0, P), 1, 1.0), (slice(0, P), -1, 1.0), (slice(0, 1), -1, 2.0),
                                     (slice(P - 1, P), 2 - P, 2.0)):
                width = cols.stop - cols.start
                pool.wait_ge(pool_done, n_done)
                g_.affine_select(out=neigh[:, cols], in_=neigh[:, cols], compare_op=ALU.not_equal, fill=fill,
                                 base=base, pattern=[[-1, width]], channel_multiplier=1).then_inc(pool_done, 1)
                n_done += 1
            pool.wait_ge(raw_decay, 2)
            g_.affine_select(out=decay[:, :, :], in_=decay[:, :, :], compare_op=ALU.is_ge, fill=0.0, base=-1,
                             pattern=[[Q, NK], [0, D]], channel_multiplier=-1).then_inc(pool_done, 1)
            g_.affine_select(out=spread[:, :, :], in_=spread[:, :, :], compare_op=ALU.is_ge, fill=0.0, base=0,
                             pattern=[[-D, KG], [0, Q]], channel_multiplier=1).then_inc(pool_done, 1)
            n_done += 2
            pool.wait_ge(pool_done, n_done)
            g_.affine_select(out=spread[:, :, :], in_=spread[:, :, :], compare_op=ALU.is_ge, fill=0.0, base=D - 1,
                             pattern=[[D, KG], [0, Q]], channel_multiplier=-1).then_inc(pool_done, 1)
            n_done += 1
            assert n_done == N_POOL
            pool.wait_ge(pool_done, n_done)
            for j in range(Q):
                pool.wait_ge(vj_hi, j + 1)
                g_.tensor_tensor(vj[P // 2:P, j], vtmp[P // 2:P, j], vj[P // 2:P, j].bitcast(f32), ALU.subtract).then_inc(vj_lo, 1)
            pool.wait_ge(hot_ready, 2)
            pool.wait_ge(zt_ready, 1)
            pool.wait_ge(pool_done, n_done)
            pool.wait_ge(consts_dve, 1)

            def add_terms(B, w):
                pool.wait_ge(S["p_ready"], NW * B + w + 1)
                at_ = 0
                for j in W_TILES[w]:
                    n = NK * (Q - j)
                    dst = pj[:, 0].rearrange("p (a t) -> p a t", a=CC)[:, :, NK * j:T]
                    src = pj[:, 1 + w % 2, at_:at_ + CC * n].rearrange("p (a t) -> p a t", a=CC)
                    if ACC_AT[j] or past(B, 1):
                        pool.wait_ge(S["acc_ready"], (Q - 1) * B + ACC_AT[j])
                    g_.tensor_tensor(dst, dst, src, ALU.add).then_inc(S["acc_ready"], 1)
                    at_ += CC * n

            def rstd(par_mv, par_rs, n, b):
                pool.wait_ge(S[f"mv{n}_ready"], b + 1)
                if past(b, 1):
                    pool.wait_ge(S[f"n{n}_ready"], b)
                g_.tensor_tensor(par_rs[:, 0:1], par_mv[:, 1:2], scal[:, 1:2], ALU.add)
                g_.tensor_tensor(par_rs[:, 2:3], par_mv[:, 0:1], scal[:, 2:3], ALU.mult).then_inc(S[f"ve{n}_ready"], 1)
                pool.wait_ge(S[f"ve{n}_ready"], b + 1)
                g_.tensor_tensor(par_rs[:, 1:2], par_rs[:, 0:1], scal[:, 0:1], ALU.pow).then_inc(S[f"rs{n}_ready"], 1)
                pool.wait_ge(S[f"rs{n}_ready"], b + 1)
                g_.tensor_tensor(par_rs[:, 2:3], par_rs[:, 2:3], par_rs[:, 1:2], ALU.mult).then_inc(S[f"nm{n}_ready"], 1)

            def step(i, par):
                A, B, Cr = i + 2, i + 1, i
                if live(A):
                    if past(A, 1):
                        pool.wait_ge(S["l0_done"], A)
                    g_.tensor_copy(subj_rows[:, :], subj_hot[:, bass.ds(A, 1)].to_broadcast([P, T])).then_inc(S["subj_set"], 1)
                    if past(A, 1):
                        pool.wait_ge(S["l1_done"], A)
                    g_.tensor_copy(lang_rows[:, :], lang_hot[:, bass.ds(A, 1)].to_broadcast([P, T])).then_inc(S["lang_set"], 1)
                if live(B):
                    pool.wait_ge(S["x2_ready"], B + 1)
                    if past(B, 2):
                        pool.wait_ge(S["x3_ready"], B - 1)
                    g_.tensor_tensor(x2b[:, 1 - par], x2, beta2[:, :], ALU.add).then_inc(S["x2b_ready"], 1)
                    pool.wait_ge(S["ctxhi_ready"], B + 1)
                    g_.tensor_tensor(ctxh[:, 1], ctxT, ctxh[:, 0].bitcast(f32), ALU.subtract).then_inc(S["ctxlo_ready"], 1)
                if live(Cr):
                    if past(Cr, 2):
                        pool.wait_ge(S["fin_ready"], Cr - 1)
                    g_.tensor_copy(zb[:, par], zt[:, bass.ds(Cr, 1), :].rearrange("p a z -> p (a z)")).then_inc(S["zb_set"], 1)
                    pool.wait_ge(S["zb_set"], Cr + 1)
                    if past(Cr, 1):
                        pool.wait_ge(S["lap_done"], Cr)
                    g_.tensor_tensor(mixt, neigh[:, :], zb[:, par, 1:2].to_broadcast([P, P]), ALU.mult).then_inc(S["mix_set"], 1)
                    g_.tensor_tensor(mixi, ident[:, :], zb[:, par, 0:1].to_broadcast([P, P]), ALU.mult).then_inc(S["mix_set"], 1)
                    pool.wait_ge(S["mix_set"], 3 * Cr + 2)
                    g_.tensor_tensor(mix, mixt, mixi, ALU.add).then_inc(S["mix_set"], 1)
                if live(B):
                    pool.wait_ge(S["ghi_ready"], B + 1)
                    g_.tensor_tensor(gh[:, 1], g, gh[:, 0].bitcast(f32), ALU.subtract).then_inc(S["glo_ready"], 1)
                    for w in range(1, NW - 1):
                        add_terms(B, w)
                if live(A):
                    pool.wait_ge(S["beta_loaded"], 16 * (A + 1))
                    pool.wait_ge(S["x1_ready"], A + 1)
                    g_.tensor_tensor(xb, xb, x1, ALU.add).then_inc(S["xb_ready"], 1)
                if live(Cr):
                    rstd(mv_c, rs_c, 2, Cr)
                if live(A):
                    rstd(mv_a, rs_a, 1, A)
                if live(Cr):
                    pool.wait_ge(S["n2_ready"], Cr + 1)
                    g_.tensor_tensor(x3, x3, gamma2[:, :], ALU.mult).then_inc(S["ng2_ready"], 1)
                    pool.wait_ge(S["ng2_ready"], Cr + 1)
                    g_.tensor_tensor(x3, x3, x2b[:, par], ALU.add).then_inc(S["x3_ready"], 1)
                    pool.wait_ge(S["x3_ready"], Cr + 1)
                    if past(Cr, 1):
                        pool.wait_ge(S["lap_ready"], Cr)
                    g_.tensor_tensor(nb[:, 1:C - 1], x3[:, 0:C - 2], x3[:, 2:C], ALU.add).then_inc(S["nb_ready"], 1)
                    g_.tensor_tensor(nb[:, 0:C:C - 1], x3[:, 1:C - 1:C - 3], x3[:, 1:C - 1:C - 3], ALU.add).then_inc(S["nbe_ready"], 1)
                if live(B):
                    add_terms(B, NW - 1)

            steps(pool, step)

        @block.scalar
        def _(act):
            a_ = nc.scalar
            with nc.allow_non_contiguous_dma(reason="small constant rows"):
                act.wait_ge(rows_zeroed, 1)
                stage = work[:, 0:n_table]
                for r in PART_ROW:
                    for name, src, n in (("b0", l0_b, NS), ("b1", l1_b1, NL), ("b2", l1_b2, NL)):
                        o, w = TB[name]
                        act.dma_start(stage[r:r + n, o:o + w], src).then_inc(rows_loaded, 16)
                    for name, src in (("bg", bg), ("bsoma", bsoma), ("btemp", btemp), ("bn1", bn1)):
                        o, w = TB[name]
                        act.dma_start(stage[r:r + 1, o:o + w], src.rearrange("(a c) -> a c", a=1)).then_inc(rows_loaded, 16)

            def slab(k, par):
                if past(k, 2):
                    act.wait_ge(wt_stored[par], transfers(k - 2, par))
                for a in range(CC):
                    act.wait_ge(slab_turned, k * CC + a + 1)
                    a_.activation(wt_buf[:, par, a], slab_bank(par, a), ACT.Copy).then_inc(act_evac, 1)

            def small():
                act.wait_ge(wn_turned, 1)
                a_.activation(wn1_r[:, 0].rearrange("p a h -> p (a h)"), bank[0][:, :], ACT.Copy).then_inc(act_evac, 1)
                a_.activation(wn2_t[:, :], bank[1][:, 0:P], ACT.Copy).then_inc(act_evac, 1)
                act.wait_ge(blend_shift, 1)
                a_.activation(bl_t, bl_t, ACT.Exp).then_inc(blend_exp, 1)
                act.wait_ge(const_loaded, N_CONST * 16)
                a_.activation(lnat2, lnat, ACT.Abs).then_inc(achain, 1)
                act.wait_ge(achain, 1)
                a_.activation(lnat2, lnat2, ACT.Exp, scale=-1.0).then_inc(achain, 1)
                act.wait_ge(achain, 2)
                a_.activation(lnat2, lnat2, ACT.Ln, bias=1.0).then_inc(achain, 1)

            slabs(act, slab, small)
            act.wait_ge(expo_ready, 1)
            a_.activation(decay[:, :, :], decay[:, :, :], ACT.Exp).then_inc(raw_decay, 1)
            a_.activation(spread[:, :, :], e_spread_f, ACT.Exp, scale=lnat[:, D:D + 1]).then_inc(raw_decay, 1)
            a_.activation(alpha_j, e_j_f, ACT.Exp, scale=lnat[:, D:D + 1]).then_inc(achain, 1)
            a_.activation(alpha_ctx, lnat[:, D + 1:D + 2], ACT.Exp).then_inc(achain, 1)
            for s_, dst in enumerate((wg_r[:, 0, 0:CC], wg_r[:, 0, CC:2 * CC], wsoma_r[:, 0], wtemp_r[:, 0], wout_r[:, 0])):
                k = NS + s_
                for a in range(CC):
                    act.wait_ge(slab_turned, k * CC + a + 1)
                    a_.activation(dst[:, a], slab_bank(k % 2, a), ACT.Copy, scale=(0.5 if s_ == 4 else 1.0)).then_inc(act_evac, 1)
                if s_ == 2:
                    for j in range(Q):
                        act.wait_ge(vj_full, j + 1)
                        a_.activation(vj[:, j], vtmp[:, j], ACT.Copy).then_inc(vj_hi, 1)
            act.wait_ge(consts_dve, 1)

            def step(i, par):
                A, B, Cr = i + 2, i + 1, i
                if live(B):
                    act.wait_ge(S["ctx_ready"], B + 1)
                    if past(B, 1):
                        act.wait_ge(S["wg_done"], B)
                    a_.activation(ctxh[:, 0], ctxT, ACT.Copy).then_inc(S["ctxhi_ready"], 1)
                if live(B):
                    act.wait_ge(S["h1_done"], B + 1)
                    if past(B, 1):
                        act.wait_ge(S["h1T_turned"], B)
                    a_.activation(h1, h1_ps, ACT.Gelu).then_inc(S["h1_ready"], 1)
                if live(Cr):
                    act.wait_ge(S["temp_ready"], Cr + 1)
                    act.wait_ge(S["state_done"], NG * (Cr + 1))
                    a_.activation(temph[:, 0], tempT, ACT.Copy).then_inc(S["temphi_ready"], 1)
                    act.wait_ge(S["gate_done"], Cr + 1)
                    act.wait_ge(S["templo_ready"], Cr + 1)
                    a_.activation(sg, B_C[:, :], ACT.Tanh, scale=0.5).then_inc(S["gate_ready"], 1)
                if live(B):
                    act.wait_ge(S["h1T_turned"], B + 1)
                    if past(B, 1):
                        act.wait_ge(S["mod_done"], B)
                    a_.activation(h1T, h1T_ps, ACT.Copy).then_inc(S["h1T_ready"], 1)
                if live(A):
                    act.wait_ge(S["xT_turned"], A + 1)
                    if past(A, 1):
                        act.wait_ge(S["h_done"], A)
                    if past(A, 2):
                        act.wait_ge(S["tn_turned"], A - 1)
                    a_.activation(actT, B_A1[:, :], ACT.Copy).then_inc(S["xT_ready"], 1)
                if live(B):
                    act.wait_ge(S["mod_done"], B + 1)
                    if past(B, 1):
                        act.wait_ge(S["m_ready"], B)
                    a_.activation(mt, mt_ps, ACT.Tanh, bias=bn2_c[:, :], scale=0.5).then_inc(S["mt_ready"], 1)
                    act.wait_ge(S["wg_done"], B + 1)
                    if past(B, 1):
                        act.wait_ge(S["glo_ready"], B)
                        act.wait_ge(S["gT_turned"], B)
                    a_.activation(g, B_WG[:, :], ACT.Tanh, scale=0.5).then_inc(S["tg_ready"], 1)
                if live(Cr):
                    act.wait_ge(S["sgT_turned"], Cr + 1)
                    if past(Cr, 1):
                        act.wait_ge(S["out_done"], Cr)
                    a_.activation(sgh[:, 0], B_C[:, :], ACT.Copy).then_inc(S["sgT_ready"], 1)
                if live(B):
                    act.wait_ge(S["gT_turned"], B + 1)
                    if past(B, 1):
                        act.wait_ge(S["p_ready"], NW * B)
                    a_.activation(gT.rearrange("p (a q k) -> p a q k", a=CC, q=Q),
                                  B_XG[:, :].rearrange("p (a k q) -> p a q k", a=CC, q=Q), ACT.Copy).then_inc(S["gT_ready"], 1)
                    act.wait_ge(S["amat_ready"], B + 1)
                    if past(B, 1):
                        act.wait_ge(S["state_done"], NG * B)
                        act.wait_ge(S["gate_done"], B)
                    a_.activation(amath[:, 0], amat, ACT.Copy).then_inc(S["amathi_ready"], 1)
                    act.wait_ge(S["g_ready"], B + 1)
                    a_.activation(gh[:, 0], g, ACT.Copy).then_inc(S["ghi_ready"], 1)
                if live(A):
                    act.wait_ge(S["x1T_turned"], A + 1)
                    act.wait_ge(S["l0_done"], A + 1)
                    a_.activation(actT, B_A1[:, :], ACT.Copy).then_inc(S["x1T_ready"], 1)
                    act.wait_ge(S["h_done"], A + 1)
                    if past(A, 1):
                        act.wait_ge(S["hT_turned"], A)
                    a_.activation(h, B_A1[:, 0:H1], ACT.Relu).then_inc(S["h_ready"], 1)
                if live(A):
                    act.wait_ge(S["hT_turned"], A + 1)
                    if past(A, 1):
                        act.wait_ge(S["l1_done"], A)
                    a_.activation(hT, B_A1[:, H1:2 * H1], ACT.Copy).then_inc(S["hT_ready"], 1)
                if live(Cr):
                    act.wait_ge(S["nm2_ready"], Cr + 1)
                    act.wait_ge(S["out_done"], Cr + 1)
                    if past(Cr, 1):
                        act.wait_ge(S["sq_ready"], Cr)
                        act.wait_ge(S["nbe_ready"], Cr)
                        act.wait_ge(S["nb_ready"], Cr)
                        act.wait_ge(S["lap_done"], Cr)
                    a_.activation(x3, B_C[:, :], ACT.Identity, scale=rs_c[:, 1:2], bias=rs_c[:, 2:3]).then_inc(S["n2_ready"], 1)
                if live(A):
                    act.wait_ge(S["nm1_ready"], A + 1)
                    if past(A, 1):
                        act.wait_ge(S["x2_ready"], A)
                    a_.activation(n1, y, ACT.Identity, scale=rs_a[:, 1:2], bias=rs_a[:, 2:3]).then_inc(S["n1_ready"], 1)
                if live(B):
                    act.wait_ge(S["soma_done"], B + 1)
                    if past(B, 1):
                        act.wait_ge(S["sg_ready"], B)
                    a_.activation(soma, B_MOD[:, :], ACT.Gelu).then_inc(S["soma_ready"], 1)
                if live(A):
                    act.wait_ge(S["x2T_turned"], A + 1)
                    if past(A, 1):
                        act.wait_ge(S["soma_done"], A)
                    a_.activation(x2h[:, 0], B_XG[:, :], ACT.Copy).then_inc(S["x2hi_ready"], 1)
                if live(B):
                    act.wait_ge(S["spread_done"], NG * (B + 1))
                    if live(A):
                        act.wait_ge(S["h_done"], A + 1)
                    if past(B, 1):
                        act.wait_ge(S["tn_turned"], B)
                    a_.activation(tn, B_WG[:, :], ACT.Copy).then_inc(S["tn_ready"], 1)
                if live(Cr):
                    act.wait_ge(S["x3_ready"], Cr + 1)
                    if past(Cr, 1):
                        act.wait_ge(S["fin_ready"], Cr)
                    a_.activation(sq, x3, ACT.Square).then_inc(S["sq_ready"], 1)

            steps(act, step)

        @block.vector
        def _(dve):
            v_ = nc.vector
            v_.memset(work[:, 0:n_table], 0.0).then_inc(rows_zeroed, 1)
            done = [0]

            def link(ins):
                ins.then_inc(dchain, 1)
                done[0] += 1
                dve.wait_ge(dchain, done[0])

            for r in range(KG):
                link(v_.memset(lo_rows[r * D:(r + 1) * D, :], float(r % 2)))
            dve.wait_ge(rows_loaded, 3 * 7 * 16)
            stage = work[:, 0:n_table]
            link(v_.tensor_copy(tables[:, :], stage))
            for part in (1, 2):
                rows = slice(PART_ROW[part], P)
                link(v_.tensor_tensor(stage[rows], stage[rows], tables[rows, :], ALU.subtract))
                link(v_.tensor_copy(tables[rows, :], stage[rows]))
            dve.wait_ge(const_loaded, N_CONST * 16)
            dve.wait_ge(iota_ready, 4)
            link(v_.tensor_copy(idf, idr))
            link(v_.tensor_scalar(e_p, e_p, QUAD - 1, None, ALU.bitwise_and))
            link(v_.tensor_copy(p_f, e_p))
            v_.tensor_scalar(subj_hot[:, :], idf[:, 0], p_f, None, ALU.is_equal).then_inc(hot_ready, 1)
            v_.tensor_scalar(lang_hot[:, :], idf[:, 1], p_f, None, ALU.is_equal).then_inc(hot_ready, 1)
            link(v_.tensor_scalar(zt[:, :, 0], zraw[:, 2], 1.0, None, ALU.add))
            link(v_.scalar_tensor_tensor(zt[:, :, 0], zraw[:, 0], -2.0, zt[:, :, 0], ALU.mult, ALU.add))
            link(v_.scalar_tensor_tensor(zt[:, :, 0], zraw[:, 1], -2.0, zt[:, :, 0], ALU.mult, ALU.add))
            link(v_.tensor_copy(zt[:, :, 1], zraw[:, 1]))
            link(v_.tensor_copy(zt[:, :, 2], zraw[:, 0]))
            v_.tensor_scalar(zt[:, :, 3], zraw[:, 2], -1.0, None, ALU.mult).then_inc(zt_ready, 1)
            link(v_.tensor_scalar(bn2_c[:, :], bn2_c[:, :], 0.5, None, ALU.mult))
            dve.wait_ge(act_evac, act_copies(NS - 3) + 1)
            v_.tensor_tensor(wn1_r[:, 1].rearrange("p a h -> p (a h)"), bank[0][:, :],
                             wn1_r[:, 0].rearrange("p a h -> p (a h)").bitcast(f32), ALU.subtract).then_inc(dve_evac, 1)
            dve.wait_ge(blend_turned, 1)
            bl_ps = bank[2][:, 0:CC * D].rearrange("p (a d) -> p a d", a=CC)
            link(v_.tensor_reduce(out=bl_m, in_=bl_ps, op=ALU.max, axis=AX.X))
            v_.tensor_tensor(bl_t, bl_ps, bl_m.unsqueeze(2).to_broadcast([P, CC, D]), ALU.subtract).then_inc(blend_shift, 1)
            dve.wait_ge(blend_exp, 1)
            link(v_.tensor_reduce(out=bl_m, in_=bl_t, op=ALU.add, axis=AX.X))
            link(v_.reciprocal(bl_m, bl_m))
            for r in range(KG):
                v_.tensor_tensor(bl_rep[:, :, r], bl_t, bl_m.unsqueeze(2).to_broadcast([P, CC, D]), ALU.mult).then_inc(blend_soft, 1)
            dve.wait_ge(blend_back, 1)
            v_.tensor_copy(blend_n[:, :], bank[3][:, :]).then_inc(blend_copied, 1)
            dve.wait_ge(achain, 3)
            link(v_.tensor_scalar(lnat, lnat, 0.0, None, ALU.max))
            link(v_.tensor_tensor(lnat, lnat, lnat2, ALU.add))
            link(v_.tensor_scalar(lnat, lnat, -1.0, None, ALU.mult))
            link(v_.tensor_scalar(decay[:, :, :], e_decay, 0.0, None, ALU.max))
            link(v_.tensor_tensor(decay[:, :, :], decay[:, :, :],
                                  lnat[:, 0:D].unsqueeze(1).to_broadcast([P, NK, D]), ALU.mult))
            link(v_.tensor_copy(e_spread_f, e_spread))
            v_.tensor_copy(e_j_f, e_j).then_inc(expo_ready, 1)
            for s_, w_ in enumerate((wg_r[:, :, 0:CC], wg_r[:, :, CC:2 * CC], wsoma_r, wtemp_r, wout_r)):
                k = NS + s_
                if s_ == 2:
                    dve.wait_ge(achain, 5)
                    dve.wait_ge(blend_copied, 1)
                    for par in range(2):
                        dve.wait_ge(wt_stored[par], 8 * NS)
                    for j in range(Q):
                        v_.tensor_scalar(vtmp[:, j], blend_n[:, :], alpha_j[:, j:j + 1], None, ALU.mult).then_inc(vj_full, 1)
                for a in range(CC):
                    dve.wait_ge(act_evac, act_copies(k - 1) + a + 1)
                    v_.scalar_tensor_tensor(w_[:, 1, a], slab_bank(k % 2, a), (0.5 if s_ == 4 else 1.0),
                                            w_[:, 0, a].bitcast(f32), ALU.mult, ALU.subtract).then_inc(dve_evac, 1)
            link(v_.memset(ctx_decay[:, :, :], 1.0))
            link(v_.tensor_scalar(ctx_decay[:, :, :], ctx_decay[:, :, :], alpha_ctx, None, ALU.mult))
            dve.wait_ge(pool_done, N_POOL)
            dve.wait_ge(vj_lo, Q)
            dve.wait_ge(dve_evac, dve_copies(NSLAB - 1))
            v_.memset(ctx_decay[:, :, 0:1], 0.0).then_inc(consts_dve, 1)
            dve.wait_ge(consts_dve, 1)

            def stats(src, st, n, b):
                v_.bn_stats(st, src).then_inc(S[f"st{n}_ready"], 1)
                dve.wait_ge(S[f"st{n}_ready"], b + 1)
                if past(b, 1):
                    dve.wait_ge(S[f"nm{n}_ready"], b)

            def aggregate(st, mv, n):
                v_.bn_aggr(mv, st).then_inc(S[f"mv{n}_ready"], 1)

            def states_blend(B, s_):
                dve.wait_ge(S["state_done"], NG * B + s_ + 1)
                if past(B, 1) and s_ == 0:
                    dve.wait_ge(S["spread_done"], NG * B)
                v_.tensor_tensor(u[:, s_], state_bank[s_][:, :], blend_n[:, :], ALU.mult).then_inc(S["u_ready"], 1)

            def chunk_terms(B, w):
                dve.wait_ge(S["w_done"], NW * B + w + 1)
                if w == 0:
                    if past(B, 1):
                        dve.wait_ge(S["temp_ready"], B)
                elif w > 2 or past(B, 1):
                    before = sum(len(js) for js in W_TILES[1:w - 1]) if w > 2 else sum(len(js) for js in W_TILES[1:NW - 2 + w]) - (Q - 1)
                    dve.wait_ge(S["acc_ready"], (Q - 1) * B + before)
                slot = 0 if w == 0 else 1 + w % 2
                at_ = 0
                for j in W_TILES[w]:
                    n = NK * (Q - j)
                    cols = slice(at_, at_ + CC * n)
                    ins = v_.tensor_tensor(pj[:, slot, cols].rearrange("p (a t) -> p a t", a=CC),
                                           ring[(w + 1) % 2][:, cols].rearrange("p (a t) -> p a t", a=CC),
                                           gT.rearrange("p (a t) -> p a t", a=CC)[:, :, 0:n], ALU.mult)
                    at_ += CC * n
                ins.then_inc(S["p_ready"], 1)

            def step(i, par):
                A, B, Cr = i + 2, i + 1, i
                if live(Cr):
                    dve.wait_ge(S["tn_turned"], Cr + 1)
                    dve.wait_ge(S["acc_ready"], (Q - 1) * (Cr + 1))
                    if past(Cr, 1):
                        dve.wait_ge(S["gate_done"], Cr)
                    v_.tensor_tensor(tempT.rearrange("p (a k q) -> p a k q", a=CC, q=Q),
                                     B_C[:, :].rearrange("p (a k q) -> p a k q", a=CC, q=Q),
                                     pj[:, 0].rearrange("p (a q k) -> p a k q", a=CC, q=Q), ALU.add).then_inc(S["temp_ready"], 1)
                    dve.wait_ge(S["temphi_ready"], Cr + 1)
                    v_.tensor_tensor(temph[:, 1], tempT, temph[:, 0].bitcast(f32), ALU.subtract).then_inc(S["templo_ready"], 1)
                    dve.wait_ge(S["gate_ready"], Cr + 1)
                    dve.wait_ge(S["soma_ready"], Cr + 1)
                    v_.scalar_tensor_tensor(sg, sg, 1.0, soma, ALU.add, ALU.mult).then_inc(S["sg_ready"], 1)
                if live(B):
                    dve.wait_ge(S["mt_ready"], B + 1)
                    v_.tensor_scalar(m, mt, 0.25, 0.5, ALU.mult, ALU.add).then_inc(S["m_ready"], 1)
                    dve.wait_ge(S["m_ready"], B + 1)
                    v_.tensor_scalar(msh[:, :], m, lo_rows[:, :], None, ALU.mult).then_inc(S["msh_ready"], 1)
                    dve.wait_ge(S["msh_ready"], B + 1)
                    v_.tensor_tensor(ms[:, :].rearrange("p (q k) -> p q k", q=Q), m.rearrange("p (k q) -> p q k", q=Q),
                                     msh[:, :].bitcast(f32).rearrange("p (k q) -> p q k", q=Q), ALU.subtract).then_inc(S["ms_ready"], 1)
                    dve.wait_ge(S["tg_ready"], B + 1)
                    v_.scalar_tensor_tensor(g, g, 1.0, x2, ALU.add, ALU.mult).then_inc(S["g_ready"], 1)
                if live(Cr):
                    dve.wait_ge(S["sgT_ready"], Cr + 1)
                    v_.tensor_tensor(sgh[:, 1], B_C[:, :], sgh[:, 0].bitcast(f32), ALU.subtract).then_inc(S["sgTlo_ready"], 1)
                if live(B):
                    dve.wait_ge(S["mn_turned"], B + 1)
                    if past(B, 1):
                        dve.wait_ge(S["spread_done"], NG * B)
                    v_.tensor_tensor(amat.rearrange("p (k d) -> p k d", d=D), decay[:, :, :],
                                     mn_ps[:, 0:D].unsqueeze(1).to_broadcast([P, NK, D]), ALU.mult).then_inc(S["amat_ready"], 1)
                if live(B):
                    dve.wait_ge(S["gT_ready"], B + 1)
                    chunk_terms(B, 0)
                    dve.wait_ge(S["amathi_ready"], B + 1)
                    v_.tensor_tensor(amath[:, 1], amat, amath[:, 0].bitcast(f32), ALU.subtract).then_inc(S["amatlo_ready"], 1)
                    chunk_terms(B, 1)
                if live(A):
                    dve.wait_ge(S["l0_done"], A + 1)
                    dve.wait_ge(S["x_loaded"], 16 * (A + 1))
                    if past(A, 1):
                        dve.wait_ge(S["xb_ready"], A)
                    v_.tensor_tensor(x1, B_A2[:, :], x_sb, ALU.add).then_inc(S["x1_ready"], 1)
                if live(B):
                    for w in range(2, NW - 1):
                        chunk_terms(B, w)
                if live(Cr):
                    dve.wait_ge(S["out_done"], Cr + 1)
                    stats(B_C[:, :], st_c, 2, Cr)
                if live(A):
                    dve.wait_ge(S["l1_done"], A + 1)
                    if past(A, 1):
                        dve.wait_ge(S["n1_ready"], A)
                    v_.tensor_tensor(y, B_A2[:, :], x1, ALU.add).then_inc(S["y_ready"], 1)
                if live(Cr):
                    aggregate(st_c, mv_c, 2)
                if live(A):
                    dve.wait_ge(S["y_ready"], A + 1)
                    stats(y, st_a, 1, A)
                if live(B):
                    chunk_terms(B, NW - 1)
                if live(A):
                    aggregate(st_a, mv_a, 1)
                if live(B):
                    for s_ in range(NG - 2):
                        states_blend(B, s_)
                if live(A):
                    dve.wait_ge(S["n1_ready"], A + 1)
                    dve.wait_ge(S["gamma_loaded"], 16 * (A + 1))
                    v_.tensor_tensor(n1, n1, gamma_t[:, :], ALU.mult).then_inc(S["ng1_ready"], 1)
                    dve.wait_ge(S["ng1_ready"], A + 1)
                    dve.wait_ge(S["xb_ready"], A + 1)
                    if past(A, 1):
                        dve.wait_ge(S["x2b_ready"], A)
                        dve.wait_ge(S["x2T_turned"], A)
                    v_.tensor_tensor(x2, n1, xb, ALU.add).then_inc(S["x2_ready"], 1)
                if live(B):
                    for s_ in range(NG - 2, NG):
                        states_blend(B, s_)
                if live(A):
                    dve.wait_ge(S["x2hi_ready"], A + 1)
                    v_.tensor_tensor(x2h[:, 1], B_XG[:, :], x2h[:, 0].bitcast(f32), ALU.subtract).then_inc(S["x2lo_ready"], 1)
                    if past(A, 1):
                        dve.wait_ge(S["ctxlo_ready"], A)
                        dve.wait_ge(S["ctxhi_ready"], A)
                    v_.tensor_tensor_scan(ctxT, ctx_decay[:, :, :].rearrange("p a t -> p (a t)"), B_XG[:, :], 0.0,
                                          ALU.mult, ALU.add).then_inc(S["ctx_ready"], 1)
                if live(Cr):
                    dve.wait_ge(S["lap_done"], Cr + 1)
                    dve.wait_ge(S["nb_ready"], Cr + 1)
                    dve.wait_ge(S["nbe_ready"], Cr + 1)
                    v_.scalar_tensor_tensor(nb, nb, zb[:, par, 2:3], B_C[:, :], ALU.mult, ALU.add).then_inc(S["lap_ready"], 1)
                    dve.wait_ge(S["lap_ready"], Cr + 1)
                    dve.wait_ge(S["sq_ready"], Cr + 1)
                    if past(Cr, 1):
                        dve.wait_ge(S["out_stored"], 16 * Cr)
                    v_.scalar_tensor_tensor(fin, sq, zb[:, par, 3:4], nb, ALU.mult, ALU.add).then_inc(S["fin_ready"], 1)

            steps(dve, step)

        @block.tensor
        def _(pe):
            mm = nc.tensor.matmul

            def turn(dst, src, n=CC):
                for a in range(n):
                    ins = nc.tensor.transpose(dst[:, a * P:(a + 1) * P], src[:, a * P:(a + 1) * P], ident[:, :])
                return ins

            def whole(dst, lhs, rhs, blocks=range(CC), start=False):
                for a in blocks:
                    ins = mm(dst, lhs[:, a * P:(a + 1) * P], rhs[:, a], start=(start and a == 0), stop=(a == CC - 1))
                return ins

            def split_hi(dst, lhs, rhs, first=0, blocks=range(CC), start=False):
                for a in blocks:
                    for part in range(2):
                        ins = mm(dst, lhs[0][:, a * P:(a + 1) * P], rhs[:, part, first + a],
                                 start=(start and a + part == 0), stop=False)
                return ins

            def split_lo(dst, lhs, rhs, first=0, blocks=range(CC), stop=False):
                for a in blocks:
                    ins = mm(dst, lhs[1][:, a * P:(a + 1) * P], rhs[:, 0, first + a], start=False, stop=(stop and a == CC - 1))
                return ins

            def split(dst, lhs, rhs, first=0, blocks=range(CC), stop=False):
                split_hi(dst, lhs, rhs, first, blocks)
                return split_lo(dst, lhs, rhs, first, blocks, stop)

            sg_parts, temp_parts = (sgh[:, 0], sgh[:, 1]), (temph[:, 0], temph[:, 1])
            x2_parts, ctx_parts = (x2h[:, 0], x2h[:, 1]), (ctxh[:, 0], ctxh[:, 1])

            pe.wait_ge(ident_ready, 1)

            def slab(k, par):
                if past(k, 2):
                    pe.wait_ge(act_evac, act_copies(k - 2))
                if isinstance(k, int) and k >= NS + 2:
                    pe.wait_ge(dve_evac, dve_copies(k - 2))
                pe.wait_ge(raw_loaded[par], transfers(k, par))
                for a in range(CC):
                    for o in range(CC):
                        ins = nc.tensor.transpose(slab_bank(par, a)[:, o * P:(o + 1) * P],
                                                  raw_slab[par][:, o, a * P:(a + 1) * P], ident[:, :])
                    ins.then_inc(slab_turned, 1)

            def small():
                pe.wait_ge(const_loaded, N_CONST * 16)
                pe.wait_ge(act_evac, act_copies(NS - 4))
                turn(bank[0], wn1_raw)
                nc.tensor.transpose(bank[1][:, 0:P], wn2_raw, ident[:, :]).then_inc(wn_turned, 1)
                for a in range(CC):
                    ins = nc.tensor.transpose(bank[2][:, a * D:(a + 1) * D], bl_raw[0:D, a * P:(a + 1) * P], ident[0:D, 0:D])
                ins.then_inc(blend_turned, 1)
                pe.wait_ge(blend_soft, KG)
                for a in range(CC):
                    ins = nc.tensor.transpose(bank[3][:, a * P:(a + 1) * P], bl_rep[:, a].rearrange("p r d -> p (r d)"), ident[:, :])
                ins.then_inc(blend_back, 1)
                pe.wait_ge(act_evac, act_copies(NS - 3) + 2)
                pe.wait_ge(blend_copied, 1)

            slabs(pe, slab, small)
            for k in range(NS, NSLAB):
                slab(k, k % 2)
            pe.wait_ge(act_evac, act_copies(NSLAB - 1))
            pe.wait_ge(consts_dve, 1)

            def chunk_weights(B, w):
                if w == 0 and past(B, 1):
                    pe.wait_ge(S["u_ready"], NG * B - 2)
                if w == 1 and past(B, 1):
                    pe.wait_ge(S["u_ready"], NG * B)
                if w >= 2:
                    pe.wait_ge(S["p_ready"], NW * B + w - 1)
                if w == 0:
                    pe.wait_ge(S["ms_ready"], B + 1)
                at_ = 0
                for j in W_TILES[w]:
                    n = NK * (Q - j)
                    for a in range(CC):
                        ins = mm(ring[(1 + w) % 2][:, at_ + a * n:at_ + (a + 1) * n], vj[:, j, a * P:(a + 1) * P],
                                 ms[:, 0:n], start=True, stop=True)
                    at_ += CC * n
                ins.then_inc(S["w_done"], 1)

            def state(B, s_):
                if s_ < 2:
                    pe.wait_ge(S["p_ready"], NW * B + NW - 1 + s_)
                elif s_ == 2:
                    pe.wait_ge(S["tg_ready"], B + 1)
                else:
                    pe.wait_ge(S["u_ready"], NG * B + 1)
                for a_part, g_part in ((0, 0), (0, 1), (1, 0)):
                    ins = mm(state_bank[s_][:, :], amath[:, a_part, s_ * P:(s_ + 1) * P], gh[:, g_part],
                             start=(a_part + g_part == 0), stop=(a_part == 1))
                ins.then_inc(S["state_done"], 1)

            def soma_part(B, blocks):
                if blocks[0] == 0:
                    mm(B_MOD[:, :], ones[:, :], table("bsoma"), start=True, stop=False)
                ins = split(B_MOD[:, :], x2_parts, wsoma_r, blocks=blocks, stop=True)
                if blocks[-1] == CC - 1:
                    ins.then_inc(S["soma_done"], 1)

            def spread_states(B):
                pe.wait_ge(S["u_ready"], NG * (B + 1))
                for s_ in range(NG):
                    ins = mm(B_WG[s_ * QUAD:(s_ + 1) * QUAD, :], spread[:, :, :].rearrange("p k q -> p (k q)"), u[:, s_],
                             start=True, stop=True, tile_position=(0, s_ * QUAD))
                    ins.then_inc(S["spread_done"], 1)

            def step(i, par):
                A, B, Cr = i + 2, i + 1, i
                if live(B):
                    pe.wait_ge(S["x2hi_ready"], B + 1)
                    if past(B, 1):
                        pe.wait_ge(S["soma_ready"], B)
                    mm(h1_ps, ones[:, :], table("bn1"), start=True, stop=False)
                    split_hi(h1_ps, x2_parts, wn1_r)
                    pe.wait_ge(S["x2lo_ready"], B + 1)
                    split_lo(h1_ps, x2_parts, wn1_r, stop=True).then_inc(S["h1_done"], 1)
                if live(Cr):
                    pe.wait_ge(S["tn_ready"], Cr + 1)
                    if past(Cr, 1):
                        pe.wait_ge(S["lap_ready"], Cr)
                    turn(B_C, tn).then_inc(S["tn_turned"], 1)
                if live(B):
                    mm(B_WG[:, :], ones[:, :], table("bg"), start=True, stop=False)
                    split(B_WG[:, :], x2_parts, wg_r)
                if live(Cr):
                    pe.wait_ge(S["temphi_ready"], Cr + 1)
                    mm(B_C[:, :], ones[:, :], table("btemp"), start=True, stop=False)
                    split_hi(B_C[:, :], temp_parts, wtemp_r)
                    pe.wait_ge(S["templo_ready"], Cr + 1)
                    split_lo(B_C[:, :], temp_parts, wtemp_r, stop=True).then_inc(S["gate_done"], 1)
                if live(B):
                    pe.wait_ge(S["h1_ready"], B + 1)
                    nc.tensor.transpose(h1T_ps, h1, ident[:, :]).then_inc(S["h1T_turned"], 1)
                if live(A):
                    pe.wait_ge(S["x_loaded"], 16 * (A + 1))
                    if past(A, 1):
                        pe.wait_ge(S["hT_ready"], A)
                    turn(B_A1, x_sb).then_inc(S["xT_turned"], 1)
                if live(B):
                    pe.wait_ge(S["ctxhi_ready"], B + 1)
                    pe.wait_ge(S["ctxlo_ready"], B + 1)
                    split(B_WG[:, :], ctx_parts, wg_r, CC, range(2))
                    pe.wait_ge(S["h1T_ready"], B + 1)
                    mm(mt_ps, wn2_t[:, :], h1T, start=True, stop=True).then_inc(S["mod_done"], 1)
                    split(B_WG[:, :], ctx_parts, wg_r, CC, range(2, CC), stop=True).then_inc(S["wg_done"], 1)
                if live(Cr):
                    pe.wait_ge(S["sg_ready"], Cr + 1)
                    turn(B_C, sg).then_inc(S["sgT_turned"], 1)
                if live(B):
                    pe.wait_ge(S["m_ready"], B + 1)
                    nc.tensor.transpose(mn_ps, m, ident[:, :]).then_inc(S["mn_turned"], 1)
                if live(A):
                    pe.wait_ge(S["xT_ready"], A + 1)
                    pe.wait_ge(S["w0_loaded"], 16 * (A + 1))
                    pe.wait_ge(S["subj_set"], A + 1)
                    if past(A, 1):
                        pe.wait_ge(S["y_ready"], A)
                    mm(B_A2[:, :], subj_rows[:, :], table("b0"), start=True, stop=False)
                    whole(B_A2[:, :], actT, w0_t, (0,))
                if live(B):
                    pe.wait_ge(S["g_ready"], B + 1)
                    turn(B_XG, g).then_inc(S["gT_turned"], 1)
                for a in range(1, CC):
                    if live(A):
                        ins = whole(B_A2[:, :], actT, w0_t, (a,))
                        if a == CC - 1:
                            ins.then_inc(S["l0_done"], 1)
                    if live(B) and a > 1:
                        chunk_weights(B, a - 2)
                if live(Cr):
                    pe.wait_ge(S["sgTlo_ready"], Cr + 1)
                    split_hi(B_C[:, :], sg_parts, wout_r, blocks=(0, 1), start=True)
                if live(B):
                    chunk_weights(B, 2)
                if live(A):
                    pe.wait_ge(S["x1_ready"], A + 1)
                    turn(B_A1, x1).then_inc(S["x1T_turned"], 1)
                if live(Cr):
                    split_hi(B_C[:, :], sg_parts, wout_r, blocks=(2, 3))
                if live(B):
                    chunk_weights(B, 3)
                if live(A):
                    pe.wait_ge(S["x1T_ready"], A + 1)
                    pe.wait_ge(S["w1_loaded"], 16 * (A + 1))
                    pe.wait_ge(S["lang_set"], A + 1)
                    mm(B_A1[:, 0:H1], lang_rows[:, :], table("b1"), start=True, stop=False)
                    whole(B_A1[:, 0:H1], actT, w1_t).then_inc(S["h_done"], 1)
                if live(Cr):
                    split_lo(B_C[:, :], sg_parts, wout_r, blocks=(0, 1))
                if live(A):
                    mm(B_A2[:, :], lang_rows[:, :], table("b2"), start=True, stop=False)
                    pe.wait_ge(S["h_ready"], A + 1)
                    nc.tensor.transpose(B_A1[:, H1:2 * H1], h, ident[:, :]).then_inc(S["hT_turned"], 1)
                if live(Cr):
                    split_lo(B_C[:, :], sg_parts, wout_r, blocks=(2, 3), stop=True).then_inc(S["out_done"], 1)
                if live(A):
                    pe.wait_ge(S["hT_ready"], A + 1)
                    pe.wait_ge(S["w2_loaded"], 16 * (A + 1))
                    mm(B_A2[:, :], hT, w2_t[:, :], start=False, stop=True).then_inc(S["l1_done"], 1)
                if live(B):
                    chunk_weights(B, NW - 1)
                    pe.wait_ge(S["amatlo_ready"], B + 1)
                    pe.wait_ge(S["glo_ready"], B + 1)
                    state(B, 0)
                    soma_part(B, (0, 1))
                    state(B, 1)
                    state(B, 2)
                    state(B, 3)
                    soma_part(B, (2, 3))
                if live(A):
                    pe.wait_ge(S["x2_ready"], A + 1)
                    if past(A, 1):
                        pe.wait_ge(S["gT_ready"], A)
                    turn(B_XG, x2).then_inc(S["x2T_turned"], 1)
                if live(Cr):
                    pe.wait_ge(S["x3_ready"], Cr + 1)
                    pe.wait_ge(S["mix_set"], 3 * (Cr + 1))
                    mm(B_C[:, :], mix, x3, start=True, stop=True).then_inc(S["lap_done"], 1)
                if live(B):
                    spread_states(B)

            steps(pe, step)


_INS = ["x", "itok_B_0_7", "itok_B_0_8", "condB_tauraws", "cond_256", "condB_bn2", "cond_1024", "condB_zX",
        "condB_zY", "condB_zR", "L0_cond_weight", "L0_cond_bias", "L1_cond_W1", "L1_cond_b1", "L1_cond_W2",
        "L1_cond_b2", "L1_cond_gamma", "L1_cond_beta", "L2_cond_tau_ctx", "L2_cond_Wg", "L2_cond_bg",
        "L2_cond_Wn1", "L2_cond_bn1", "L2_cond_Wsoma", "L2_cond_bsoma", "L2_cond_Wtemp", "L2_cond_btemp",
        "L2_cond_Wout", "L2_cond_gamma", "L2_cond_beta"]


def kernel(**inputs):
    import numpy as np
    import concourse.bacc as bacc
    from concourse.bass_utils import run_bass_kernel_spmd

    nc = bacc.Bacc("TRN2", target_bir_lowering=False, num_devices=1)
    arrays, args = {}, []
    for name in _INS:
        a = np.ascontiguousarray(inputs[name])
        a = a.reshape(a.shape or (1,))
        arrays[f"in_{name}"] = a
        args.append(nc.dram_tensor(f"in_{name}", a.shape, mybir.dt.from_np(a.dtype), kind="ExternalInput").ap())
    shape = arrays["in_x"].shape
    args.append(nc.dram_tensor("out_0", shape, mybir.dt.float32, kind="ExternalOutput").ap())
    cond_resid_kernel(nc, *args)
    r = run_bass_kernel_spmd(nc, [arrays], core_ids=[0])
    return r.results[0]["out_0"]
```

```python
import concourse.bass as bass
from concourse import mybir
from contextlib import ExitStack


def cond_resid_kernel(nc, x, subject, language, tau, wn2, bn2, blend, zx, zy, zr, l0_w, l0_b,
                      l1_w1, l1_b1, l1_w2, l1_b2, l1_gamma, l1_beta, tau_ctx, wg, bg, wn1, bn1,
                      wsoma, bsoma, wtemp, btemp, wout, l2_gamma, l2_beta, out):
    f32, f32r, bf16, i32 = mybir.dt.float32, mybir.dt.float32r, mybir.dt.bfloat16, mybir.dt.int32
    ALU, ACT, AX = mybir.AluOpType, mybir.ActivationFunctionType, mybir.AxisListType

    P = 128
    NB, T, C = x.shape
    NS = l0_w.shape[0]
    NL, _, H1 = l1_w1.shape
    D = tau.shape[0]
    HN = wn1.shape[1]
    CC = C // P
    Q = 8
    NK = T // Q
    KG = P // D
    NG = NK // KG
    QUAD = 32
    EPS = 1e-5
    W_TILES = [(0,), (1, 7), (2, 6), (3, 5), (4,)]
    NW = len(W_TILES)
    assert T == P and D == QUAD and C == 512 and H1 == P and HN == P and NL <= QUAD and NS <= QUAD

    with ExitStack() as ctx:
        def sb(name, shape, dt=f32):
            return ctx.enter_context(nc.sbuf_tensor(name, shape, dt))

        def sem(name):
            return ctx.enter_context(nc.semaphore(name))

        wg_r = sb("wg_r", [P, 2, 2 * CC, C], f32r)
        wsoma_r = sb("wsoma_r", [P, 2, CC, C], f32r)
        wn1_r = sb("wn1_r", [P, 2, CC, HN], f32r)
        wtemp_r = sb("wtemp_r", [P, 2, CC, C], f32r)
        wout_r = sb("wout_r", [P, 2, CC, C], f32r)
        wn2_t = sb("wn2_t", [P, P])
        w0_land = sb("w0_land", [P, CC // 2, C])
        w0_r = sb("w0_r", [P, 2, CC, C], f32r)
        w1_t = sb("w1_t", [P, CC, H1])
        w2_t = sb("w2_t", [P, C])
        gamma_t = sb("gamma_t", [P, C])
        PART_ROW = (0, 2 * QUAD, 3 * QUAD)
        TB = {}
        at = 0
        for name, width in (("b0", C), ("b2", C), ("bg", C), ("bsoma", C),
                            ("btemp", C), ("b1", H1), ("bn1", HN)):
            TB[name] = (at, width)
            at += width
        tables = sb("tables", [P, at], bf16)
        n_table = at

        def table(name):
            o, w = TB[name]
            return tables[:, o:o + w]

        ones = sb("ones", [P, P], bf16)
        subj_hot = sb("subj_hot", [P, NB], bf16)
        lang_hot = sb("lang_hot", [P, NB], bf16)
        subj_rows = sb("subj_rows", [P, T], bf16)
        lang_rows = sb("lang_rows", [P, T], bf16)
        ident = sb("ident", [P, P])
        neigh = sb("neigh", [P, P])
        decay = sb("decay", [P, NK, D])
        spread = sb("spread", [P, KG, Q])
        blend_n = sb("blend_n", [P, C])
        vj = sb("vj", [P, Q, C], f32r)
        ctx_decay = sb("ctx_decay", [P, CC, T])
        gamma2 = sb("gamma2", [P, C])
        beta2 = sb("beta2", [P, C])
        zt = sb("zt", [P, NB, 4])
        zb = sb("zb", [P, 2, 4])
        bn2_c = sb("bn2_c", [P, 1])
        lo_rows = sb("lo_rows", [P, 1])
        scal = sb("scal", [P, 3])
        ids_sb = sb("ids_sb", [1, 2, NB], i32)
        n_work = 0
        plan = {}
        for name, width in (("actT", C), ("x1", C), ("h", H1), ("hT", H1), ("y", C),
                            ("xb", C), ("x2", C), ("h1", HN),
                            ("h1T", HN), ("mt", T), ("m", T), ("pj", 3 * C),
                            ("u", NG * C), ("tempT", C), ("soma", C),
                            ("x3", C), ("x2b", 2 * C), ("nb", C),
                            ("mix", P), ("mixt", P), ("mixi", P), ("small", 64), ("x", C)):
            plan[name] = (n_work, width)
            n_work += width
        work = sb("work", [P, n_work])

        def buf(name):
            o, w = plan[name]
            return work[:, o:o + w]

        x_sb = buf("x")
        actT, x1, h, hT, y, xb, x2 = (buf(n) for n in ("actT", "x1", "h", "hT", "y", "xb", "x2"))
        n1 = y
        h1, h1T, mt, m = (buf(n) for n in ("h1", "h1T", "mt", "m"))
        pj = buf("pj").rearrange("p (w c) -> p w c", w=3)
        u = buf("u").rearrange("p (a c) -> p a c", a=NG)
        tempT, soma, x3 = (buf(n) for n in ("tempT", "soma", "x3"))
        amat = u[:, NG - 1]
        tn = actT
        sg = tempT
        gT = tempT
        g = soma
        ctxT = pj[:, 2]
        x2b = buf("x2b").rearrange("p (a c) -> p a c", a=2)
        nb = buf("nb")
        sq, fin = x3, nb
        mix, mixt, mixi = buf("mix"), buf("mixt"), buf("mixi")
        sm = buf("small")
        st_a, mv_a, rs_a = sm[:, 0:6], sm[:, 8:10], sm[:, 12:15]
        st_c, mv_c, rs_c = sm[:, 16:22], sm[:, 24:26], sm[:, 28:31]
        prep = [n_table]

        def scratch(width, dt=f32):
            v = work[:, prep[0]:prep[0] + width]
            prep[0] += width
            assert prep[0] <= plan["small"][0]
            return v.bitcast(dt) if dt is not f32 else v

        raw = scratch(2 * CC * C).rearrange("p (s a c) -> p s a c", s=2, a=CC)
        lnat, lnat2 = scratch(D + 2), scratch(D + 2)
        zraw = scratch(3 * NB).rearrange("p (z b) -> p z b", z=3)
        idr = scratch(2 * NB, i32).rearrange("p (z b) -> p z b", z=2)
        idf = scratch(2 * NB).rearrange("p (z b) -> p z b", z=2)
        wn1_raw, wn2_raw = scratch(CC * HN).rearrange("p (a h) -> p a h", a=CC), scratch(D)
        early = scratch(2 * C)
        e_decay = early[:, 0:NK * D].bitcast(i32).rearrange("p (k d) -> p k d", k=NK)
        bl_raw = early[:, C:2 * C]
        vtmp = early.rearrange("p (s c) -> p s c", s=2)
        e_spread = scratch(Q * KG, i32).rearrange("p (k q) -> p k q", q=Q)
        e_spread_f = scratch(Q * KG).rearrange("p (k q) -> p k q", q=Q)
        e_j, e_p = scratch(Q, i32), scratch(1, i32)
        e_j_f, p_f, alpha_j, alpha_ctx = scratch(Q), scratch(1), scratch(Q), scratch(1)
        bl_m = scratch(CC)
        bl_t = scratch(CC * D).rearrange("p (a d) -> p a d", a=CC)
        bl_rep = scratch(CC * KG * D).rearrange("p (a r d) -> p a r d", a=CC, r=KG)
        x2h = sb("x2h", [P, 2, C], f32r)
        ctxh = sb("ctxh", [P, 2, C], f32r)
        temph = sb("temph", [P, 2, C], f32r)
        sgh = ctxh
        gh = temph
        xh = temph
        amath = sb("amath", [P, 2, C], f32r)
        ms = sb("ms", [P, T], f32r)
        msh = sb("msh", [P, T], f32r)

        bank = [ctx.enter_context(nc.psum_tensor(f"bank{i}", [P, C], f32)) for i in range(8)]
        B_XG, B_C, B_A1, B_MOD, B_WG, B_R0, B_A2, B_R1 = bank
        h1_ps, h1T_ps, mt_ps, mn_ps = (B_MOD[:, 0:HN], B_MOD[:, P:2 * P], B_MOD[:, 2 * P:3 * P],
                                       B_MOD[:, 3 * P:4 * P])
        ring = [B_R0, B_R1]
        state_bank = [B_R0, B_R1, B_WG, B_R0]

        ident_ready = sem("ident_ready")
        raw_loaded = [sem(f"raw_loaded_{n}") for n in ("wg_x", "wg_ctx", "wsoma", "wtemp", "wout")]
        wn1_loaded = sem("wn1_loaded")
        hi_made = sem("hi_made")
        lo_made = sem("lo_made")
        lo_made_pool = sem("lo_made_pool")
        wn1_hi = sem("wn1_hi")
        const_loaded = sem("const_loaded")
        const2_loaded = sem("const2_loaded")
        ids_loaded = sem("ids_loaded")
        rows_zeroed = sem("rows_zeroed")
        rows_loaded = sem("rows_loaded")
        iota_ready = sem("iota_ready")
        pool_done = sem("pool_done")
        dchain = sem("dve_step_done")
        achain = sem("act_step_done")
        expo_ready = sem("expo_ready")
        raw_decay = sem("raw_decay")
        blend_turned = sem("blend_turned")
        blend_soft = sem("blend_soft")
        blend_back = sem("blend_back")
        blend_shift = sem("blend_shift")
        blend_exp = sem("blend_exp")
        blend_copied = sem("blend_copied")
        vj_full = sem("vj_full")
        vj_hi = sem("vj_hi")
        vj_lo = sem("vj_lo")
        tables_ready = sem("tables_ready")
        hot_ready = sem("hot_ready")
        zt_ready = sem("zt_ready")
        S = {n: sem(n) for n in ("x_loaded", "w0_loaded", "w1_loaded", "w2_loaded", "gamma_loaded", "beta_loaded",
                                 "out_stored")}
        names = """subj_set lang_set zb_set mix_set
            xT_turned xT_ready l0_done x1_ready x1T_turned x1T_ready h_done h_ready hT_turned hT_ready
            l1_done y_ready st1_ready mv1_ready ve1_ready rs1_ready nm1_ready n1_ready
            ng1_ready xb_ready x2_ready x2T_turned ctx_ready x2hi_ready x2lo_ready ctxhi_ready ctxlo_ready
            h1_done h1_ready h1T_turned h1T_ready mod_done mt_ready m_ready msh_ready ms_ready mn_turned
            amat_ready wg_done tg_ready g_ready gT_turned gT_ready w_done p_ready acc_ready soma_done
            soma_ready state_done u_ready spread_done tn_ready tn_turned temp_ready x2b_ready gate_done gate_ready sg_ready
            temphi_ready templo_ready sgTlo_ready ghi_ready glo_ready xTlo_ready w0hi_ready w0lo_ready amathi_ready amatlo_ready
            sgT_turned sgT_ready out_done st2_ready mv2_ready ve2_ready rs2_ready nm2_ready n2_ready
            ng2_ready x3_ready sq_ready nb_ready nbe_ready lap_done lap_ready fin_ready""".split()
        S.update({n: sem(n) for n in names})

        def live(b):
            return not isinstance(b, int) or 0 <= b < NB

        def past(b, n):
            return not isinstance(b, int) or b >= n

        def first(i):
            return isinstance(i, int) and i == -2

        def steps(engine, step):
            for i in (-2, -1, 0, 1):
                step(i, i % 2)
            with engine.Fori(2, NB - 3, 2) as i:
                step(i, 0)
                step(i + 1, 1)
            for i in (NB - 2, NB - 1):
                step(i, i % 2)

        MATRICES = [(wg[0:C], wg_r[:, :, 0:CC], 1.0), (wg[C:2 * C], wg_r[:, :, CC:2 * CC], 1.0),
                    (wsoma, wsoma_r, 1.0), (wtemp, wtemp_r, 1.0), (wout, wout_r, 0.5)]
        BY_POOL = (2, 3)
        N_CONST = 8
        N_CONST2 = 5
        N_POOL = 6 + 4 + 3
        ACC_AT = {j: n for n, j in enumerate(j for js in W_TILES for j in js if j)}

        block = ctx.enter_context(nc.Block())

        @block.sync
        def _(sp):
            with nc.allow_non_contiguous_dma(reason="small constant rows and columns"):
                def load_matrix(n):
                    if n >= 2:
                        sp.wait_ge(hi_made, CC * (n - 1))
                        if n - 2 in BY_POOL:
                            sp.wait_ge(lo_made_pool, CC * (n - 2 - BY_POOL[0] + 1))
                        else:
                            sp.wait_ge(lo_made, CC * (n - 1))
                    sp.dma_start(raw[:, n % 2], MATRICES[n][0].rearrange("(a p) c -> p a c", p=P)).then_inc(raw_loaded[n], 16)

                sp.dma_start(ids_sb[0:1, 0, :], subject.rearrange("(a b) -> a b", a=1)).then_inc(ids_loaded, 16)
                sp.dma_start(ids_sb[0:1, 1, :], language.rearrange("(a b) -> a b", a=1)).then_inc(ids_loaded, 16)
                load_matrix(0)
                load_matrix(1)
                for dst, src in ((idr[:, 0], subject), (idr[:, 1], language), (zraw[:, 0], zx), (zraw[:, 1], zy), (zraw[:, 2], zr)):
                    sp.dma_start(dst, src.partition_broadcast(P)).then_inc(const2_loaded, 16)
                sp.dma_start(wn1_raw, wn1.rearrange("(a p) h -> p a h", p=P)).then_inc(wn1_loaded, 16)
                load_matrix(2)
                load_matrix(3)
                load_matrix(4)
                sp.wait_ge(ids_loaded, 2 * 16)

                def load_w0(b, half, s_id):
                    if half or past(b, 1):
                        sp.wait_ge(S["w0hi_ready"], 2 * b + half)
                        sp.wait_ge(S["w0lo_ready"], 2 * b + half)
                    blocks = slice(half * P * CC // 2, (half + 1) * P * CC // 2)
                    sp.dma_start(w0_land[:, :, :], l0_w[bass.ds(s_id, 1), blocks].rearrange("s (a p) c -> p (s a) c", p=P)).then_inc(S["w0_loaded"], 16)

                def load_row(b):
                    s_id = sp.value_load(ids_sb[0:1, 0, bass.ds(b, 1)], min_val=0, max_val=NS - 1)
                    l_id = sp.value_load(ids_sb[0:1, 1, bass.ds(b, 1)], min_val=0, max_val=NL - 1)
                    load_w0(b, 0, s_id)
                    if past(b, 1):
                        sp.wait_ge(S["x1_ready"], b)
                    sp.dma_start(x_sb, x[bass.ds(b, 1)].rearrange("a t c -> (a t) c")).then_inc(S["x_loaded"], 16)
                    if past(b, 1):
                        sp.wait_ge(S["h_done"], b)
                    sp.dma_start(w1_t[:, :, :], l1_w1[bass.ds(l_id, 1)].rearrange("l (a p) h -> p (l a) h", p=P)).then_inc(S["w1_loaded"], 16)
                    if past(b, 1):
                        sp.wait_ge(S["l1_done"], b)
                    sp.dma_start(w2_t[:, :], l1_w2[bass.ds(l_id, 1)].rearrange("l h c -> (l h) c")).then_inc(S["w2_loaded"], 16)
                    if past(b, 1):
                        sp.wait_ge(S["ng1_ready"], b)
                    sp.dma_start(gamma_t[:, :], l1_gamma[bass.ds(l_id, 1)].rearrange("l c -> (l c)").partition_broadcast(P)).then_inc(S["gamma_loaded"], 16)
                    if past(b, 1):
                        sp.wait_ge(S["x2_ready"], b)
                    elif isinstance(b, int) and b == 0:
                        sp.wait_ge(tables_ready, 1)
                    sp.dma_start(xb, l1_beta[bass.ds(l_id, 1)].rearrange("l c -> (l c)").partition_broadcast(P)).then_inc(S["beta_loaded"], 16)
                    load_w0(b, 1, s_id)

                def store_row(b):
                    sp.wait_ge(S["fin_ready"], b + 1)
                    sp.dma_start(out[bass.ds(b, 1)].rearrange("a t c -> (a t) c"), fin).then_inc(S["out_stored"], 16)

                def step(i, par):
                    if live(i + 2):
                        load_row(i + 2)
                    if live(i - 1):
                        store_row(i - 1)

                steps(sp, step)
                store_row(NB - 1)
                sp.wait_ge(S["out_stored"], 16 * NB)

        @block.gpsimd
        def _(pool):
            g_ = nc.gpsimd
            g_.memset(ident[:, :], 0.0).then_inc(pool_done, 1)
            pool.wait_ge(pool_done, 1)
            g_.affine_select(out=ident[:, :], in_=ident[:, :], compare_op=ALU.not_equal, fill=1.0, base=0,
                             pattern=[[-1, P]], channel_multiplier=1).then_inc(ident_ready, 1)
            with nc.allow_non_contiguous_dma(reason="small constant rows and columns"):
                def one(dst, src):
                    pool.dma_start(dst, src).then_inc(const_loaded, 16)
                one(bl_raw[0:D, :], blend)
                one(lnat[:, 0:D], tau.partition_broadcast(P))
                one(lnat[:, D + 1:D + 2], tau_ctx.partition_broadcast(P))
                one(wn2_raw, wn2)
                for dst, src in ((lnat[:, D:D + 1], tau), (bn2_c[:, :], bn2)):
                    one(dst, src.partition_broadcast(KG).rearrange("k (d a) -> k d a", a=1))
                one(gamma2[:, :], l2_gamma.partition_broadcast(P))
                one(beta2[:, :], l2_beta.partition_broadcast(P))
            g_.iota(e_decay, pattern=[[Q, NK], [0, D]], base=-1, channel_multiplier=-1).then_inc(iota_ready, 1)
            g_.iota(e_spread, pattern=[[0, KG], [1, Q]], base=1, channel_multiplier=0).then_inc(iota_ready, 1)
            g_.iota(e_j, pattern=[[1, Q]], base=0, channel_multiplier=0).then_inc(iota_ready, 1)
            g_.iota(e_p, pattern=[[0, 1]], base=0, channel_multiplier=1).then_inc(iota_ready, 1)
            g_.memset(ones[:, :], 1.0).then_inc(pool_done, 1)
            for n, value in enumerate((-0.5, EPS, -1.0)):
                g_.memset(scal[:, n:n + 1], value).then_inc(pool_done, 1)
            g_.memset(neigh[:, :], 0.0).then_inc(pool_done, 1)
            n_done = 6
            for cols, base, fill in ((slice(0, P), 1, 1.0), (slice(0, P), -1, 1.0), (slice(0, 1), -1, 2.0),
                                     (slice(P - 1, P), 2 - P, 2.0)):
                width = cols.stop - cols.start
                pool.wait_ge(pool_done, n_done)
                g_.affine_select(out=neigh[:, cols], in_=neigh[:, cols], compare_op=ALU.not_equal, fill=fill,
                                 base=base, pattern=[[-1, width]], channel_multiplier=1).then_inc(pool_done, 1)
                n_done += 1

            def late_constants():
                pool.wait_ge(raw_decay, 2)
                g_.affine_select(out=decay[:, :, :], in_=decay[:, :, :], compare_op=ALU.is_ge, fill=0.0, base=-1,
                                 pattern=[[Q, NK], [0, D]], channel_multiplier=-1).then_inc(pool_done, 1)
                g_.affine_select(out=spread[:, :, :], in_=spread[:, :, :], compare_op=ALU.is_ge, fill=0.0, base=0,
                                 pattern=[[-D, KG], [0, Q]], channel_multiplier=1).then_inc(pool_done, 1)
                pool.wait_ge(pool_done, N_POOL - 1)
                g_.affine_select(out=spread[:, :, :], in_=spread[:, :, :], compare_op=ALU.is_ge, fill=0.0, base=D - 1,
                                 pattern=[[D, KG], [0, Q]], channel_multiplier=-1).then_inc(pool_done, 1)
                pool.wait_ge(pool_done, N_POOL)
                pool.wait_ge(S["lang_set"], 1)
                for j in range(Q):
                    pool.wait_ge(vj_hi, j + 1)
                    g_.tensor_tensor(vj[P // 2:P, j], vtmp[P // 2:P, j % 2], vj[P // 2:P, j].bitcast(f32), ALU.subtract).then_inc(vj_lo, 1)

            pool.wait_ge(pool_done, n_done)
            assert n_done == N_POOL - 3
            for n in BY_POOL:
                parts = MATRICES[n][1]
                for a in range(CC):
                    pool.wait_ge(hi_made, CC * n + a + 1)
                    g_.tensor_tensor(parts[:, 1, a], raw[:, n % 2, a], parts[:, 0, a].bitcast(f32), ALU.subtract).then_inc(lo_made_pool, 1)
            pool.wait_ge(tables_ready, 1)

            def add_terms(B, w):
                pool.wait_ge(S["p_ready"], NW * B + w + 1)
                at_ = 0
                for j in W_TILES[w]:
                    n = NK * (Q - j)
                    dst = pj[:, 0].rearrange("p (a t) -> p a t", a=CC)[:, :, NK * j:T]
                    src = pj[:, 1 + w % 2, at_:at_ + CC * n].rearrange("p (a t) -> p a t", a=CC)
                    if ACC_AT[j] or past(B, 1):
                        pool.wait_ge(S["acc_ready"], (Q - 1) * B + ACC_AT[j])
                    g_.tensor_tensor(dst, dst, src, ALU.add).then_inc(S["acc_ready"], 1)
                    at_ += CC * n

            def rstd(par_mv, par_rs, n, b):
                pool.wait_ge(S[f"mv{n}_ready"], b + 1)
                if past(b, 1):
                    pool.wait_ge(S[f"n{n}_ready"], b)
                g_.tensor_tensor(par_rs[:, 0:1], par_mv[:, 1:2], scal[:, 1:2], ALU.add)
                g_.tensor_tensor(par_rs[:, 2:3], par_mv[:, 0:1], scal[:, 2:3], ALU.mult).then_inc(S[f"ve{n}_ready"], 1)
                pool.wait_ge(S[f"ve{n}_ready"], b + 1)
                g_.tensor_tensor(par_rs[:, 1:2], par_rs[:, 0:1], scal[:, 0:1], ALU.pow).then_inc(S[f"rs{n}_ready"], 1)
                pool.wait_ge(S[f"rs{n}_ready"], b + 1)
                g_.tensor_tensor(par_rs[:, 2:3], par_rs[:, 2:3], par_rs[:, 1:2], ALU.mult).then_inc(S[f"nm{n}_ready"], 1)

            def step(i, par):
                A, B, Cr = i + 2, i + 1, i
                if live(A):
                    if past(A, 1):
                        pool.wait_ge(S["l0_done"], A)
                    g_.tensor_copy(subj_rows[:, :], subj_hot[:, bass.ds(A, 1)].to_broadcast([P, T])).then_inc(S["subj_set"], 1)
                    if past(A, 1):
                        pool.wait_ge(S["l1_done"], A)
                    g_.tensor_copy(lang_rows[:, :], lang_hot[:, bass.ds(A, 1)].to_broadcast([P, T])).then_inc(S["lang_set"], 1)
                if first(i):
                    late_constants()
                    pool.wait_ge(vj_lo, Q)
                if live(B):
                    pool.wait_ge(S["x2_ready"], B + 1)
                    if past(B, 2):
                        pool.wait_ge(S["x3_ready"], B - 1)
                    g_.tensor_tensor(x2b[:, 1 - par], x2, beta2[:, :], ALU.add).then_inc(S["x2b_ready"], 1)
                    pool.wait_ge(S["ctxhi_ready"], B + 1)
                    g_.tensor_tensor(ctxh[:, 1], ctxT, ctxh[:, 0].bitcast(f32), ALU.subtract).then_inc(S["ctxlo_ready"], 1)
                if live(Cr):
                    if past(Cr, 2):
                        pool.wait_ge(S["fin_ready"], Cr - 1)
                    g_.tensor_copy(zb[:, par], zt[:, bass.ds(Cr, 1), :].rearrange("p a z -> p (a z)")).then_inc(S["zb_set"], 1)
                    pool.wait_ge(S["zb_set"], Cr + 1)
                    if past(Cr, 1):
                        pool.wait_ge(S["lap_done"], Cr)
                    g_.tensor_tensor(mixt, neigh[:, :], zb[:, par, 1:2].to_broadcast([P, P]), ALU.mult).then_inc(S["mix_set"], 1)
                    g_.tensor_tensor(mixi, ident[:, :], zb[:, par, 0:1].to_broadcast([P, P]), ALU.mult).then_inc(S["mix_set"], 1)
                    pool.wait_ge(S["mix_set"], 3 * Cr + 2)
                    g_.tensor_tensor(mix, mixt, mixi, ALU.add).then_inc(S["mix_set"], 1)
                if live(B):
                    pool.wait_ge(S["ghi_ready"], B + 1)
                    g_.tensor_tensor(gh[:, 1], g, gh[:, 0].bitcast(f32), ALU.subtract).then_inc(S["glo_ready"], 1)
                    for w in range(1, NW - 1):
                        add_terms(B, w)
                if live(A):
                    pool.wait_ge(S["beta_loaded"], 16 * (A + 1))
                    pool.wait_ge(S["x1_ready"], A + 1)
                    g_.tensor_tensor(xb, xb, x1, ALU.add).then_inc(S["xb_ready"], 1)
                if live(Cr):
                    rstd(mv_c, rs_c, 2, Cr)
                if live(A):
                    rstd(mv_a, rs_a, 1, A)
                if live(Cr):
                    pool.wait_ge(S["n2_ready"], Cr + 1)
                    g_.tensor_tensor(x3, x3, gamma2[:, :], ALU.mult).then_inc(S["ng2_ready"], 1)
                    pool.wait_ge(S["ng2_ready"], Cr + 1)
                    g_.tensor_tensor(x3, x3, x2b[:, par], ALU.add).then_inc(S["x3_ready"], 1)
                    pool.wait_ge(S["x3_ready"], Cr + 1)
                    if past(Cr, 1):
                        pool.wait_ge(S["lap_ready"], Cr)
                        pool.wait_ge(S["out_stored"], 16 * Cr)
                    g_.tensor_tensor(nb[:, 1:C - 1], x3[:, 0:C - 2], x3[:, 2:C], ALU.add).then_inc(S["nb_ready"], 1)
                    g_.tensor_tensor(nb[:, 0:C:C - 1], x3[:, 1:C - 1:C - 3], x3[:, 1:C - 1:C - 3], ALU.add).then_inc(S["nbe_ready"], 1)
                if live(B):
                    add_terms(B, NW - 1)

            steps(pool, step)

        @block.scalar
        def _(act):
            a_ = nc.scalar
            with nc.allow_non_contiguous_dma(reason="small constant rows"):
                act.wait_ge(rows_zeroed, 1)
                for name, src in (("b0", l0_b), ("b1", l1_b1), ("b2", l1_b2), ("bg", bg), ("bsoma", bsoma),
                                  ("btemp", btemp), ("bn1", bn1)):
                    o, w = TB[name]
                    if len(src.shape) == 1:
                        src = src.rearrange("(a c) -> a c", a=1)
                    act.dma_start(work[0:src.shape[0], o:o + w], src).then_inc(rows_loaded, 16)

            def hi_parts(n):
                act.wait_ge(raw_loaded[n], 16)
                _, parts, factor = MATRICES[n]
                for a in range(CC):
                    a_.activation(parts[:, 0, a], raw[:, n % 2, a], ACT.Copy, scale=factor).then_inc(hi_made, 1)

            hi_parts(0)
            hi_parts(1)
            act.wait_ge(wn1_loaded, 16)
            a_.activation(wn1_r[:, 0], wn1_raw, ACT.Copy).then_inc(wn1_hi, 1)
            hi_parts(2)
            act.wait_ge(const_loaded, N_CONST * 16)
            a_.activation(wn2_t[:, :].rearrange("p (r d) -> p r d", r=KG), wn2_raw.unsqueeze(1).to_broadcast([P, KG, D]), ACT.Copy).then_inc(wn1_hi, 1)
            a_.activation(lnat2, lnat, ACT.Abs).then_inc(achain, 1)
            act.wait_ge(achain, 1)
            a_.activation(lnat2, lnat2, ACT.Exp, scale=-1.0).then_inc(achain, 1)
            act.wait_ge(achain, 2)
            a_.activation(lnat2, lnat2, ACT.Ln, bias=1.0).then_inc(achain, 1)
            hi_parts(3)
            act.wait_ge(blend_shift, 1)
            a_.activation(bl_t, bl_t, ACT.Exp).then_inc(blend_exp, 1)
            act.wait_ge(expo_ready, 1)
            a_.activation(decay[:, :, :], decay[:, :, :], ACT.Exp).then_inc(raw_decay, 1)
            a_.activation(spread[:, :, :], e_spread_f, ACT.Exp, scale=lnat[:, D:D + 1]).then_inc(raw_decay, 1)
            a_.activation(alpha_j, e_j_f, ACT.Exp, scale=lnat[:, D:D + 1]).then_inc(achain, 1)
            a_.activation(alpha_ctx, lnat[:, D + 1:D + 2], ACT.Exp).then_inc(achain, 1)

            def w0_hi(b, half):
                act.wait_ge(S["w0_loaded"], 32 * b + 16 * half + 16)
                if past(b, 1):
                    act.wait_ge(S["l0_done"], b)
                a_.activation(w0_r[:, 0, half * CC // 2:(half + 1) * CC // 2], w0_land[:, :, :], ACT.Copy).then_inc(S["w0hi_ready"], 1)

            act.wait_ge(tables_ready, 1)

            def vj_hi_parts(distances):
                for j in distances:
                    act.wait_ge(vj_full, j + 1)
                    a_.activation(vj[:, j], vtmp[:, j % 2], ACT.Copy).then_inc(vj_hi, 1)

            def step(i, par):
                A, B, Cr = i + 2, i + 1, i
                if live(B):
                    act.wait_ge(S["ctx_ready"], B + 1)
                    if past(B, 1):
                        act.wait_ge(S["wg_done"], B)
                    a_.activation(ctxh[:, 0], ctxT, ACT.Copy).then_inc(S["ctxhi_ready"], 1)
                if live(A):
                    w0_hi(A, 0)
                if live(B):
                    act.wait_ge(S["h1_done"], B + 1)
                    if past(B, 1):
                        act.wait_ge(S["h1T_turned"], B)
                    a_.activation(h1, h1_ps, ACT.Gelu).then_inc(S["h1_ready"], 1)
                if live(Cr):
                    act.wait_ge(S["temp_ready"], Cr + 1)
                    act.wait_ge(S["state_done"], NG * (Cr + 1))
                    a_.activation(temph[:, 0], tempT, ACT.Copy).then_inc(S["temphi_ready"], 1)
                    act.wait_ge(S["gate_done"], Cr + 1)
                    act.wait_ge(S["templo_ready"], Cr + 1)
                    a_.activation(sg, B_C[:, :], ACT.Tanh, scale=0.5).then_inc(S["gate_ready"], 1)
                if live(B):
                    act.wait_ge(S["h1T_turned"], B + 1)
                    if past(B, 1):
                        act.wait_ge(S["mod_done"], B)
                    a_.activation(h1T, h1T_ps, ACT.Copy).then_inc(S["h1T_ready"], 1)
                if live(A):
                    act.wait_ge(S["xT_turned"], A + 1)
                    if live(Cr):
                        act.wait_ge(S["gate_done"], Cr + 1)
                    a_.activation(xh[:, 0], B_A1[:, :], ACT.Copy).then_inc(S["xT_ready"], 1)
                    if first(i):
                        vj_hi_parts(range(0, 2))
                    w0_hi(A, 1)
                if live(B):
                    act.wait_ge(S["mod_done"], B + 1)
                    if past(B, 1):
                        act.wait_ge(S["m_ready"], B)
                    a_.activation(mt, mt_ps, ACT.Tanh, bias=bn2_c[:, :], scale=0.5).then_inc(S["mt_ready"], 1)
                    act.wait_ge(S["wg_done"], B + 1)
                    if past(B, 1):
                        act.wait_ge(S["glo_ready"], B)
                    if live(Cr):
                        act.wait_ge(S["sg_ready"], Cr + 1)
                        act.wait_ge(S["gT_turned"], B)
                    a_.activation(g, B_WG[:, :], ACT.Tanh, scale=0.5).then_inc(S["tg_ready"], 1)
                if live(Cr):
                    act.wait_ge(S["sgT_turned"], Cr + 1)
                    if past(Cr, 1):
                        act.wait_ge(S["out_done"], Cr)
                    a_.activation(sgh[:, 0], B_C[:, :], ACT.Copy).then_inc(S["sgT_ready"], 1)
                if live(B):
                    act.wait_ge(S["gT_turned"], B + 1)
                    if past(B, 1):
                        act.wait_ge(S["p_ready"], NW * B)
                    a_.activation(gT.rearrange("p (a q k) -> p a q k", a=CC, q=Q),
                                  B_XG[:, :].rearrange("p (a k q) -> p a q k", a=CC, q=Q), ACT.Copy).then_inc(S["gT_ready"], 1)
                    act.wait_ge(S["amat_ready"], B + 1)
                    if past(B, 1):
                        act.wait_ge(S["state_done"], NG * B)
                        act.wait_ge(S["gate_done"], B)
                    a_.activation(amath[:, 0], amat, ACT.Copy).then_inc(S["amathi_ready"], 1)
                    act.wait_ge(S["g_ready"], B + 1)
                    if live(A):
                        act.wait_ge(S["l0_done"], A + 1)
                    a_.activation(gh[:, 0], g, ACT.Copy).then_inc(S["ghi_ready"], 1)
                if first(i):
                    vj_hi_parts(range(2, 5))
                if live(A):
                    act.wait_ge(S["x1T_turned"], A + 1)
                    if live(Cr):
                        act.wait_ge(S["tn_turned"], Cr + 1)
                    a_.activation(actT, B_A1[:, :], ACT.Copy).then_inc(S["x1T_ready"], 1)
                    if first(i):
                        vj_hi_parts(range(5, Q))
                    act.wait_ge(S["h_done"], A + 1)
                    if past(A, 1):
                        act.wait_ge(S["hT_turned"], A)
                    a_.activation(h, B_A1[:, 0:H1], ACT.Relu).then_inc(S["h_ready"], 1)
                    act.wait_ge(S["hT_turned"], A + 1)
                    if past(A, 1):
                        act.wait_ge(S["l1_done"], A)
                    a_.activation(hT, B_A1[:, H1:2 * H1], ACT.Copy).then_inc(S["hT_ready"], 1)
                if first(i):
                    hi_parts(4)
                if live(Cr):
                    act.wait_ge(S["nm2_ready"], Cr + 1)
                    act.wait_ge(S["out_done"], Cr + 1)
                    if past(Cr, 1):
                        act.wait_ge(S["fin_ready"], Cr)
                        act.wait_ge(S["nbe_ready"], Cr)
                        act.wait_ge(S["nb_ready"], Cr)
                        act.wait_ge(S["lap_done"], Cr)
                    a_.activation(x3, B_C[:, :], ACT.Identity, scale=rs_c[:, 1:2], bias=rs_c[:, 2:3]).then_inc(S["n2_ready"], 1)
                if live(A):
                    act.wait_ge(S["nm1_ready"], A + 1)
                    if past(A, 1):
                        act.wait_ge(S["x2_ready"], A)
                    a_.activation(n1, y, ACT.Identity, scale=rs_a[:, 1:2], bias=rs_a[:, 2:3]).then_inc(S["n1_ready"], 1)
                if live(B):
                    act.wait_ge(S["soma_done"], B + 1)
                    act.wait_ge(S["glo_ready"], B + 1)
                    if past(B, 1):
                        act.wait_ge(S["sg_ready"], B)
                    a_.activation(soma, B_MOD[:, :], ACT.Gelu).then_inc(S["soma_ready"], 1)
                if live(A):
                    act.wait_ge(S["x2T_turned"], A + 1)
                    if past(A, 1):
                        act.wait_ge(S["soma_done"], A)
                    a_.activation(x2h[:, 0], B_XG[:, :], ACT.Copy).then_inc(S["x2hi_ready"], 1)
                if live(B):
                    act.wait_ge(S["spread_done"], NG * (B + 1))
                    if live(A):
                        act.wait_ge(S["h_done"], A + 1)
                    if past(B, 1):
                        act.wait_ge(S["tn_turned"], B)
                    a_.activation(tn, B_WG[:, :], ACT.Copy).then_inc(S["tn_ready"], 1)
                if live(Cr):
                    act.wait_ge(S["x3_ready"], Cr + 1)
                    act.wait_ge(S["lap_done"], Cr + 1)
                    act.wait_ge(S["nb_ready"], Cr + 1)
                    act.wait_ge(S["nbe_ready"], Cr + 1)
                    a_.activation(sq, x3, ACT.Square).then_inc(S["sq_ready"], 1)

            steps(act, step)

        @block.vector
        def _(dve):
            v_ = nc.vector
            v_.memset(work[0:QUAD, 0:n_table], 0.0).then_inc(rows_zeroed, 1)
            done = [0]

            def link(ins):
                ins.then_inc(dchain, 1)
                done[0] += 1
                dve.wait_ge(dchain, done[0])

            def lo_parts(n):
                _, parts, factor = MATRICES[n]
                for a in range(CC):
                    dve.wait_ge(hi_made, CC * n + a + 1)
                    v_.scalar_tensor_tensor(parts[:, 1, a], raw[:, n % 2, a], factor, parts[:, 0, a].bitcast(f32),
                                            ALU.mult, ALU.subtract).then_inc(lo_made, 1)

            for r in range(KG):
                link(v_.memset(lo_rows[r * D:(r + 1) * D, :], float(r % 2)))
            link(v_.memset(tables[QUAD:2 * QUAD, :], 0.0))
            lo_parts(0)
            lo_parts(1)
            dve.wait_ge(rows_loaded, 7 * 16)
            for part in range(3):
                rows = slice(PART_ROW[part], PART_ROW[part] + QUAD)
                if part:
                    before = slice(PART_ROW[part - 1], PART_ROW[part - 1] + QUAD)
                    link(v_.tensor_tensor(work[rows, 0:n_table], work[before, 0:n_table], tables[before, :], ALU.subtract))
                link(v_.tensor_copy(tables[rows, :], work[rows, 0:n_table]))
            dve.wait_ge(wn1_hi, 1)
            link(v_.tensor_tensor(wn1_r[:, 1], wn1_raw, wn1_r[:, 0].bitcast(f32), ALU.subtract))
            dve.wait_ge(const2_loaded, N_CONST2 * 16)
            dve.wait_ge(const_loaded, N_CONST * 16)
            dve.wait_ge(iota_ready, 4)
            link(v_.tensor_copy(idf, idr))
            link(v_.tensor_scalar(e_p, e_p, QUAD - 1, None, ALU.bitwise_and))
            link(v_.tensor_copy(p_f, e_p))
            v_.tensor_scalar(subj_hot[:, :], idf[:, 0], p_f, None, ALU.is_equal).then_inc(hot_ready, 1)
            v_.tensor_scalar(lang_hot[:, :], idf[:, 1], p_f, None, ALU.is_equal).then_inc(hot_ready, 1)
            link(v_.tensor_scalar(zt[:, :, 0], zraw[:, 2], 1.0, None, ALU.add))
            link(v_.scalar_tensor_tensor(zt[:, :, 0], zraw[:, 0], -2.0, zt[:, :, 0], ALU.mult, ALU.add))
            link(v_.scalar_tensor_tensor(zt[:, :, 0], zraw[:, 1], -2.0, zt[:, :, 0], ALU.mult, ALU.add))
            link(v_.tensor_copy(zt[:, :, 1], zraw[:, 1]))
            link(v_.tensor_copy(zt[:, :, 2], zraw[:, 0]))
            v_.tensor_scalar(zt[:, :, 3], zraw[:, 2], -1.0, None, ALU.mult).then_inc(zt_ready, 1)
            link(v_.tensor_scalar(bn2_c[:, :], bn2_c[:, :], 0.5, None, ALU.mult))
            dve.wait_ge(blend_turned, 1)
            bl_ps = bank[2][:, 0:CC * D].rearrange("p (a d) -> p a d", a=CC)
            link(v_.tensor_reduce(out=bl_m, in_=bl_ps, op=ALU.max, axis=AX.X))
            v_.tensor_tensor(bl_t, bl_ps, bl_m.unsqueeze(2).to_broadcast([P, CC, D]), ALU.subtract).then_inc(blend_shift, 1)
            dve.wait_ge(blend_exp, 1)
            link(v_.tensor_reduce(out=bl_m, in_=bl_t, op=ALU.add, axis=AX.X))
            link(v_.reciprocal(bl_m, bl_m))
            for r in range(KG):
                v_.tensor_tensor(bl_rep[:, :, r], bl_t, bl_m.unsqueeze(2).to_broadcast([P, CC, D]), ALU.mult).then_inc(blend_soft, 1)
            dve.wait_ge(blend_back, 1)
            v_.tensor_copy(blend_n[:, :], bank[3][:, :]).then_inc(blend_copied, 1)
            dve.wait_ge(achain, 3)
            link(v_.tensor_scalar(lnat, lnat, 0.0, None, ALU.max))
            link(v_.tensor_tensor(lnat, lnat, lnat2, ALU.add))
            link(v_.tensor_scalar(lnat, lnat, -1.0, None, ALU.mult))
            link(v_.tensor_scalar(decay[:, :, :], e_decay, 0.0, None, ALU.max))
            link(v_.tensor_tensor(decay[:, :, :], decay[:, :, :],
                                  lnat[:, 0:D].unsqueeze(1).to_broadcast([P, NK, D]), ALU.mult))
            link(v_.tensor_copy(e_spread_f, e_spread))
            v_.tensor_copy(e_j_f, e_j).then_inc(expo_ready, 1)
            link(v_.memset(ctx_decay[:, :, :], 1.0))
            dve.wait_ge(achain, 5)
            link(v_.tensor_scalar(ctx_decay[:, :, :], ctx_decay[:, :, :], alpha_ctx, None, ALU.mult))
            dve.wait_ge(blend_copied, 1)
            v_.memset(ctx_decay[:, :, 0:1], 0.0).then_inc(tables_ready, 1)
            dve.wait_ge(tables_ready, 1)

            def w0_lo(b, half):
                dve.wait_ge(S["w0hi_ready"], 2 * b + half + 1)
                blocks = slice(half * CC // 2, (half + 1) * CC // 2)
                v_.tensor_tensor(w0_r[:, 1, blocks], w0_land[:, :, :], w0_r[:, 0, blocks].bitcast(f32), ALU.subtract).then_inc(S["w0lo_ready"], 1)

            def vj_parts(distances):
                for j in distances:
                    if j >= 2:
                        dve.wait_ge(vj_lo, j - 1)
                    v_.tensor_scalar(vtmp[:, j % 2], blend_n[:, :], alpha_j[:, j:j + 1], None, ALU.mult).then_inc(vj_full, 1)

            def stats(src, st, n, b):
                v_.bn_stats(st, src).then_inc(S[f"st{n}_ready"], 1)
                dve.wait_ge(S[f"st{n}_ready"], b + 1)
                if past(b, 1):
                    dve.wait_ge(S[f"nm{n}_ready"], b)

            def aggregate(st, mv, n):
                v_.bn_aggr(mv, st).then_inc(S[f"mv{n}_ready"], 1)

            def states_blend(B, s_):
                dve.wait_ge(S["state_done"], NG * B + s_ + 1)
                if past(B, 1) and s_ == 0:
                    dve.wait_ge(S["spread_done"], NG * B)
                v_.tensor_tensor(u[:, s_], state_bank[s_][:, :], blend_n[:, :], ALU.mult).then_inc(S["u_ready"], 1)

            def chunk_terms(B, w):
                dve.wait_ge(S["w_done"], NW * B + w + 1)
                if w == 0:
                    if past(B, 1):
                        dve.wait_ge(S["temp_ready"], B)
                elif w > 2 or past(B, 1):
                    if w > 2:
                        before = sum(len(js) for js in W_TILES[1:w - 1])
                    else:
                        before = sum(len(js) for js in W_TILES[1:NW - 2 + w]) - (Q - 1)
                    dve.wait_ge(S["acc_ready"], (Q - 1) * B + before)
                if w == 1:
                    dve.wait_ge(S["ctxlo_ready"], B + 1)
                slot = 0 if w == 0 else 1 + w % 2
                at_ = 0
                for j in W_TILES[w]:
                    n = NK * (Q - j)
                    cols = slice(at_, at_ + CC * n)
                    ins = v_.tensor_tensor(pj[:, slot, cols].rearrange("p (a t) -> p a t", a=CC),
                                           ring[(w + 1) % 2][:, cols].rearrange("p (a t) -> p a t", a=CC),
                                           gT.rearrange("p (a t) -> p a t", a=CC)[:, :, 0:n], ALU.mult)
                    at_ += CC * n
                ins.then_inc(S["p_ready"], 1)

            def step(i, par):
                A, B, Cr = i + 2, i + 1, i
                if live(Cr):
                    dve.wait_ge(S["tn_turned"], Cr + 1)
                    dve.wait_ge(S["acc_ready"], (Q - 1) * (Cr + 1))
                    if past(Cr, 1):
                        dve.wait_ge(S["gate_done"], Cr)
                    v_.tensor_tensor(tempT.rearrange("p (a k q) -> p a k q", a=CC, q=Q),
                                     B_C[:, :].rearrange("p (a k q) -> p a k q", a=CC, q=Q),
                                     pj[:, 0].rearrange("p (a q k) -> p a k q", a=CC, q=Q), ALU.add).then_inc(S["temp_ready"], 1)
                if live(A):
                    w0_lo(A, 0)
                if live(Cr):
                    dve.wait_ge(S["temphi_ready"], Cr + 1)
                    v_.tensor_tensor(temph[:, 1], tempT, temph[:, 0].bitcast(f32), ALU.subtract).then_inc(S["templo_ready"], 1)
                    dve.wait_ge(S["gate_ready"], Cr + 1)
                    dve.wait_ge(S["soma_ready"], Cr + 1)
                    v_.scalar_tensor_tensor(sg, sg, 1.0, soma, ALU.add, ALU.mult).then_inc(S["sg_ready"], 1)
                if live(A):
                    dve.wait_ge(S["xT_ready"], A + 1)
                    v_.tensor_tensor(xh[:, 1], B_A1[:, :], xh[:, 0].bitcast(f32), ALU.subtract).then_inc(S["xTlo_ready"], 1)
                    if first(i):
                        vj_parts(range(0, 2))
                    w0_lo(A, 1)
                if live(B):
                    dve.wait_ge(S["mt_ready"], B + 1)
                    v_.tensor_scalar(m, mt, 0.25, 0.5, ALU.mult, ALU.add).then_inc(S["m_ready"], 1)
                    dve.wait_ge(S["m_ready"], B + 1)
                    v_.tensor_scalar(msh[:, :], m, lo_rows[:, :], None, ALU.mult).then_inc(S["msh_ready"], 1)
                    dve.wait_ge(S["msh_ready"], B + 1)
                    v_.tensor_tensor(ms[:, :].rearrange("p (q k) -> p q k", q=Q), m.rearrange("p (k q) -> p q k", q=Q),
                                     msh[:, :].bitcast(f32).rearrange("p (k q) -> p q k", q=Q), ALU.subtract).then_inc(S["ms_ready"], 1)
                    dve.wait_ge(S["tg_ready"], B + 1)
                    v_.scalar_tensor_tensor(g, g, 1.0, x2, ALU.add, ALU.mult).then_inc(S["g_ready"], 1)
                if live(Cr):
                    dve.wait_ge(S["sgT_ready"], Cr + 1)
                    v_.tensor_tensor(sgh[:, 1], B_C[:, :], sgh[:, 0].bitcast(f32), ALU.subtract).then_inc(S["sgTlo_ready"], 1)
                if live(B):
                    dve.wait_ge(S["mn_turned"], B + 1)
                    if past(B, 1):
                        dve.wait_ge(S["spread_done"], NG * B)
                    v_.tensor_tensor(amat.rearrange("p (k d) -> p k d", d=D), decay[:, :, :],
                                     mn_ps[:, 0:D].unsqueeze(1).to_broadcast([P, NK, D]), ALU.mult).then_inc(S["amat_ready"], 1)
                    dve.wait_ge(S["gT_ready"], B + 1)
                    chunk_terms(B, 0)
                    dve.wait_ge(S["amathi_ready"], B + 1)
                    v_.tensor_tensor(amath[:, 1], amat, amath[:, 0].bitcast(f32), ALU.subtract).then_inc(S["amatlo_ready"], 1)
                    chunk_terms(B, 1)
                if first(i):
                    vj_parts(range(2, 5))
                if live(A):
                    dve.wait_ge(S["l0_done"], A + 1)
                    dve.wait_ge(S["x_loaded"], 16 * (A + 1))
                    if past(A, 1):
                        dve.wait_ge(S["xb_ready"], A)
                    v_.tensor_tensor(x1, B_A2[:, :], x_sb, ALU.add).then_inc(S["x1_ready"], 1)
                if first(i):
                    vj_parts(range(5, Q))
                if live(B):
                    for w in range(2, NW - 1):
                        chunk_terms(B, w)
                if live(Cr):
                    dve.wait_ge(S["out_done"], Cr + 1)
                    stats(B_C[:, :], st_c, 2, Cr)
                if live(A):
                    dve.wait_ge(S["l1_done"], A + 1)
                    if past(A, 1):
                        dve.wait_ge(S["x2_ready"], A)
                    v_.tensor_tensor(y, B_A2[:, :], x1, ALU.add).then_inc(S["y_ready"], 1)
                if live(Cr):
                    aggregate(st_c, mv_c, 2)
                if live(A):
                    dve.wait_ge(S["y_ready"], A + 1)
                    stats(y, st_a, 1, A)
                if live(B):
                    chunk_terms(B, NW - 1)
                if live(A):
                    aggregate(st_a, mv_a, 1)
                if live(B):
                    for s_ in range(NG - 2):
                        states_blend(B, s_)
                if first(i):
                    lo_parts(4)
                    dve.wait_ge(pool_done, N_POOL)
                    dve.wait_ge(vj_lo, Q)
                    dve.wait_ge(lo_made, CC * (len(MATRICES) - len(BY_POOL)))
                    dve.wait_ge(lo_made_pool, CC * len(BY_POOL))
                    dve.wait_ge(wn1_hi, 2)
                if live(A):
                    dve.wait_ge(S["n1_ready"], A + 1)
                    dve.wait_ge(S["gamma_loaded"], 16 * (A + 1))
                    v_.tensor_tensor(n1, n1, gamma_t[:, :], ALU.mult).then_inc(S["ng1_ready"], 1)
                    dve.wait_ge(S["ng1_ready"], A + 1)
                    dve.wait_ge(S["xb_ready"], A + 1)
                    if past(A, 1):
                        dve.wait_ge(S["x2b_ready"], A)
                        dve.wait_ge(S["x2T_turned"], A)
                    v_.tensor_tensor(x2, n1, xb, ALU.add).then_inc(S["x2_ready"], 1)
                if live(B):
                    for s_ in range(NG - 2, NG):
                        states_blend(B, s_)
                if live(A):
                    dve.wait_ge(S["x2hi_ready"], A + 1)
                    v_.tensor_tensor(x2h[:, 1], B_XG[:, :], x2h[:, 0].bitcast(f32), ALU.subtract).then_inc(S["x2lo_ready"], 1)
                    if past(A, 1):
                        dve.wait_ge(S["ctxlo_ready"], A)
                        dve.wait_ge(S["ctxhi_ready"], A)
                        dve.wait_ge(S["acc_ready"], (Q - 1) * (A - 1) + sum(len(js) for js in W_TILES[1:NW - 1]))
                    v_.tensor_tensor_scan(ctxT, ctx_decay[:, :, :].rearrange("p a t -> p (a t)"), B_XG[:, :], 0.0,
                                          ALU.mult, ALU.add).then_inc(S["ctx_ready"], 1)
                if live(Cr):
                    dve.wait_ge(S["lap_done"], Cr + 1)
                    dve.wait_ge(S["nb_ready"], Cr + 1)
                    dve.wait_ge(S["nbe_ready"], Cr + 1)
                    v_.scalar_tensor_tensor(nb, nb, zb[:, par, 2:3], B_C[:, :], ALU.mult, ALU.add).then_inc(S["lap_ready"], 1)
                    dve.wait_ge(S["lap_ready"], Cr + 1)
                    dve.wait_ge(S["sq_ready"], Cr + 1)
                    v_.scalar_tensor_tensor(fin, sq, zb[:, par, 3:4], nb, ALU.mult, ALU.add).then_inc(S["fin_ready"], 1)

            steps(dve, step)

        @block.tensor
        def _(pe):
            mm = nc.tensor.matmul

            def turn(dst, src, n=CC):
                for a in range(n):
                    ins = nc.tensor.transpose(dst[:, a * P:(a + 1) * P], src[:, a * P:(a + 1) * P], ident[:, :])
                return ins

            def whole(dst, lhs, rhs, blocks=range(CC), start=False):
                for a in blocks:
                    ins = mm(dst, lhs[:, a * P:(a + 1) * P], rhs[:, a], start=(start and a == 0), stop=(a == CC - 1))
                return ins

            def split_hi(dst, lhs, rhs, first=0, blocks=range(CC), start=False):
                for a in blocks:
                    for part in range(2):
                        ins = mm(dst, lhs[0][:, a * P:(a + 1) * P], rhs[:, part, first + a],
                                 start=(start and a + part == 0), stop=False)
                return ins

            def split_lo(dst, lhs, rhs, first=0, blocks=range(CC), stop=False):
                for a in blocks:
                    ins = mm(dst, lhs[1][:, a * P:(a + 1) * P], rhs[:, 0, first + a], start=False, stop=(stop and a == CC - 1))
                return ins

            def split(dst, lhs, rhs, first=0, blocks=range(CC), stop=False):
                split_hi(dst, lhs, rhs, first, blocks)
                return split_lo(dst, lhs, rhs, first, blocks, stop)

            sg_parts, temp_parts = (sgh[:, 0], sgh[:, 1]), (temph[:, 0], temph[:, 1])
            x_parts = xh[:, 0], xh[:, 1]
            x2_parts, ctx_parts = (x2h[:, 0], x2h[:, 1]), (ctxh[:, 0], ctxh[:, 1])

            pe.wait_ge(ident_ready, 1)

            pe.wait_ge(const_loaded, N_CONST * 16)
            for a in range(CC):
                ins = nc.tensor.transpose(bank[2][:, a * D:(a + 1) * D], bl_raw[0:D, a * P:(a + 1) * P], ident[0:D, 0:D])
            ins.then_inc(blend_turned, 1)
            pe.wait_ge(blend_soft, KG)
            for a in range(CC):
                ins = nc.tensor.transpose(bank[3][:, a * P:(a + 1) * P], bl_rep[:, a].rearrange("p r d -> p (r d)"), ident[:, :])
            ins.then_inc(blend_back, 1)
            pe.wait_ge(tables_ready, 1)

            def chunk_weights(B, w):
                if w == 0 and past(B, 1):
                    pe.wait_ge(S["u_ready"], NG * B - 2)
                if w == 1 and past(B, 1):
                    pe.wait_ge(S["u_ready"], NG * B)
                if w >= 2:
                    pe.wait_ge(S["p_ready"], NW * B + w - 1)
                if w == 0:
                    pe.wait_ge(S["ms_ready"], B + 1)
                at_ = 0
                for j in W_TILES[w]:
                    n = NK * (Q - j)
                    for a in range(CC):
                        ins = mm(ring[(1 + w) % 2][:, at_ + a * n:at_ + (a + 1) * n], vj[:, j, a * P:(a + 1) * P],
                                 ms[:, 0:n], start=True, stop=True)
                    at_ += CC * n
                ins.then_inc(S["w_done"], 1)

            def state(B, s_):
                if s_ < 2:
                    pe.wait_ge(S["p_ready"], NW * B + NW - 1 + s_)
                elif s_ == 2:
                    pe.wait_ge(S["tg_ready"], B + 1)
                else:
                    pe.wait_ge(S["u_ready"], NG * B + 1)
                for a_part, g_part in ((0, 0), (0, 1), (1, 0)):
                    ins = mm(state_bank[s_][:, :], amath[:, a_part, s_ * P:(s_ + 1) * P], gh[:, g_part],
                             start=(a_part + g_part == 0), stop=(a_part == 1))
                ins.then_inc(S["state_done"], 1)

            def soma_part(B, blocks):
                if blocks[0] == 0:
                    mm(B_MOD[:, :], ones[:, :], table("bsoma"), start=True, stop=False)
                ins = split(B_MOD[:, :], x2_parts, wsoma_r, blocks=blocks, stop=True)
                if blocks[-1] == CC - 1:
                    ins.then_inc(S["soma_done"], 1)

            def spread_states(B):
                pe.wait_ge(S["u_ready"], NG * (B + 1))
                for s_ in range(NG):
                    ins = mm(B_WG[s_ * QUAD:(s_ + 1) * QUAD, :], spread[:, :, :].rearrange("p k q -> p (k q)"), u[:, s_],
                             start=True, stop=True, tile_position=(0, s_ * QUAD))
                    ins.then_inc(S["spread_done"], 1)

            def step(i, par):
                A, B, Cr = i + 2, i + 1, i
                if live(B):
                    pe.wait_ge(S["x2hi_ready"], B + 1)
                    if past(B, 1):
                        pe.wait_ge(S["soma_ready"], B)
                    mm(h1_ps, ones[:, :], table("bn1"), start=True, stop=False)
                    split_hi(h1_ps, x2_parts, wn1_r)
                    pe.wait_ge(S["x2lo_ready"], B + 1)
                    split_lo(h1_ps, x2_parts, wn1_r, stop=True).then_inc(S["h1_done"], 1)
                if live(Cr):
                    pe.wait_ge(S["tn_ready"], Cr + 1)
                    if past(Cr, 1):
                        pe.wait_ge(S["lap_ready"], Cr)
                    turn(B_C, tn).then_inc(S["tn_turned"], 1)
                if live(B):
                    mm(B_WG[:, :], ones[:, :], table("bg"), start=True, stop=False)
                    split(B_WG[:, :], x2_parts, wg_r)
                if live(Cr):
                    pe.wait_ge(S["temphi_ready"], Cr + 1)
                    mm(B_C[:, :], ones[:, :], table("btemp"), start=True, stop=False)
                    split_hi(B_C[:, :], temp_parts, wtemp_r)
                    pe.wait_ge(S["templo_ready"], Cr + 1)
                    split_lo(B_C[:, :], temp_parts, wtemp_r, stop=True).then_inc(S["gate_done"], 1)
                if live(B):
                    pe.wait_ge(S["h1_ready"], B + 1)
                    nc.tensor.transpose(h1T_ps, h1, ident[:, :]).then_inc(S["h1T_turned"], 1)
                if live(A):
                    pe.wait_ge(S["x_loaded"], 16 * (A + 1))
                    if past(A, 1):
                        pe.wait_ge(S["hT_ready"], A)
                    turn(B_A1, x_sb).then_inc(S["xT_turned"], 1)
                if live(B):
                    pe.wait_ge(S["ctxhi_ready"], B + 1)
                    pe.wait_ge(S["ctxlo_ready"], B + 1)
                    split(B_WG[:, :], ctx_parts, wg_r, CC, range(2))
                    pe.wait_ge(S["h1T_ready"], B + 1)
                    mm(mt_ps, wn2_t[:, :], h1T, start=True, stop=True).then_inc(S["mod_done"], 1)
                    split(B_WG[:, :], ctx_parts, wg_r, CC, range(2, CC), stop=True).then_inc(S["wg_done"], 1)
                if live(Cr):
                    pe.wait_ge(S["sg_ready"], Cr + 1)
                    turn(B_C, sg).then_inc(S["sgT_turned"], 1)
                if live(B):
                    pe.wait_ge(S["m_ready"], B + 1)
                    nc.tensor.transpose(mn_ps, m, ident[:, :]).then_inc(S["mn_turned"], 1)
                if live(A):
                    pe.wait_ge(S["xTlo_ready"], A + 1)
                    pe.wait_ge(S["w0lo_ready"], 2 * A + 1)
                    pe.wait_ge(S["subj_set"], A + 1)
                    if past(A, 1):
                        pe.wait_ge(S["y_ready"], A)
                    mm(B_A2[:, :], subj_rows[:, :], table("b0"), start=True, stop=False)
                    split(B_A2[:, :], x_parts, w0_r, blocks=(0,))
                if live(B):
                    pe.wait_ge(S["g_ready"], B + 1)
                    turn(B_XG, g).then_inc(S["gT_turned"], 1)
                for a in range(1, CC):
                    if live(A):
                        if a == CC // 2:
                            pe.wait_ge(S["w0lo_ready"], 2 * A + 2)
                        ins = split(B_A2[:, :], x_parts, w0_r, blocks=(a,), stop=True)
                        if a == CC - 1:
                            ins.then_inc(S["l0_done"], 1)
                    if live(B) and a > 1:
                        chunk_weights(B, a - 2)
                if live(Cr):
                    pe.wait_ge(S["sgTlo_ready"], Cr + 1)
                    split_hi(B_C[:, :], sg_parts, wout_r, blocks=(0, 1), start=True)
                if live(B):
                    chunk_weights(B, 2)
                if live(A):
                    pe.wait_ge(S["x1_ready"], A + 1)
                    turn(B_A1, x1).then_inc(S["x1T_turned"], 1)
                if live(Cr):
                    split_hi(B_C[:, :], sg_parts, wout_r, blocks=(2, 3))
                if live(B):
                    chunk_weights(B, 3)
                if live(A):
                    pe.wait_ge(S["x1T_ready"], A + 1)
                    pe.wait_ge(S["w1_loaded"], 16 * (A + 1))
                    pe.wait_ge(S["lang_set"], A + 1)
                    mm(B_A1[:, 0:H1], lang_rows[:, :], table("b1"), start=True, stop=False)
                    whole(B_A1[:, 0:H1], actT, w1_t).then_inc(S["h_done"], 1)
                if live(Cr):
                    split_lo(B_C[:, :], sg_parts, wout_r, blocks=(0, 1))
                if live(A):
                    mm(B_A2[:, :], lang_rows[:, :], table("b2"), start=True, stop=False)
                    pe.wait_ge(S["h_ready"], A + 1)
                    nc.tensor.transpose(B_A1[:, H1:2 * H1], h, ident[:, :]).then_inc(S["hT_turned"], 1)
                if live(Cr):
                    split_lo(B_C[:, :], sg_parts, wout_r, blocks=(2, 3), stop=True).then_inc(S["out_done"], 1)
                if live(A):
                    pe.wait_ge(S["hT_ready"], A + 1)
                    pe.wait_ge(S["w2_loaded"], 16 * (A + 1))
                    mm(B_A2[:, :], hT, w2_t[:, :], start=False, stop=True).then_inc(S["l1_done"], 1)
                if live(B):
                    chunk_weights(B, NW - 1)
                    pe.wait_ge(S["amatlo_ready"], B + 1)
                    pe.wait_ge(S["glo_ready"], B + 1)
                    state(B, 0)
                    soma_part(B, (0, 1))
                    state(B, 1)
                    state(B, 2)
                    state(B, 3)
                    soma_part(B, (2, 3))
                if live(A):
                    pe.wait_ge(S["x2_ready"], A + 1)
                    if past(A, 1):
                        pe.wait_ge(S["gT_ready"], A)
                    turn(B_XG, x2).then_inc(S["x2T_turned"], 1)
                if live(Cr):
                    pe.wait_ge(S["x3_ready"], Cr + 1)
                    pe.wait_ge(S["mix_set"], 3 * (Cr + 1))
                    mm(B_C[:, :], mix, x3, start=True, stop=True).then_inc(S["lap_done"], 1)
                if live(B):
                    spread_states(B)

            steps(pe, step)


_INS = ["x", "itok_B_0_7", "itok_B_0_8", "condB_tauraws", "cond_256", "condB_bn2", "cond_1024", "condB_zX",
        "condB_zY", "condB_zR", "L0_cond_weight", "L0_cond_bias", "L1_cond_W1", "L1_cond_b1", "L1_cond_W2",
        "L1_cond_b2", "L1_cond_gamma", "L1_cond_beta", "L2_cond_tau_ctx", "L2_cond_Wg", "L2_cond_bg",
        "L2_cond_Wn1", "L2_cond_bn1", "L2_cond_Wsoma", "L2_cond_bsoma", "L2_cond_Wtemp", "L2_cond_btemp",
        "L2_cond_Wout", "L2_cond_gamma", "L2_cond_beta"]


_IN_OUT = {"L0_cond_weight", "L2_cond_Wg", "L2_cond_Wn1", "cond_256", "L2_cond_Wsoma", "L2_cond_Wtemp", "L2_cond_Wout"}


def kernel(**inputs):
    import numpy as np
    import concourse.bacc as bacc
    from concourse.bass_utils import run_bass_kernel_spmd

    nc = bacc.Bacc("TRN2", target_bir_lowering=False, num_devices=1)
    arrays, args = {}, []
    for name in _INS:
        a = np.asarray(inputs[name])
        if name in _IN_OUT:
            a = np.swapaxes(a, -1, -2)
        a = np.ascontiguousarray(a)
        a = a.reshape(a.shape or (1,))
        arrays[f"in_{name}"] = a
        args.append(nc.dram_tensor(f"in_{name}", a.shape, mybir.dt.from_np(a.dtype), kind="ExternalInput").ap())
    shape = arrays["in_x"].shape
    args.append(nc.dram_tensor("out_0", shape, mybir.dt.float32, kind="ExternalOutput").ap())
    cond_resid_kernel(nc, *args)
    r = run_bass_kernel_spmd(nc, [arrays], core_ids=[0])
    return r.results[0]["out_0"]
```
